# Optimizing a Trainium2 kernel written in Bass

```python
import numpy as np
import jax
import jax.numpy as jnp

def _softmax(x, axis=-1):
    return jax.nn.softmax(x, axis=axis)

def _gelu(x):
    return jax.nn.gelu(x, approximate=True)

def _silu(x):
    return jax.nn.silu(x)

def _sigmoid(x):
    return jax.nn.sigmoid(x)

def _layernorm(x, axis=-1, eps=1e-05):
    m = jnp.mean(x, axis=axis, keepdims=True)
    v = jnp.var(x, axis=axis, keepdims=True)
    return (x - m) / jnp.sqrt(v + eps)

def _scatter_add(tgt, idx, src, axis=0):
    return tgt.at[idx].add(src)

def _segment_sum(src, seg, n):
    return jax.ops.segment_sum(src, seg, n)
kernel_name = 'mk_decoder_preln_d1_seqx_r8_ff43dc'

def setup_inputs(seed: int=0):
    np.random.seed(seed)
    _w = jnp.asarray

    def _rec_inputs():
        import jax
        import jax.numpy as jnp
        _rk = jax.random.key(seed)
        x = -0.000125 + 0.9999 * jax.random.normal(jax.random.fold_in(_rk, 1), (2, 256, 512), jnp.float32)
        _lenS = 256 - jax.random.randint(jax.random.fold_in(_rk, 7), (2,), 0, max(1, 256 // 4) + 1, jnp.int32)
        _lenS2 = 512 - jax.random.randint(jax.random.fold_in(_rk, 8), (2,), 0, max(1, 512 // 4) + 1, jnp.int32)
        _ctx_4096P = jax.random.normal(jax.random.fold_in(_rk, 11), (2, 16, 512), jnp.float32)
        _ctx_4096c = jax.random.dirichlet(jax.random.fold_in(_rk, 511), 0.3 * jnp.ones((16,), jnp.float32), (2, 512))
        _ctx_4096t = jnp.einsum('bsk,bkd->bsd', _ctx_4096c, _ctx_4096P)
        _ctx_4096t = _ctx_4096t * jax.lax.rsqrt(jnp.mean(jnp.square(_ctx_4096t)) + 1e-12) * 0.953939
        ctx_4096 = -5.72187e-05 + 0.999849 * (_ctx_4096t + 0.3 * jax.random.normal(jax.random.fold_in(_rk, 611), (2, 512, 512), jnp.float32))
        return (x, ctx_4096)
    x, ctx_4096 = _rec_inputs()

    def _L0_attn_setup():
        import jax, jax.numpy as jnp
        import numpy as np
        H_M, P_M, G_M, N_M, K_CONV, CHUNK = (128, 64, 8, 128, 4, 128)
        D_MODEL = 512
        D_INNER = H_M * P_M
        CONV_DIM = D_INNER + 2 * G_M * N_M
        PROJ_DIM = D_INNER + CONV_DIM + H_M
        EPS = 1e-05

        def segsum(x):
            l = x.shape[-1]
            xe = jnp.broadcast_to(x[..., None], x.shape + (l,))
            m1 = jnp.tril(jnp.ones((l, l), dtype=bool), -1)
            s = jnp.cumsum(jnp.where(m1, xe, 0.0), axis=-2)
            m2 = jnp.tril(jnp.ones((l, l), dtype=bool), 0)
            return jnp.where(m2, s, -jnp.inf)

        def causal_conv(x, w, bconv):
            k = w.shape[1]
            s = x.shape[1]
            xp = jnp.pad(x, ((0, 0), (k - 1, 0), (0, 0)))
            y = sum((xp[:, i:i + s, :] * w[:, i] for i in range(k)))
            return y + bconv
        key = jax.random.key(seed)
        ks = jax.random.split(key, 8)
        B_, S = (1, 256)
        sc = 0.02
        return {'x': jax.random.normal(ks[0], (B_, S, D_MODEL), dtype=jnp.float32), 'norm_w': jnp.ones((D_MODEL,), dtype=jnp.float32), 'in_proj_w': jax.random.normal(ks[1], (PROJ_DIM, D_MODEL), dtype=jnp.float32) * sc, 'conv_w': jax.random.normal(ks[2], (CONV_DIM, K_CONV), dtype=jnp.float32) * 0.2, 'conv_b': jnp.zeros((CONV_DIM,), dtype=jnp.float32), 'dt_bias': jax.random.uniform(ks[3], (H_M,), dtype=jnp.float32) * 0.1, 'A_log': jnp.log(1.0 + 15.0 * jax.random.uniform(ks[4], (H_M,), dtype=jnp.float32)), 'Dp': jnp.ones((H_M,), dtype=jnp.float32), 'gnorm_w': jnp.ones((D_INNER,), dtype=jnp.float32), 'out_proj_w': jax.random.normal(ks[5], (D_MODEL, D_INNER), dtype=jnp.float32) * sc}
    _L0_attn_all = _L0_attn_setup()
    _L0_attn_in = {k: v for k, v in _L0_attn_all.items() if k in ('norm_w', 'in_proj_w', 'conv_w', 'conv_b', 'dt_bias', 'A_log', 'Dp', 'gnorm_w', 'out_proj_w')}
    del _L0_attn_all

    def _L0_xattn_setup():
        import jax, jax.numpy as jnp
        import numpy as np
        QMIN = 0.0
        QMAX = 255.0

        def fake_quant(x, scale, zp):
            s = scale.reshape(())
            z = zp.reshape(())
            q = jnp.clip(jnp.round(x / s + z), QMIN, QMAX)
            return (q - z) * s
        key = jax.random.key(seed)
        k1, k2 = jax.random.split(key)
        B, M, K, N = (4, 256, 512, 512)
        x1 = jax.random.normal(k1, (B, M, K), dtype=jnp.float32)
        x2 = jax.random.normal(k2, (B, K, N), dtype=jnp.float32)
        x1_scale = jnp.full((1,), 8.0 / 255.0, dtype=jnp.float32)
        x1_zp = jnp.full((1,), 128.0, dtype=jnp.float32)
        x2_scale = jnp.full((1,), 8.0 / 255.0, dtype=jnp.float32)
        x2_zp = jnp.full((1,), 128.0, dtype=jnp.float32)
        return {'x1': x1, 'x2': x2, 'x1_scale': x1_scale, 'x1_zp': x1_zp, 'x2_scale': x2_scale, 'x2_zp': x2_zp}
    _L0_xattn_all = _L0_xattn_setup()
    _L0_xattn_in = {k: v for k, v in _L0_xattn_all.items() if k in ('x1_scale', 'x1_zp', 'x2_scale', 'x2_zp')}
    del _L0_xattn_all

    def _L0_ffn_setup():
        import jax, jax.numpy as jnp
        import numpy as np
        B, L, H, Dh, M = (4, 256, 16, 32, 128)
        D = H * Dh
        key = jax.random.key(seed)
        kx, ku, kd, kp = jax.random.split(key, 4)
        x = jax.random.normal(kx, (B, L, D), dtype=jnp.float32)
        up = jax.random.normal(ku, (H, Dh, M), dtype=jnp.float32)
        down = jax.random.normal(kd, (H, M, Dh), dtype=jnp.float32)
        perm = jax.random.permutation(kp, D)
        return {'x': x, 'up': up, 'down': down, 'perm': perm}
    _L0_ffn_all = _L0_ffn_setup()
    _L0_ffn_in = {k: v for k, v in _L0_ffn_all.items() if k in ('up', 'down', 'perm')}
    del _L0_ffn_all
    return {'x': x, 'ctx_4096': ctx_4096, 'L0_attn_norm_w': _L0_attn_in['norm_w'], 'L0_attn_in_proj_w': _L0_attn_in['in_proj_w'], 'L0_attn_conv_w': _L0_attn_in['conv_w'], 'L0_attn_conv_b': _L0_attn_in['conv_b'], 'L0_attn_dt_bias': _L0_attn_in['dt_bias'], 'L0_attn_A_log': _L0_attn_in['A_log'], 'L0_attn_Dp': _L0_attn_in['Dp'], 'L0_attn_gnorm_w': _L0_attn_in['gnorm_w'], 'L0_attn_out_proj_w': _L0_attn_in['out_proj_w'], 'L0_xattn_x1_scale': _L0_xattn_in['x1_scale'], 'L0_xattn_x1_zp': _L0_xattn_in['x1_zp'], 'L0_xattn_x2_scale': _L0_xattn_in['x2_scale'], 'L0_xattn_x2_zp': _L0_xattn_in['x2_zp'], 'L0_ffn_up': _L0_ffn_in['up'], 'L0_ffn_down': _L0_ffn_in['down'], 'L0_ffn_perm': _L0_ffn_in['perm']}

def reference(x, ctx_4096, L0_attn_norm_w, L0_attn_in_proj_w, L0_attn_conv_w, L0_attn_conv_b, L0_attn_dt_bias, L0_attn_A_log, L0_attn_Dp, L0_attn_gnorm_w, L0_attn_out_proj_w, L0_xattn_x1_scale, L0_xattn_x1_zp, L0_xattn_x2_scale, L0_xattn_x2_zp, L0_ffn_up, L0_ffn_down, L0_ffn_perm):
    import jax
    import jax.numpy as jnp

    def _L0_attn_ref(x, norm_w, in_proj_w, conv_w, conv_b, dt_bias, A_log, Dp, gnorm_w, out_proj_w):
        import jax, jax.numpy as jnp
        import numpy as np
        H_M, P_M, G_M, N_M, K_CONV, CHUNK = (128, 64, 8, 128, 4, 128)
        D_MODEL = 512
        D_INNER = H_M * P_M
        CONV_DIM = D_INNER + 2 * G_M * N_M
        PROJ_DIM = D_INNER + CONV_DIM + H_M
        EPS = 1e-05

        def segsum(x):
            l = x.shape[-1]
            xe = jnp.broadcast_to(x[..., None], x.shape + (l,))
            m1 = jnp.tril(jnp.ones((l, l), dtype=bool), -1)
            s = jnp.cumsum(jnp.where(m1, xe, 0.0), axis=-2)
            m2 = jnp.tril(jnp.ones((l, l), dtype=bool), 0)
            return jnp.where(m2, s, -jnp.inf)

        def causal_conv(x, w, bconv):
            k = w.shape[1]
            s = x.shape[1]
            xp = jnp.pad(x, ((0, 0), (k - 1, 0), (0, 0)))
            y = sum((xp[:, i:i + s, :] * w[:, i] for i in range(k)))
            return y + bconv
        b, s, _ = x.shape
        residual = x
        h = x * jax.lax.rsqrt(jnp.mean(x * x, axis=-1, keepdims=True) + EPS) * norm_w
        proj = jnp.einsum('bsd,od->bso', h, in_proj_w)
        gate = proj[..., :D_INNER]
        hBC = proj[..., D_INNER:D_INNER + CONV_DIM]
        dt = proj[..., D_INNER + CONV_DIM:]
        hBC = jax.nn.silu(causal_conv(hBC, conv_w, conv_b))
        hid = hBC[..., :D_INNER].reshape(b, s, H_M, P_M)
        B = hBC[..., D_INNER:D_INNER + G_M * N_M].reshape(b, s, G_M, N_M)
        C = hBC[..., D_INNER + G_M * N_M:].reshape(b, s, G_M, N_M)
        dt = jax.nn.softplus(dt + dt_bias)
        A = -jnp.exp(A_log)
        pad = -s % CHUNK
        D_res = Dp[None, None, :, None] * hid
        hid_dt = hid * dt[..., None]
        A_full = A[None, None, :] * dt

        def padseq(t):
            return jnp.pad(t, [(0, 0), (0, pad)] + [(0, 0)] * (t.ndim - 2))
        hid_dt, A_full, Bp, Cp = (padseq(hid_dt), padseq(A_full), padseq(B), padseq(C))
        S = s + pad
        c, l = (S // CHUNK, CHUNK)
        hc = hid_dt.reshape(b, c, l, H_M, P_M)
        Ac = A_full.reshape(b, c, l, H_M).transpose(0, 3, 1, 2)
        rep = H_M // G_M
        Bh = jnp.repeat(Bp.reshape(b, c, l, G_M, N_M), rep, axis=3)
        Ch = jnp.repeat(Cp.reshape(b, c, l, G_M, N_M), rep, axis=3)
        A_cs = jnp.cumsum(Ac, axis=-1)
        L = jnp.exp(segsum(Ac))
        M = jnp.einsum('bcihn,bcjhn->bcijh', Ch, Bh) * jnp.transpose(L, (0, 2, 3, 4, 1))
        Y_diag = jnp.einsum('bcijh,bcjhp->bcihp', M, hc)
        decay_states = jnp.exp(A_cs[..., -1:] - A_cs)
        states = jnp.einsum('bclhn,bhcl,bclhp->bchpn', Bh, decay_states, hc)
        A_last = jnp.pad(A_cs[..., -1], ((0, 0), (0, 0), (1, 0)))
        decay_chunk = jnp.exp(segsum(A_last))
        states_cat = jnp.concatenate([jnp.zeros_like(states[:, :1]), states], axis=1)
        prev_states = jnp.einsum('bhij,bjhpn->bihpn', decay_chunk, states_cat)[:, :-1]
        Y_off = jnp.einsum('bclhn,bchpn,bhcl->bclhp', Ch, prev_states, jnp.exp(A_cs))
        y = (Y_diag + Y_off).reshape(b, S, H_M, P_M)[:, :s] + D_res
        y = y.reshape(b, s, D_INNER)
        yg = y * jax.nn.silu(gate)
        gsz = D_INNER // G_M
        ygr = yg.reshape(b, s, G_M, gsz)
        ygr = ygr * jax.lax.rsqrt(jnp.mean(ygr * ygr, axis=-1, keepdims=True) + EPS)
        y = ygr.reshape(b, s, D_INNER) * gnorm_w
        out = jnp.einsum('bsd,od->bso', y, out_proj_w)
        return residual + out

    def _L0_xattn_ref(x1, x2, x1_scale, x1_zp, x2_scale, x2_zp):
        import jax, jax.numpy as jnp
        import numpy as np
        QMIN = 0.0
        QMAX = 255.0

        def fake_quant(x, scale, zp):
            s = scale.reshape(())
            z = zp.reshape(())
            q = jnp.clip(jnp.round(x / s + z), QMIN, QMAX)
            return (q - z) * s
        q1 = fake_quant(x1, x1_scale, x1_zp)
        q2 = fake_quant(x2, x2_scale, x2_zp)
        return jnp.matmul(q1, q2)

    def _L0_ffn_ref(x, up, down, perm):
        import jax, jax.numpy as jnp
        import numpy as np
        B, L, H, Dh, M = (4, 256, 16, 32, 128)
        D = H * Dh
        b, l, Dm = x.shape
        h, d = (up.shape[0], up.shape[1])
        unperm = jnp.argsort(perm)
        t = x.reshape(b * l, Dm)
        t = t[:, perm]
        t = t.reshape(b * l, h, d)
        t = jnp.einsum('bhd,hdm->bhm', t, up)
        t = jax.nn.gelu(t, approximate=False)
        t = jnp.einsum('bhm,hmd->bhd', t, down)
        t = t.reshape(b * l, h * d)
        t = t[:, unperm]
        out = t.reshape(b, l, Dm)
        return out
    x = x + _L0_attn_ref(_layernorm(x, axis=-1), L0_attn_norm_w, L0_attn_in_proj_w, L0_attn_conv_w, L0_attn_conv_b, L0_attn_dt_bias, L0_attn_A_log, L0_attn_Dp, L0_attn_gnorm_w, L0_attn_out_proj_w)
    x = x + _L0_xattn_ref(_layernorm(x, axis=-1), ctx_4096, L0_xattn_x1_scale, L0_xattn_x1_zp, L0_xattn_x2_scale, L0_xattn_x2_zp)
    x = x + _L0_ffn_ref(_layernorm(x, axis=-1), L0_ffn_up, L0_ffn_down, L0_ffn_perm)
    return x

_drawn_inputs = setup_inputs


def setup_inputs(seed=0):
    import zlib

    import numpy as np

    out = dict(_drawn_inputs(seed))
    spreads = {'L0_attn_norm_w': (1.0, 0.2),
     'L0_attn_conv_b': (0.0, 0.1),
     'L0_attn_Dp': (1.0, 0.2),
     'L0_attn_gnorm_w': (1.0, 0.2)}
    factors = {}
    for name, (base, spread) in spreads.items():
        noise = np.random.default_rng([zlib.crc32(name.encode()), seed]).standard_normal(out[name].shape)
        drawn = base * np.exp(spread * noise) if base else spread * noise
        out[name] = jnp.asarray(drawn.astype(out[name].dtype))
    for name, factor in factors.items():
        out[name] = (out[name] * factor).astype(out[name].dtype)
    return out
```

```python
from contextlib import ExitStack

import concourse.bass as bass
from concourse import mybir

F32 = mybir.dt.float32
F32R = mybir.dt.float32r
BF16 = mybir.dt.bfloat16
I32 = mybir.dt.int32
ALU = mybir.AluOpType
ACT = mybir.ActivationFunctionType
AX_X = mybir.AxisListType.X

P = 128
BATCH, SEQ, D = 2, 256, 512
TOK = BATCH * SEQ
TT = TOK // P
DK = D // P
GROUPS, HEADS, HD = 8, 128, 64
GH = HEADS // GROUPS
INNER = HEADS * HD
GC = INNER // GROUPS
CT = GC // P
NIN = 2 + 2 * CT
NCONV = 2 + CT
TAPS = 4
PAR = TAPS + 1
EPS = 1e-5
W_RING, RAW_RING = 6, 3
WO_RING, RAWO_RING = 4, 2
CTX = 512
CUT = -1e30
FH, FD, FM = 16, 32, 128
MAGIC = 1.5 * 2.0 ** 23


def since(base, i, ring):
    return base + max(i + 1 - ring, 0)


def wait(eng, sem, value):
    if isinstance(value, int) and value <= 0:
        return
    eng.wait_ge(sem, value)


def decoder_layer(nc, x, ctx_in, w_in, w_dt, w_out, conv_par, norm_w, dt_bias, a_log, d_skip,
                  gnorm, quant, up, down, perm, perm_by_part, out):
    acs_dram = nc.dram_tensor("acs_parts", [3, HEADS, TOK], BF16, kind="Internal").ap()

    with ExitStack() as ctx:
        def sb(name, shape, dt=F32):
            return ctx.enter_context(nc.sbuf_tensor(name, shape, dt))

        def psum(name, shape):
            return ctx.enter_context(nc.psum_tensor(name, shape, F32))

        def sem(name):
            return ctx.enter_context(nc.semaphore(name))

        res = sb("res", [P, TT, D])
        h_hi = sb("h_hi", [P, DK, TOK], F32R)
        h_lo = sb("h_lo", [P, DK, TOK], F32R)
        raw = sb("raw", [P, RAW_RING, DK * P])
        w_hi = sb("w_hi", [P, W_RING, DK * P], F32R)
        w_lo = sb("w_lo", [P, W_RING, DK * P], F32R)
        rawo = sb("rawo", [P, RAWO_RING, D])
        wo_hi = sb("wo_hi", [P, WO_RING, D], F32R)
        wo_lo = sb("wo_lo", [P, WO_RING, D], F32R)
        hid = sb("hid", [P, CT, TOK])
        gate = sb("gate", [P, CT, TOK])
        bc = sb("bc", [P, 2, TOK])
        th = sb("th", [P, 2, TOK])
        gth = sb("gth", [P, TOK])
        hdt = sb("hdt", [P, TT, GC])
        gmA = sb("gmA", [P, BATCH, SEQ])
        gmB = sb("gmB", [P, BATCH, P])
        eA = sb("eA", [P, 2, 2, TOK])
        eB = sb("eB", [P, 2, 2, BATCH * P])
        z = sb("z", [P, 2, TOK])
        z_hi = sb("z_hi", [P, CT, TOK], F32R)
        z_lo = sb("z_lo", [P, CT, TOK], F32R)
        sq = sb("sq", [P, TOK])
        sqsum = sb("sqsum", [P, TOK])
        mov = sb("mov", [P, 4, TOK], BF16)
        sta = sb("sta", [P, 4, TOK], BF16)
        cut = sb("cut", [P, 2 * BATCH, P], BF16)
        ident_b = sb("ident_b", [P, P], BF16)
        ident = sb("ident", [P, P])
        ones = sb("ones", [P, 1])
        convp = sb("convp", [P, GROUPS, NCONV * PAR])
        curc = sb("curc", [P, NCONV * PAR])
        skipgn = sb("skipgn", [P, GROUPS, 2 * CT])
        curs = sb("curs", [P, 2 * CT])
        dtT = sb("dtT", [P, TT, HEADS])
        dtg = sb("dtg", [P, TT, GH])
        nw = sb("nw", [P, DK])
        gn_in = sb("gn_in", [P, GROUPS * CT])
        d2 = sb("d2", [2, GROUPS * CT])
        sel = sb("sel", [2, P])
        hcol = sb("hcol", [P, 3])
        half = sb("half", [P, TT])
        stats = sb("stats", [P, TT, 6])
        mv = sb("mv", [P, TT, 2])
        rstd = sb("rstd", [P, TT])
        rms = sb("rms", [P, TT])
        ssum = sb("ssum", [P, TT])
        rgrp = sb("rgrp", [P, TT])
        qs = sb("qs", [P, 4])
        qd = sb("qd", [P, 8])
        rowq = sb("rowq", [P, TT])

        ps_in = psum("ps_in", [P, 2, 512])
        ps_df = psum("ps_df", [P, 2, 512])
        ps_y = psum("ps_y", [P, 512])
        ps_t = psum("ps_t", [P, 512])
        ps_o = psum("ps_o", [P, 2, 512])

        s_x = sem("x_loaded")
        s_par = sem("params_loaded")
        s_wdt = sem("wdt_loaded")
        s_raw = [sem(f"raw_loaded{i}") for i in range(RAW_RING)]
        s_rawo = [sem(f"rawo_loaded{i}") for i in range(RAWO_RING)]
        s_hi = sem("w_hi_done")
        s_lo = sem("w_lo_done")
        s_ohi = sem("wo_hi_done")
        s_olo = sem("wo_lo_done")
        s_in = sem("in_ready")
        s_tap0 = sem("tap0_done")
        s_taps = sem("taps_done")
        s_cth = sem("conv_tanh_done")
        s_conv = sem("conv_done")
        s_gth = sem("gate_tanh_done")
        s_gate = sem("gate_done")
        s_t = sem("turn_ready")
        s_tf = sem("turn_free")
        s_rows = sem("rows_loaded")
        s_df = sem("diff_ready")
        s_exp = sem("exp_done")
        s_m = sem("decay_ready")
        s_y = sem("y_ready")
        s_z1 = sem("y_free")
        s_z = sem("z_done")
        s_zhi = sem("z_hi_done")
        s_zlo = sem("z_lo_done")
        s_sq = sem("square_done")
        s_sqs = sem("square_sum_done")
        s_ss = sem("token_sum_ready")
        s_ms = sem("mean_square_done")
        s_r = sem("rms_done")
        s_ou = sem("wo_used")
        s_oin = sem("out_in_ready")
        s_ofi = sem("out_added_in")
        s_of = sem("out_added")
        s_cur = sem("in_params")
        s_curs = sem("ssd_params")
        s_v = sem("vector_step")
        s_vt = sem("vector_tap")
        s_pv = sem("prologue_vector")
        s_pa = sem("prologue_scalar")
        s_pp = sem("prologue_gpsimd")
        s_pt = sem("prologue_tensor")
        s_acs = sem("acs_stored")
        s_ctx = sem("context_loaded")
        s_ffw = sem("ffn_loaded")
        s_ev = sem("epilogue_vector")
        s_ea = sem("input_squares")
        s_ep = sem("epilogue_gpsimd")
        s_evq = sem("q1_turned")
        s_ft = sem("ffn_tensor")
        s_ff = sem("ffn_vector")
        s_et = sem("epilogue_tensor")
        s_gt = sem("ffn_up_ready")
        s_gl = sem("gelu_done")
        s_store = sem("out_tile_ready")
        s_out = sem("out_stored")

        u = hdt[:, 0:2, :].rearrange("p a (b n) -> p (a b) n", b=2)
        v = hdt[:, 2:4, :].rearrange("p a (b n) -> p (a b) n", b=2)
        sp_v, sp_a, sp_e, sp_w, sp_c, sp_l, dt_h, acs = (gate[:, i, :] for i in range(8))
        r1, r2 = hid[:, 0, :], hid[:, 1, :]
        one_row = hid[:, 2, :]
        parts = hid[:, 4:6, :].bitcast(BF16).rearrange("p a n -> p (a n)")[:, 0:3 * TOK].rearrange(
            "p (r n) -> p r n", r=3)
        wdt_raw = hid[:, 6, :]
        dt_slot = WO_RING - 1
        ctx_raw = gate[:, :, :].rearrange("p a n -> p (a n)").rearrange("p (b k n) -> p b k n", b=BATCH, k=DK)
        q2 = hdt[:, 0:2, :].rearrange("p a n -> p (a n)").bitcast(BF16).rearrange(
            "p (b k n) -> p b k n", b=BATCH, k=DK)
        e1 = hdt[:, 2:4, :].rearrange("p a (b n) -> p (a b) n", b=2)
        q1 = eA[:, 0, :, :].rearrange("p a n -> p (a n)").bitcast(BF16).rearrange("p (t d) -> p t d", t=TT)
        q1T = eA[:, 1, :, :].rearrange("p a n -> p (a n)").bitcast(BF16).rearrange("p (k n) -> p k n", k=DK)
        ones_bf = eB[:, 0, 0, :].bitcast(BF16)[:, 0:P]
        ident_bf = eB[:, 0, 1, :].bitcast(BF16)[:, 0:P]
        perm_row_i = z[:, 0, :].bitcast(I32)
        perm_row = z[:, 1, :]
        iota_row = th[:, 0, :]
        perm_col_i = gth[:, 0:DK].bitcast(I32)
        perm_col = gth[:, DK:2 * DK]
        dcol = gth[:, 2 * DK:3 * DK]
        take = w_hi[:, 0:DK, :]
        put = w_lo[:, 0:DK, :]
        up_sb = bc[:, 0, :].rearrange("p (a m) -> p a m", a=DK)
        down_sb = bc[:, 1, :].rearrange("p (h d) -> p h d", h=FH)
        fT = hdt[:, 0:2, :].rearrange("p a (b n) -> p (a b) n", b=2)
        gel = [hid, gate]

        loops = GROUPS

        block = ctx.enter_context(nc.Block())

        @block.sync
        def _(sp):
            sp.dma_start(res[:, :, :], x.rearrange("(t p) d -> p t d", p=P)).then_inc(s_x, 16)
            sp.dma_start(wdt_raw, w_dt).then_inc(s_wdt, 16)
            loads = [(nw[:, :], norm_w), (hcol[:, 0:1], dt_bias), (hcol[:, 1:2], a_log), (d2[:, :], d_skip),
                     (gn_in[:, :], gnorm), (convp[:, :, :], conv_par),
                     (qs[:, :], quant.partition_broadcast(P))]
            for dst, src in loads:
                sp.dma_start(dst, src).then_inc(s_par, 16)
            sp.wait_ge(s_pv, 7)
            sp.dma_start(acs_dram.rearrange("r h t -> h r t"), parts).then_inc(s_acs, 16)

            def rows(g):
                for q in range(4):
                    src = acs_dram[:, bass.ds(g * GH + 4 * q, 4), :]
                    sp.dma_start(mov[32 * q:32 * q + 3, :, :], src).then_inc(s_rows, 16)
                    sp.dma_start(sta[32 * q + 3:32 * q + 6, :, :], src).then_inc(s_rows, 16)

            def load_in(n, i):
                wait(sp, s_lo, since(NIN * n, i, RAW_RING))
                sp.dma_start(raw[:, i % RAW_RING, :], w_in[bass.ds(n, 1), i, :, :]
                             .rearrange("a p c -> (a p) c")).then_inc(s_raw[i % RAW_RING], 16)

            def load_out(m, q):
                wait(sp, s_olo, since(CT * m, q, RAWO_RING))
                sp.dma_start(rawo[:, q % RAWO_RING, :], w_out[bass.ds(m, 1), q, :, :]
                             .rearrange("a p c -> (a p) c")).then_inc(s_rawo[q % RAWO_RING], 16)

            def iteration(n, do_in, do_ssd):
                m = n - 1
                for i in range(NIN):
                    if do_in:
                        load_in(n, i)
                    if do_ssd and i >= 13 and i % 2:
                        load_out(m, (i - 13) // 2)
                if do_in:
                    if do_ssd:
                        sp.wait_ge(s_df, 3 * CT * m + 3 * CT)
                    else:
                        sp.wait_ge(s_acs, 16)
                        sp.wait_ge(s_pv, 9)
                    rows(n)
                if do_ssd:
                    for q in range(3, CT):
                        load_out(m, q)

            iteration(0, True, False)
            iteration(1, True, True)
            with sp.Fori(2, loops) as n:
                iteration(n, True, True)
            iteration(loops, False, True)
            sp.wait_ge(s_z, CT * loops)
            sp.dma_start(ctx_raw, ctx_in.rearrange("b (k p) n -> p b k n", p=P)).then_inc(s_ctx, 16)
            sp.wait_ge(s_zlo, CT * loops)
            sp.wait_ge(s_sq, CT * loops)
            sp.wait_ge(s_gate, CT * loops)
            sp.wait_ge(s_t, (CT + 2) * loops)
            sp.dma_start(up_sb, up).then_inc(s_ffw, 16)
            sp.dma_start(down_sb, down).then_inc(s_ffw, 16)
            sp.dma_start(perm_row_i, perm.partition_broadcast(P)).then_inc(s_ffw, 16)
            sp.dma_start(perm_col_i, perm_by_part).then_inc(s_ffw, 16)
            for t in range(TT):
                sp.wait_ge(s_store, t + 1)
                sp.dma_start(out[t * P:(t + 1) * P, :], res[:, t, :]).then_inc(s_out, 16)
            sp.wait_ge(s_out, 16 * TT)

        @block.gpsimd
        def _(pool):
            pool.memset(ident[:, :], 0.0).then_inc(s_pp, 1)
            pool.memset(cut[:, :, :], 0.0).then_inc(s_pp, 1)
            pool.memset(sel[:, :], 1.0).then_inc(s_pp, 1)
            pool.memset(half[:, :], -0.5).then_inc(s_pp, 1)
            pool.wait_ge(s_pp, 4)
            pool.affine_select(out=ident[:, :], in_=ident[:, :], compare_op=ALU.not_equal, fill=1.0, base=0,
                               pattern=[[-1, P]], channel_multiplier=1).then_inc(s_pp, 1)
            pool.affine_select(out=cut[:, :, :], in_=cut[:, :, :], compare_op=ALU.is_ge, fill=CUT, base=0,
                               pattern=[[0, 2 * BATCH], [1, P]], channel_multiplier=-1).then_inc(s_pp, 1)
            pool.affine_select(out=sel[:, :], in_=sel[:, :], compare_op=ALU.is_ge, fill=0.0, base=0,
                               pattern=[[1, P]], channel_multiplier=-HD).then_inc(s_pp, 1)
            pool.wait_ge(s_pp, 7)
            pool.affine_select(out=sel[:, :], in_=sel[:, :], compare_op=ALU.is_ge, fill=0.0, base=HD - 1,
                               pattern=[[-1, P]], channel_multiplier=HD).then_inc(s_pp, 1)
            pool.wait_ge(s_pv, 1)
            pool.tensor_tensor(rstd[:, :], rstd[:, :], half[:, :], ALU.pow).then_inc(s_pp, 1)
            pool.wait_ge(s_pv, 3)
            pool.tensor_tensor(rms[:, :], rms[:, :], half[:, :], ALU.pow).then_inc(s_pp, 1)
            pool.wait_ge(s_pa, 1)
            pool.tensor_tensor(wo_lo[:, dt_slot, :], wdt_raw, wo_hi[:, dt_slot, :].bitcast(F32),
                               ALU.subtract).then_inc(s_pp, 1)

            def split_in(n, i):
                pool.wait_ge(s_hi, NIN * n + i + 1)
                wait(pool, s_in, since(NIN * n, i, W_RING))
                pool.tensor_tensor(w_lo[:, i % W_RING, :], raw[:, i % RAW_RING, :],
                                   w_hi[:, i % W_RING, :].bitcast(F32), ALU.subtract).then_inc(s_lo, 1)

            def split_out(m, q):
                pool.wait_ge(s_ohi, CT * m + q + 1)
                wait(pool, s_ou, since(CT * m, q, WO_RING))
                pool.tensor_tensor(wo_lo[:, q % WO_RING, :], rawo[:, q % RAWO_RING, :],
                                   wo_hi[:, q % WO_RING, :].bitcast(F32), ALU.subtract).then_inc(s_olo, 1)

            def iteration(n, do_in, do_ssd):
                m = n - 1
                if do_in:
                    for i in range(4):
                        split_in(n, i)
                for t in range(CT):
                    if do_in:
                        for i in (4 + 2 * t, 5 + 2 * t):
                            if i < NIN:
                                split_in(n, i)
                    if do_ssd:
                        if t:
                            pool.wait_ge(s_sq, CT * m + t + 1)
                            if t > 1:
                                pool.wait_ge(s_sqs, (CT - 1) * m + t - 1)
                            pool.tensor_tensor(sqsum[:, :], sqsum[:, :], sq[:, :], ALU.add).then_inc(s_sqs, 1)
                        if t >= 4:
                            split_out(m, t - 4)
                if do_ssd:
                    split_out(m, 4)
                    split_out(m, 5)
                    pool.wait_ge(s_ms, m + 1)
                    pool.tensor_tensor(rgrp[:, :], ssum[:, :], half[:, :], ALU.pow).then_inc(s_r, 1)
                    split_out(m, 6)
                    split_out(m, 7)

            iteration(0, True, False)
            iteration(1, True, True)
            with pool.Fori(2, loops) as n:
                iteration(n, True, True)
            iteration(loops, False, True)

            pool.wait_ge(s_conv, NCONV * loops)
            pool.iota(iota_row, [[1, D]], base=0, channel_multiplier=0,
                      allow_small_or_imprecise_dtypes=True).then_inc(s_ep, 1)
            pool.wait_ge(s_gate, CT * loops)
            pool.iota(dcol, [[P, DK]], base=0, channel_multiplier=1,
                      allow_small_or_imprecise_dtypes=True).then_inc(s_ep, 1)
            for k in range(2):
                pool.wait_ge(s_ev, 1 + 2 * k)
                pool.tensor_tensor(rstd[:, :], rstd[:, :], half[:, :], ALU.pow).then_inc(s_ep, 1)

        @block.scalar
        def _(act):
            for t in range(TT):
                act.wait_ge(s_v, 3 * TT + t + 1)
                act.activation(v[:, t, :], u[:, t, :], ACT.Square, accum_out=ssum[:, t:t + 1]).then_inc(s_ea, 1)
            act.wait_ge(s_wdt, 16)
            act.activation(wo_hi[:, dt_slot, :], wdt_raw, ACT.Copy).then_inc(s_pa, 1)
            act.wait_ge(s_par, 16 * 7)
            act.activation(hcol[:, 2:3], hcol[:, 1:2], ACT.Exp).then_inc(s_pa, 1)
            act.wait_ge(s_pv, 5)
            act.activation(sp_e, sp_a, ACT.Exp, scale=-1.0).then_inc(s_pa, 1)
            act.wait_ge(s_pv, 6)
            act.activation(sp_l, sp_w, ACT.Ln).then_inc(s_pa, 1)
            act.preload_act_table(ACT.Exp)
            act.wait_ge(s_acs, 16)

            def cast_in(n, i):
                act.wait_ge(s_raw[i % RAW_RING], (NIN // RAW_RING * 16) * n + 16 * (i // RAW_RING + 1))
                wait(act, s_in, since(NIN * n, i, W_RING))
                act.activation(w_hi[:, i % W_RING, :], raw[:, i % RAW_RING, :], ACT.Copy).then_inc(s_hi, 1)

            def cast_out(m, q):
                act.wait_ge(s_rawo[q % RAWO_RING], (CT // RAWO_RING * 16) * m + 16 * (q // RAWO_RING + 1))
                wait(act, s_ou, since(CT * m, q, WO_RING))
                act.activation(wo_hi[:, q % WO_RING, :], rawo[:, q % RAWO_RING, :], ACT.Copy).then_inc(s_ohi, 1)

            def conv_dst(c):
                return bc[:, c, :] if c < 2 else hid[:, c - 2, :]

            def tap0(n, c, do_ssd):
                i = c if c < 2 else 2 * c - 1
                act.wait_ge(s_in, NIN * n + i + 1)
                if c == 0:
                    act.wait_ge(s_cur, 2 * n + 1)
                if c < 2:
                    wait(act, s_t, (CT + 2) * n)
                elif do_ssd:
                    act.wait_ge(s_z1, CT * (n - 1) + c - 1)
                act.activation(conv_dst(c), ps_in[:, i % 2, :], ACT.Identity, scale=curc[:, c * PAR + 3:c * PAR + 4],
                               bias=curc[:, c * PAR + 4:c * PAR + 5]).then_inc(s_tap0, 1)

            def conv_tanh(n, c):
                act.wait_ge(s_taps, NCONV * n + c + 1)
                wait(act, s_conv, since(NCONV * n, c, 2))
                act.activation(th[:, c % 2, :], conv_dst(c), ACT.Tanh, scale=0.5).then_inc(s_cth, 1)

            def exps(m, t, banks):
                for k in banks:
                    act.wait_ge(s_df, 3 * CT * m + 3 * t + k + 1)
                    if k == 0:
                        wait(act, s_y, since(CT * m, t, 2))
                    dst = eA[:, t % 2, k, :] if k < 2 else eB[:, t % 2, :, :].rearrange("p a n -> p (a n)")
                    act.activation(dst, ps_df[:, (3 * t + k) % 2, :], ACT.Exp).then_inc(s_exp, 1)

            def iteration(n, do_in, do_ssd):
                m = n - 1
                if do_in:
                    for i in range(4):
                        cast_in(n, i)
                    tap0(n, 0, do_ssd)
                    tap0(n, 1, do_ssd)
                    conv_tanh(n, 0)
                    conv_tanh(n, 1)
                for t in range(CT):
                    if do_in:
                        if t:
                            tap0(n, t + 1, do_ssd)
                    if do_ssd and t + 1 < CT:
                        exps(m, t + 1, (0, 1))
                    if do_in and t:
                        conv_tanh(n, t + 1)
                    if do_ssd:
                        act.wait_ge(s_z, CT * m + t + 1)
                        wait(act, s_ou, CT * m)
                        act.activation(z_hi[:, t, :], z[:, t % 2, :], ACT.Copy,
                                       scale=curs[:, CT + t:CT + t + 1]).then_inc(s_zhi, 1)
                        if t == 0:
                            wait(act, s_ss, m)
                        else:
                            wait(act, s_sqs, (CT - 1) * m + t - 1)
                        act.activation(sqsum[:, :] if t == 0 else sq[:, :], z[:, t % 2, :],
                                       ACT.Square).then_inc(s_sq, 1)
                        if t + 1 < CT:
                            exps(m, t + 1, (2,))
                    if do_in:
                        act.wait_ge(s_in, NIN * n + 3 + 2 * t)
                        wait(act, s_gate, CT * n + t)
                        act.activation(gth[:, :], ps_in[:, 0, :], ACT.Tanh, scale=0.5).then_inc(s_gth, 1)
                        for i in (4 + 2 * t, 5 + 2 * t):
                            if i < NIN:
                                cast_in(n, i)
                    if do_ssd and t >= 4:
                        cast_out(m, t - 4)
                if do_in:
                    tap0(n, CT + 1, do_ssd)
                    conv_tanh(n, CT + 1)
                if do_ssd:
                    cast_out(m, 4)
                    cast_out(m, 5)
                if do_in:
                    exps(n, 0, (0, 1))
                if do_ssd:
                    cast_out(m, 6)
                    cast_out(m, 7)
                if do_in:
                    exps(n, 0, (2,))

            iteration(0, True, False)
            iteration(1, True, True)
            with act.Fori(2, loops) as n:
                iteration(n, True, True)
            iteration(loops, False, True)
            for h in range(FH):
                act.wait_ge(s_gt, h + 1)
                act.activation(gel[h // CT][:, h % CT, :], ps_in[:, h % 2, :], ACT.Gelu).then_inc(s_gl, 1)

        @block.vector
        def _(dve):
            chain = [0]

            def step(ins):
                chain[0] += 1
                ins.then_inc(s_v, 1)
                dve.wait_ge(s_v, chain[0])

            dve.wait_ge(s_x, 16)
            for t in range(TT):
                step(dve.bn_stats(stats[:, t, :], res[:, t, :]))
                step(dve.bn_aggr(mv[:, t, :], stats[:, t, :]))
            for t in range(TT):
                step(dve.tensor_scalar(rstd[:, t:t + 1], mv[:, t, 1:2], EPS, None, ALU.add))
            dve.memset(ones[:, :], 1.0).then_inc(s_pv, 1)
            dve.wait_ge(s_pp, 9)
            for t in range(TT):
                step(dve.tensor_scalar(u[:, t, :], res[:, t, :], mv[:, t, 0:1], rstd[:, t:t + 1],
                                       ALU.subtract, ALU.mult))
            for t in range(TT):
                step(dve.tensor_tensor(res[:, t, :], res[:, t, :], u[:, t, :], ALU.add))
            dve.memset(one_row, 1.0).then_inc(s_pv, 1)
            dve.wait_ge(s_ea, TT)
            dve.tensor_scalar(rms[:, :], ssum[:, :], 1.0 / D, EPS, ALU.mult, ALU.add).then_inc(s_pv, 1)
            dve.wait_ge(s_pp, 10)
            for t in range(TT):
                step(dve.tensor_scalar(v[:, t, :], u[:, t, :], rms[:, t:t + 1], None, ALU.mult))
            dve.wait_ge(s_par, 16 * 7)
            for k in range(DK):
                dve.wait_ge(s_pt, k + 1)
                src = ps_in[:, k % 2, :]
                step(dve.tensor_scalar(h_hi[:, k, :], src, nw[:, k:k + 1], None, ALU.mult))
                step(dve.scalar_tensor_tensor(h_lo[:, k, :], src, nw[:, k:k + 1], h_hi[:, k, :].bitcast(F32),
                                              ALU.mult, ALU.subtract))
            dve.wait_ge(s_pt, DK + 1)
            step(dve.tensor_scalar(sp_v, ps_y[:, :], hcol[:, 0:1], None, ALU.add))
            dve.tensor_scalar(sp_c, sp_v, -1.0, None, ALU.mult).then_inc(s_pv, 1)
            dve.wait_ge(s_pv, 4)
            dve.tensor_tensor(sp_a, sp_v, sp_c, ALU.max).then_inc(s_pv, 1)
            dve.wait_ge(s_pa, 3)
            dve.tensor_scalar(sp_w, sp_e, 1.0, None, ALU.add).then_inc(s_pv, 1)
            dve.wait_ge(s_pv, 6)
            step(dve.tensor_scalar(sp_a, sp_w, -1.0, None, ALU.add))
            step(dve.tensor_tensor(sp_c, sp_e, sp_a, ALU.subtract))
            step(dve.reciprocal(sp_a, sp_w))
            step(dve.tensor_tensor(sp_c, sp_c, sp_a, ALU.mult))
            dve.wait_ge(s_pa, 4)
            step(dve.tensor_tensor(sp_c, sp_c, sp_l, ALU.add))
            step(dve.scalar_tensor_tensor(dt_h, sp_v, 0.0, sp_c, ALU.max, ALU.add))
            step(dve.tensor_scalar(r1, dt_h, hcol[:, 2:3], -1.0, ALU.mult, ALU.mult))
            for b in range(BATCH):
                seq = slice(b * SEQ, (b + 1) * SEQ)
                step(dve.tensor_tensor_scan(acs[:, seq], one_row[:, seq], r1[:, seq], 0.0, ALU.mult, ALU.add))
            step(dve.tensor_copy(parts[:, 0, :], acs))
            step(dve.tensor_tensor(r1, acs, parts[:, 0, :], ALU.subtract))
            step(dve.tensor_copy(parts[:, 1, :], r1))
            step(dve.tensor_tensor(r2, r1, parts[:, 1, :], ALU.subtract))
            dve.tensor_copy(parts[:, 2, :], r2).then_inc(s_pv, 1)
            step(dve.tensor_copy(ident_b[:, :], ident[:, :]))
            dve.memset(mov[:, :, :], -1.0).then_inc(s_pv, 1)
            dve.memset(sta[:, :, :], 1.0).then_inc(s_pv, 1)
            for g in range(GROUPS):
                step(dve.tensor_scalar(skipgn[:, g, CT:2 * CT], gn_in[:, g * CT:(g + 1) * CT], 0.5, None, ALU.mult))
            dve.wait_ge(s_pt, DK + 2)
            dve.tensor_scalar(skipgn[:, :, 0:CT], ps_o[:, 0, 0:GROUPS * CT].rearrange("p (g t) -> p g t", g=GROUPS),
                              0.5, None, ALU.mult).then_inc(s_pv, 1)
            dve.wait_ge(s_pt, DK + 3)
            dve.tensor_scalar(dtT[:, :, :], ps_t[:, :].rearrange("p (c h) -> p c h", c=TT), 0.5, None,
                              ALU.mult).then_inc(s_pv, 1)
            dve.wait_ge(s_pv, 11)

            def conv_dst(c):
                return bc[:, c, :] if c < 2 else hid[:, c - 2, :]

            def taps(n, c):
                i = c if c < 2 else 2 * c - 1
                dve.wait_ge(s_tap0, NCONV * n + c + 1)
                y = conv_dst(c).rearrange("p (b s) -> p b s", b=BATCH)
                src = ps_in[:, i % 2, :].rearrange("p (b s) -> p b s", b=BATCH)
                for a in range(1, TAPS):
                    last = dve.scalar_tensor_tensor(y[:, :, a:], src[:, :, 0:SEQ - a],
                                                    curc[:, c * PAR + 3 - a:c * PAR + 4 - a], y[:, :, a:],
                                                    ALU.mult, ALU.add)
                    if a < TAPS - 1:
                        last.then_inc(s_vt, 1)
                        dve.wait_ge(s_vt, (TAPS - 2) * (NCONV * n + c) + a)
                last.then_inc(s_taps, 1)

            def conv_silu(n, c):
                dve.wait_ge(s_cth, NCONV * n + c + 1)
                dve.scalar_tensor_tensor(conv_dst(c), th[:, c % 2, :], 1.0, conv_dst(c), ALU.add, ALU.mult)\
                   .then_inc(s_conv, 1)

            def turned(n, t):
                dve.wait_ge(s_t, (CT + 2) * n + t + 1)
                dve.tensor_tensor(
                    hdt[:, :, t * P:(t + 1) * P].rearrange("p c (h q) -> p c h q", h=2),
                    ps_t[:, :].rearrange("p (c h q) -> p c h q", c=TT, h=2),
                    dtg[:, :, 2 * t:2 * t + 2].unsqueeze(3).broadcast_to([P, TT, 2, HD]),
                    ALU.mult).then_inc(s_tf, 1)

            def scores(n):
                dve.wait_ge(s_t, (CT + 2) * n + CT + 1)
                dve.tensor_scalar(gmA[:, :, :], ps_t[:, :].rearrange("p (b i) -> p b i", b=BATCH), 0.25, None,
                                  ALU.mult).then_inc(s_tf, 1)
                dve.wait_ge(s_t, (CT + 2) * n + CT + 2)
                dve.tensor_scalar(gmB[:, :, :], ps_t[:, 0:BATCH * P].rearrange("p (b i) -> p b i", b=BATCH), 0.25,
                                  None, ALU.mult).then_inc(s_tf, 1)

            def decays_a(m, t):
                dve.wait_ge(s_exp, 3 * CT * m + 3 * t + 2)
                if t == 0:
                    dve.wait_ge(s_tf, (CT + 2) * (m + 1))
                a = eA[:, t % 2, :, :]
                dve.tensor_tensor(a, a, gmA[:, :, :].rearrange("p b i -> p (b i)").unsqueeze(1)
                                  .broadcast_to([P, 2, TOK]), ALU.mult)

            def decays_b(m, t):
                dve.wait_ge(s_exp, 3 * CT * m + 3 * t + 3)
                b = eB[:, t % 2, :, :]
                dve.tensor_tensor(b, b, gmB[:, :, :].rearrange("p b i -> p (b i)").unsqueeze(1)
                                  .broadcast_to([P, 2, BATCH * P]), ALU.mult).then_inc(s_m, 1)

            def iteration(n, do_in, do_ssd):
                m = n - 1
                if do_in:
                    wait(dve, s_tap0, NCONV * n)
                    dve.tensor_copy(curc[:, :], convp[:, bass.ds(n, 1), :].rearrange("p a c -> p (a c)"))\
                       .then_inc(s_cur, 1)
                    dve.tensor_copy(dtg[:, :, :], dtT[:, :, bass.ds(n * GH, GH)]).then_inc(s_cur, 1)
                if do_ssd:
                    wait(dve, s_zhi, CT * m)
                    dve.tensor_copy(curs[:, :], skipgn[:, bass.ds(m, 1), :].rearrange("p a c -> p (a c)"))\
                       .then_inc(s_curs, 1)
                if do_in:
                    dve.wait_ge(s_cur, 2 * n + 2)
                    taps(n, 0)
                    taps(n, 1)
                    conv_silu(n, 0)
                    conv_silu(n, 1)
                if do_ssd:
                    dve.wait_ge(s_curs, m + 1)
                for t in range(CT):
                    if do_in and t:
                        taps(n, t + 1)
                    if do_ssd:
                        dve.wait_ge(s_y, CT * m + t + 1)
                        wait(dve, s_sq, since(CT * m, t, 2))
                        dve.scalar_tensor_tensor(z[:, t % 2, :], hid[:, t, :], curs[:, t:t + 1], ps_y[:, :],
                                                 ALU.mult, ALU.add).then_inc(s_z1, 1)
                        dve.wait_ge(s_z1, CT * m + t + 1)
                        dve.tensor_tensor(z[:, t % 2, :], z[:, t % 2, :], gate[:, t, :], ALU.mult).then_inc(s_z, 1)
                    if do_in and t:
                        conv_silu(n, t + 1)
                    if do_ssd:
                        if t + 1 < CT:
                            decays_a(m, t + 1)
                        dve.wait_ge(s_zhi, CT * m + t + 1)
                        wait(dve, s_ou, CT * m)
                        dve.scalar_tensor_tensor(z_lo[:, t, :], z[:, t % 2, :], curs[:, CT + t:CT + t + 1],
                                                 z_hi[:, t, :].bitcast(F32), ALU.mult, ALU.subtract)\
                           .then_inc(s_zlo, 1)
                        if t + 1 < CT:
                            decays_b(m, t + 1)
                    if do_in:
                        dve.wait_ge(s_gth, CT * n + t + 1)
                        dve.scalar_tensor_tensor(gate[:, t, :], gth[:, :], 1.0, ps_in[:, 0, :], ALU.add, ALU.mult)\
                           .then_inc(s_gate, 1)
                        if t:
                            turned(n, t - 1)
                if do_in:
                    taps(n, CT + 1)
                    conv_silu(n, CT + 1)
                if do_ssd:
                    dve.wait_ge(s_ss, m + 1)
                    dve.tensor_scalar(ssum[:, :], ps_y[:, 0:TT], 1.0 / (4 * GC), EPS, ALU.mult, ALU.add)\
                       .then_inc(s_ms, 1)
                if do_in:
                    turned(n, CT - 1)
                    scores(n)
                    decays_a(n, 0)
                    decays_b(n, 0)
                if do_ssd:
                    dve.wait_ge(s_r, m + 1)
                    dve.wait_ge(s_oin, m + 1)
                    for t in (2, 3, 0, 1):
                        if t == 0:
                            dve.wait_ge(s_ou, CT * (m + 1))
                        src = ps_in[:, t - 2, :] if t >= 2 else ps_o[:, t, :]
                        dve.scalar_tensor_tensor(res[:, t, :], src, rgrp[:, t:t + 1], res[:, t, :],
                                                 ALU.mult, ALU.add).then_inc(s_ofi if t >= 2 else s_of, 1)

            iteration(0, True, False)
            iteration(1, True, True)
            with dve.Fori(2, loops) as n:
                iteration(n, True, True)
            iteration(loops, False, True)

            dve.wait_ge(s_of, 2 * loops)

            def layernorm(k):
                for t in range(TT):
                    step(dve.bn_stats(stats[:, t, :], res[:, t, :]))
                    step(dve.bn_aggr(mv[:, t, :], stats[:, t, :]))
                dve.tensor_scalar(rstd[:, :], mv[:, :, 1], EPS, None, ALU.add).then_inc(s_ev, 1)
                dve.wait_ge(s_ep, 3 + k)
                for t in range(TT):
                    last = dve.tensor_scalar(e1[:, t, :], res[:, t, :], mv[:, t, 0:1], rstd[:, t:t + 1],
                                             ALU.subtract, ALU.mult)
                    step(last) if t < TT - 1 or k == 0 else last.then_inc(s_ev, 1)

            def quantise(dst, src, s):
                step(dve.tensor_scalar(src, src, qd[:, s:s + 1], qs[:, 2 * s + 1:2 * s + 2], ALU.mult, ALU.add))
                step(dve.tensor_scalar(src, src, 0.0, 255.0, ALU.max, ALU.min))
                return dve.tensor_scalar(dst, src, MAGIC, -(MAGIC + 128.0), ALU.add, ALU.add)

            for s in range(2):
                step(dve.reciprocal(qd[:, s:s + 1], qs[:, 2 * s:2 * s + 1]))
                step(dve.tensor_scalar(qd[:, 2 + s:3 + s], qs[:, 2 * s + 1:2 * s + 2], -128.0, None, ALU.add))
            step(dve.tensor_tensor(qd[:, 4:5], qs[:, 0:1], qs[:, 2:3], ALU.mult))
            step(dve.scalar_tensor_tensor(qd[:, 5:6], qd[:, 2:3], -1.0, qd[:, 4:5], ALU.mult, ALU.mult))
            step(dve.tensor_copy(ident_bf, ident[:, :]))
            step(dve.memset(ones_bf, 1.0))
            dve.wait_ge(s_ctx, 16)
            step(quantise(q2, ctx_raw, 1))
            layernorm(0)
            quantise(q1, e1, 0).then_inc(s_ev, 1)
            dve.wait_ge(s_ev, 2)
            for t in range(TT):
                step(dve.reduce_sum(rowq[:, t:t + 1], q1[:, t, :], AX_X))
            step(dve.tensor_scalar(qd[:, 6:7], qd[:, 2:3], float(D), None, ALU.mult))
            step(dve.tensor_scalar(rowq[:, :], rowq[:, :], qd[:, 6:7], qd[:, 3:4], ALU.subtract, ALU.mult))
            step(dve.tensor_scalar(rowq[:, :], rowq[:, :], qd[:, 4:5], -1.0, ALU.mult, ALU.mult))
            for t in range(TT):
                step(dve.tensor_scalar(res[:, t, :], res[:, t, :], rowq[:, t:t + 1], None, ALU.add))
            for k in range(DK):
                dve.wait_ge(s_et, k + 1)
                dve.tensor_copy(q1T[:, k, :], (ps_t if k % 2 else ps_y)[:, :].bitcast(BF16)[:, 0:TOK])\
                   .then_inc(s_evq, 1)
            for t in range(TT):
                if t == 0:
                    dve.wait_ge(s_et, DK + 1)
                step(dve.scalar_tensor_tensor(res[:, t, :], ps_df[:, t // 2, :], qd[:, 5:6], res[:, t, :],
                                              ALU.mult, ALU.add))
                dve.wait_ge(s_et, DK + 2 + t)
                src = ps_in[:, t - 2, :] if t >= 2 else ps_o[:, t, :]
                step(dve.scalar_tensor_tensor(res[:, t, :], src, qd[:, 4:5], res[:, t, :], ALU.mult, ALU.add))

            dve.wait_ge(s_ffw, 64)
            layernorm(1)
            step(dve.tensor_copy(perm_row, perm_row_i))
            step(dve.tensor_copy(perm_col, perm_col_i))
            for k in range(DK):
                step(dve.tensor_scalar(take[:, k, :], perm_row, dcol[:, k:k + 1], None, ALU.is_equal))
                step(dve.tensor_scalar(put[:, k, :], iota_row, perm_col[:, k:k + 1], None, ALU.is_equal))
            for k in range(DK):
                dve.wait_ge(s_ft, k + 1)
                src = ps_df[:, k % 2, :]
                step(dve.tensor_copy(h_hi[:, k, :], src))
                dve.tensor_tensor(h_lo[:, k, :], src, h_hi[:, k, :].bitcast(F32), ALU.subtract).then_inc(s_ff, 1)
            for k in range(DK):
                dve.wait_ge(s_ft, DK + k + 1)
                dve.tensor_copy(fT[:, k, :], ps_o[:, k % 2, :]).then_inc(s_ff, 1)
            for k in range(DK):
                dve.wait_ge(s_ft, 2 * DK + k + 1)
                src = ps_o[:, k % 2, :]
                step(dve.tensor_copy(h_hi[:, k, :], src))
                dve.tensor_tensor(h_lo[:, k, :], src, h_hi[:, k, :].bitcast(F32), ALU.subtract).then_inc(s_ff, 1)
            for t in range(TT):
                dve.wait_ge(s_ft, 3 * DK + t + 1)
                dve.tensor_tensor(res[:, t, :], res[:, t, :], ps_df[:, t % 2, :], ALU.add).then_inc(s_store, 1)

        @block.tensor
        def _(pe):
            def split3(dst, lhs, rhs, first, last):
                (lh, ll), (rh, rl) = lhs, rhs
                pe.matmul(dst, lh, rh, start=first, stop=False)
                pe.matmul(dst, lh, rl, start=False, stop=False)
                return pe.matmul(dst, ll, rh, start=False, stop=last)

            pe.wait_ge(s_pp, 5)
            for k in range(DK):
                if k == 0:
                    pe.wait_ge(s_v, 6 * TT)
                if k >= 2:
                    pe.wait_ge(s_v, 6 * TT + 2 * (k - 1))
                for t in range(TT):
                    last = pe.transpose(ps_in[:, k % 2, t * P:(t + 1) * P], v[:, t, k * P:(k + 1) * P], ident[:, :])
                last.then_inc(s_pt, 1)
            pe.wait_ge(s_v, 6 * TT + 2 * DK)
            pe.wait_ge(s_pp, 11)
            for k in range(DK):
                cols = slice(k * P, (k + 1) * P)
                last = split3(ps_y[:, :], (wo_hi[:, dt_slot, cols], wo_lo[:, dt_slot, cols]),
                              (h_hi[:, k, :], h_lo[:, k, :]), k == 0, k == DK - 1)
            last.then_inc(s_pt, 1)
            pe.wait_ge(s_par, 16 * 7)
            pe.wait_ge(s_pp, 8)
            pe.matmul(ps_o[:, 0, 0:GROUPS * CT], sel[:, :], d2[:, :], start=True, stop=True).then_inc(s_pt, 1)
            pe.wait_ge(s_v, 6 * TT + 2 * DK + 7)
            for t in range(TT):
                last = pe.transpose(ps_t[:, t * P:(t + 1) * P], dt_h[:, t * P:(t + 1) * P], ident[:, :])
            last.then_inc(s_pt, 1)
            pe.wait_ge(s_pv, 11)

            def project(n, i, do_ssd):
                pe.wait_ge(s_lo, NIN * n + i + 1)
                if i % 2 or i == 2:
                    wait(pe, s_taps, NCONV * n + (0 if i == 1 else (i + 1) // 2))
                else:
                    wait(pe, s_gate, CT * n + max(i // 2 - 1, 0))
                if do_ssd and i == 0:
                    wait(pe, s_ofi, 2 * (n - 1))
                for k in range(DK):
                    cols = slice(k * P, (k + 1) * P)
                    last = split3(ps_in[:, i % 2, :], (w_hi[:, i % W_RING, cols], w_lo[:, i % W_RING, cols]),
                                  (h_hi[:, k, :], h_lo[:, k, :]), k == 0, k == DK - 1)
                last.then_inc(s_in, 1)

            def turn(n, t):
                pe.wait_ge(s_conv, NCONV * n + t + 3)
                wait(pe, s_tf, (CT + 2) * n + t)
                for c in range(TT):
                    last = pe.transpose(ps_t[:, c * P:(c + 1) * P], hid[:, t, c * P:(c + 1) * P], ident[:, :])
                last.then_inc(s_t, 1)

            def scores_a(n):
                pe.wait_ge(s_tf, (CT + 2) * n + CT)
                for b in range(BATCH):
                    at = b * SEQ
                    last = pe.matmul(ps_t[:, at:at + SEQ], bc[:, 0, at:at + P], bc[:, 1, at:at + SEQ],
                                     start=True, stop=True)
                last.then_inc(s_t, 1)

            def scores_b(n):
                pe.wait_ge(s_tf, (CT + 2) * n + CT + 1)
                for b in range(BATCH):
                    at = b * SEQ + P
                    last = pe.matmul(ps_t[:, b * P:(b + 1) * P], bc[:, 0, at:at + P], bc[:, 1, at:at + P],
                                     start=True, stop=True)
                last.then_inc(s_t, 1)

            def diffs(m, t, banks):
                if t == 0:
                    pe.wait_ge(s_rows, 16 * 8 * (m + 1))
                for k in banks:
                    wait(pe, s_exp, since(3 * CT * m, 3 * t + k, 2))
                    bank = ps_df[:, (3 * t + k) % 2, :]
                    first = True
                    for hh in ((k,) if k < 2 else (0, 1)):
                        h = 2 * t + hh
                        q = slice(32 * (h // 4), 32 * (h // 4) + 6)
                        for b in range(BATCH):
                            at = b * SEQ if k < 2 else b * SEQ + P
                            width = SEQ if k < 2 else P
                            to = b * SEQ if k < 2 else (hh * BATCH + b) * P
                            pe.matmul(bank[:, to:to + width], sta[q, h % 4, at:at + P],
                                      mov[q, h % 4, at:at + width], start=first, stop=False, skip_group_check=True)
                            first = False
                    blocks, count = (bank.rearrange("p (b i) -> p b i", b=BATCH)[:, :, 0:P], BATCH) if k < 2 else \
                        (bank.rearrange("p (b i) -> p b i", b=2 * BATCH), 2 * BATCH)
                    last = pe.matmul(blocks, ident_b[:, :], cut[:, 0:count, :], start=False, stop=True,
                                     skip_group_check=True)
                    last.then_inc(s_df, 1)

            def outputs(m, t):
                pe.wait_ge(s_m, CT * m + t + 1)
                if t == 0:
                    wait(pe, s_ms, m)
                wait(pe, s_z1, CT * m + t)
                for b in range(BATCH):
                    at = b * SEQ
                    for half_seq in range(2):
                        for hh in range(2):
                            rows_ = slice(HD * hh, HD * (hh + 1))
                            w = hdt[:, 2 * b + half_seq, t * P + HD * hh:t * P + HD * (hh + 1)]
                            if half_seq == 0:
                                last = pe.matmul(ps_y[rows_, at:at + SEQ], w, eA[:, t % 2, hh, at:at + SEQ],
                                                 start=True, stop=False, skip_group_check=True)
                            else:
                                last = pe.matmul(ps_y[rows_, at + P:at + SEQ], w,
                                                 eB[:, t % 2, hh, b * P:(b + 1) * P],
                                                 start=False, stop=True, skip_group_check=True)
                last.then_inc(s_y, 1)

            def out_pair(m, j, do_in):
                if j == 0:
                    wait(pe, s_of, 2 * m)
                pe.wait_ge(s_zlo, CT * m + 2 * j + 2)
                pe.wait_ge(s_olo, CT * m + 2 * j + 2)
                last_pair = j == CT // 2 - 1
                for pair in ((2, 3), (0, 1)) if last_pair else ((0, 1), (2, 3)):
                    if j == 0 and pair == (2, 3) and do_in:
                        pe.wait_ge(s_gate, CT * (m + 2))
                        pe.wait_ge(s_taps, NCONV * (m + 2))
                    for k in (2 * j, 2 * j + 1):
                        for t in pair:
                            dst = ps_in[:, t - 2, :] if t >= 2 else ps_o[:, t, :]
                            cols = slice(t * P, (t + 1) * P)
                            last = split3(dst, (z_hi[:, k, cols], z_lo[:, k, cols]),
                                          (wo_hi[:, k % WO_RING, :], wo_lo[:, k % WO_RING, :]), k == 0, k == CT - 1)
                        if last_pair and pair == (2, 3):
                            if k == CT - 1:
                                last.then_inc(s_oin, 1)
                        elif last_pair or pair == (2, 3):
                            last.then_inc(s_ou, 1)

            def iteration(n, do_in, do_ssd):
                m = n - 1
                if do_in:
                    project(n, 0, do_ssd)
                    project(n, 1, do_ssd)
                for t in range(CT):
                    if do_ssd:
                        outputs(m, t)
                        if t + 1 < CT:
                            diffs(m, t + 1, (0, 1))
                    if do_in:
                        project(n, 2 + 2 * t, do_ssd)
                    if do_ssd and t + 1 < CT:
                        diffs(m, t + 1, (2,))
                    if do_in:
                        project(n, 3 + 2 * t, do_ssd)
                        if t:
                            turn(n, t - 1)
                if do_ssd:
                    out_pair(m, 0, do_in)
                    pe.wait_ge(s_sqs, (CT - 1) * (m + 1))
                    pe.wait_ge(s_z1, CT * (m + 1))
                    for t in range(TT):
                        last = pe.matmul(ps_y[:, t:t + 1], sqsum[:, t * P:(t + 1) * P], ones[:, :],
                                         start=True, stop=True)
                    last.then_inc(s_ss, 1)
                if do_in:
                    turn(n, CT - 1)
                if do_ssd:
                    out_pair(m, 1, do_in)
                if do_in:
                    scores_a(n)
                    diffs(n, 0, (0, 1))
                if do_ssd:
                    out_pair(m, 2, do_in)
                if do_in:
                    scores_b(n)
                    diffs(n, 0, (2,))
                if do_ssd:
                    out_pair(m, 3, do_in)

            iteration(0, True, False)
            iteration(1, True, True)
            with pe.Fori(2, loops) as n:
                iteration(n, True, True)
            iteration(loops, False, True)

            pe.wait_ge(s_of, 2 * loops)
            pe.wait_ge(s_ev, 2)
            for k in range(DK):
                if k >= 2:
                    pe.wait_ge(s_evq, k - 1)
                bank = (ps_t if k % 2 else ps_y)[:, :].bitcast(BF16)
                for t in range(TT):
                    last = pe.transpose(bank[:, t * P:(t + 1) * P], q1[:, t, k * P:(k + 1) * P], ident_bf)
                last.then_inc(s_et, 1)
            for b in range(BATCH):
                for k in range(DK):
                    last = pe.matmul(ps_df[:, b, :], ones_bf, q2[:, b, k, :], start=(k == 0), stop=(k == DK - 1))
            last.then_inc(s_et, 1)
            pe.wait_ge(s_evq, DK)
            for t in range(TT):
                dst = ps_in[:, t - 2, :] if t >= 2 else ps_o[:, t, :]
                for k in range(DK):
                    last = pe.matmul(dst, q1T[:, k, t * P:(t + 1) * P], q2[:, t // 2, k, :],
                                     start=(k == 0), stop=(k == DK - 1))
                last.then_inc(s_et, 1)

            pe.wait_ge(s_ev, 4)
            for k in range(DK):
                if k >= 2:
                    pe.wait_ge(s_ff, k - 1)
                for t in range(TT):
                    last = pe.transpose(ps_df[:, k % 2, t * P:(t + 1) * P], e1[:, t, k * P:(k + 1) * P], ident[:, :])
                last.then_inc(s_ft, 1)
            pe.wait_ge(s_ff, DK)
            for k in range(DK):
                if k >= 2:
                    pe.wait_ge(s_ff, DK + k - 1)
                for d in range(DK):
                    for part in (h_hi, h_lo):
                        last = pe.matmul(ps_o[:, k % 2, :], take[:, d, k * P:(k + 1) * P], part[:, d, :],
                                         start=(d == 0 and part is h_hi), stop=(d == DK - 1 and part is h_lo))
                last.then_inc(s_ft, 1)
            pe.wait_ge(s_ff, 2 * DK)

            def up_product(h):
                if h >= 2:
                    pe.wait_ge(s_gl, h - 1)
                r = slice(32 * (h % 4), 32 * (h % 4) + 32)
                pe.matmul(ps_in[:, h % 2, :], up_sb[r, h // 4, :], fT[r, h // 4, :],
                          start=True, stop=True).then_inc(s_gt, 1)

            def down_product(h):
                pe.wait_ge(s_gl, h + 1)
                k = h // 4
                if h % 4 == 0 and k >= 2:
                    pe.wait_ge(s_ff, 2 * DK + k - 1)
                last = pe.matmul(ps_o[32 * (h % 4):32 * (h % 4) + 32, k % 2, :], down_sb[:, h, :],
                                 gel[h // CT][:, h % CT, :], start=True, stop=True, skip_group_check=True)
                if h % 4 == 3:
                    last.then_inc(s_ft, 1)

            for h in range(FH + 2):
                if h < FH:
                    up_product(h)
                if h >= 2:
                    down_product(h - 2)
            pe.wait_ge(s_ff, 3 * DK)
            for t in range(TT):
                if t >= 2:
                    pe.wait_ge(s_store, t - 1)
                for k in range(DK):
                    for part in (h_hi, h_lo):
                        last = pe.matmul(ps_df[:, t % 2, :], part[:, k, t * P:(t + 1) * P], put[:, k, :],
                                         start=(k == 0 and part is h_hi), stop=(k == DK - 1 and part is h_lo))
                last.then_inc(s_ft, 1)


_INS = ["x", "ctx", "w_in", "w_dt", "w_out", "conv_par", "norm_w", "dt_bias", "a_log", "d_skip", "gnorm",
        "quant", "up", "down", "perm", "perm_by_part"]


def lay_out(np, i):
    w = np.asarray(i["L0_attn_in_proj_w"])
    bcn = GROUPS * P

    def tiles(rows):
        r = rows.reshape(-1, P, DK, P)
        return r.transpose(0, 3, 2, 1)

    gate_t = tiles(w[:INNER]).reshape(GROUPS, CT, P, DK, P)
    hid_t = tiles(w[INNER:2 * INNER]).reshape(GROUPS, CT, P, DK, P)
    b_t = tiles(w[2 * INNER:2 * INNER + bcn]).reshape(GROUPS, 1, P, DK, P)
    c_t = tiles(w[2 * INNER + bcn:2 * INNER + 2 * bcn]).reshape(GROUPS, 1, P, DK, P)
    by_turns = np.stack([gate_t, hid_t], axis=2).reshape(GROUPS, 2 * CT, P, DK, P)
    w_in = np.concatenate([b_t, c_t, by_turns], axis=1).reshape(GROUPS, NIN, P, DK * P)
    w_dt = tiles(w[2 * INNER + 2 * bcn:]).reshape(P, DK * P)
    w_out = np.asarray(i["L0_attn_out_proj_w"]).T.reshape(GROUPS, CT, P, D)

    par = np.concatenate([np.asarray(i["L0_attn_conv_w"]), np.asarray(i["L0_attn_conv_b"])[:, None]], axis=1)
    hp = par[:INNER].reshape(GROUPS, CT, P, PAR)
    bp = par[INNER:INNER + bcn].reshape(GROUPS, 1, P, PAR)
    cp = par[INNER + bcn:].reshape(GROUPS, 1, P, PAR)
    conv_par = np.concatenate([bp, cp, hp], axis=1).transpose(2, 0, 1, 3).reshape(P, GROUPS, NCONV * PAR)
    quant = np.concatenate([np.asarray(i["L0_xattn_" + n]) for n in ("x1_scale", "x1_zp", "x2_scale", "x2_zp")])
    return {
        "x": np.asarray(i["x"]).reshape(TOK, D),
        "ctx": np.asarray(i["ctx_4096"]),
        "w_in": w_in, "w_dt": w_dt, "w_out": w_out, "conv_par": conv_par,
        "norm_w": np.asarray(i["L0_attn_norm_w"]).reshape(DK, P).T,
        "dt_bias": np.asarray(i["L0_attn_dt_bias"]).reshape(HEADS, 1),
        "a_log": np.asarray(i["L0_attn_A_log"]).reshape(HEADS, 1),
        "d_skip": np.asarray(i["L0_attn_Dp"]).reshape(GROUPS * CT, 2).T,
        "gnorm": np.asarray(i["L0_attn_gnorm_w"]).reshape(GROUPS * CT, P).T,
        "quant": quant,
        "up": np.asarray(i["L0_ffn_up"]).reshape(DK, P, FM).transpose(1, 0, 2),
        "down": np.asarray(i["L0_ffn_down"]).transpose(1, 0, 2),
        "perm": np.asarray(i["L0_ffn_perm"]),
        "perm_by_part": np.asarray(i["L0_ffn_perm"]).reshape(DK, P).T,
    }


def kernel(**inputs):
    import numpy as np
    import concourse.bacc as bacc
    from concourse.bass_utils import run_bass_kernel_spmd

    nc = bacc.Bacc("TRN2", target_bir_lowering=False, num_devices=1)
    laid = lay_out(np, inputs)
    arrays, args = {}, []
    for name in _INS:
        a = np.ascontiguousarray(laid[name])
        arrays[f"in_{name}"] = a
        args.append(nc.dram_tensor(f"in_{name}", a.shape, mybir.dt.from_np(a.dtype), kind="ExternalInput").ap())
    args.append(nc.dram_tensor("out_x", (TOK, D), F32, kind="ExternalOutput").ap())
    decoder_layer(nc, *args)
    r = run_bass_kernel_spmd(nc, [arrays], core_ids=[0])
    return r.results[0]["out_x"].reshape(BATCH, SEQ, D)
```

```python
from contextlib import ExitStack

import concourse.bass as bass
from concourse import mybir

F32 = mybir.dt.float32
F32R = mybir.dt.float32r
BF16 = mybir.dt.bfloat16
I32 = mybir.dt.int32
ALU = mybir.AluOpType
ACT = mybir.ActivationFunctionType
AX_X = mybir.AxisListType.X

P = 128
BATCH, SEQ, D = 2, 256, 512
TOK = BATCH * SEQ
TT = TOK // P
DK = D // P
GROUPS, HEADS, HD = 8, 128, 64
GH = HEADS // GROUPS
INNER = HEADS * HD
GC = INNER // GROUPS
CT = GC // P
NIN = 2 + 2 * CT
NCONV = 2 + CT
TAPS = 4
PAR = TAPS + 1
EPS = 1e-5
W_RING, RAW_RING = 6, 3
WO_RING, RAWO_RING = 4, 2
CTX = 512
CUT = -1e30
FH, FD, FM = 16, 32, 128
MAGIC = 1.5 * 2.0 ** 23


def since(base, i, ring):
    return base + max(i + 1 - ring, 0)


def wait(eng, sem, value):
    if isinstance(value, int) and value <= 0:
        return
    eng.wait_ge(sem, value)


def decoder_layer(nc, x, ctx_in, w_in, w_dt, w_out, conv_par, norm_w, dt_bias, a_log, d_skip,
                  gnorm, quant, up, down, perm, perm_by_part, out):
    acs_dram = nc.dram_tensor("acs_parts", [3, HEADS, TOK], BF16, kind="Internal").ap()

    with ExitStack() as ctx:
        def sb(name, shape, dt=F32):
            return ctx.enter_context(nc.sbuf_tensor(name, shape, dt))

        def psum(name, shape):
            return ctx.enter_context(nc.psum_tensor(name, shape, F32))

        def sem(name):
            return ctx.enter_context(nc.semaphore(name))

        res = sb("res", [P, TT, D])
        h_hi = sb("h_hi", [P, DK, TOK], F32R)
        h_lo = sb("h_lo", [P, DK, TOK], F32R)
        raw = sb("raw", [P, RAW_RING, DK * P])
        w_hi = sb("w_hi", [P, W_RING, DK * P], F32R)
        w_lo = sb("w_lo", [P, W_RING, DK * P], F32R)
        rawo = sb("rawo", [P, RAWO_RING, D])
        wo_hi = sb("wo_hi", [P, WO_RING, D], F32R)
        wo_lo = sb("wo_lo", [P, WO_RING, D], F32R)
        hid = sb("hid", [P, CT, TOK])
        gate = sb("gate", [P, CT, TOK])
        bc = sb("bc", [P, 2, TOK])
        th = sb("th", [P, 2, TOK])
        gth = sb("gth", [P, TOK])
        hdt = sb("hdt", [P, TT, GC])
        gmA = sb("gmA", [P, BATCH, SEQ])
        gmB = sb("gmB", [P, BATCH, P])
        eA = sb("eA", [P, 2, 2, TOK])
        eB = sb("eB", [P, 2, 2, BATCH * P])
        z = sb("z", [P, 2, TOK])
        z_hi = sb("z_hi", [P, CT, TOK], F32R)
        z_lo = sb("z_lo", [P, CT, TOK], F32R)
        sq = sb("sq", [P, TOK])
        sqsum = sb("sqsum", [P, TOK])
        mov = sb("mov", [P, 4, TOK], BF16)
        sta = sb("sta", [P, 4, TOK], BF16)
        cut = sb("cut", [P, 2 * BATCH, P], BF16)
        ident_b = sb("ident_b", [P, P], BF16)
        ident = sb("ident", [P, P])
        ones = sb("ones", [P, 1])
        convp = sb("convp", [P, GROUPS, NCONV * PAR])
        curc = sb("curc", [P, NCONV * PAR])
        skipgn = sb("skipgn", [P, GROUPS, 2 * CT])
        curs = sb("curs", [P, 2 * CT])
        dtT = sb("dtT", [P, TT, HEADS])
        dtg = sb("dtg", [P, TT, GH])
        nw = sb("nw", [P, DK])
        gn_in = sb("gn_in", [P, GROUPS * CT])
        d2 = sb("d2", [2, GROUPS * CT])
        sel = sb("sel", [2, P])
        hcol = sb("hcol", [P, 3])
        half = sb("half", [P, 2, TT])
        stats = sb("stats", [P, TT, 6])
        mv = sb("mv", [P, TT, 2])
        rstd = sb("rstd", [P, TT])
        rstds = sb("rstds", [P, 2, TT])
        ssum = sb("ssum", [P, TT])
        rgrp = sb("rgrp", [P, TT])
        qs = sb("qs", [P, 4])
        qd = sb("qd", [P, 8])
        qa = sb("qa", [P, TT])
        qb = sb("qb", [P, TT])
        rowq = sb("rowq", [P, TT])
        ones_b = sb("ones_b", [P, P], BF16)
        perm_row = sb("perm_row", [P, D])
        iota_row = sb("iota_row", [P, D])
        perm_col_i = sb("perm_col_i", [P, DK], I32)
        perm_col = sb("perm_col", [P, DK])
        dcol = sb("dcol", [P, DK])

        ps_in = psum("ps_in", [P, 2, 512])
        ps_df = psum("ps_df", [P, 2, 512])
        ps_y = psum("ps_y", [P, 512])
        ps_t = psum("ps_t", [P, 512])
        ps_o = psum("ps_o", [P, 2, 512])

        s_x = [sem(f"x_loaded{t}") for t in range(TT)]
        s_par = sem("params_loaded")
        s_wdt = sem("wdt_loaded")
        s_raw = [sem(f"raw_loaded{i}") for i in range(RAW_RING)]
        s_rawo = [sem(f"rawo_loaded{i}") for i in range(RAWO_RING)]
        s_hi = sem("w_hi_done")
        s_lo = sem("w_lo_done")
        s_ohi = sem("wo_hi_done")
        s_olo = sem("wo_lo_done")
        s_in = sem("in_ready")
        s_tap0 = sem("tap0_done")
        s_taps = sem("taps_done")
        s_cth = sem("conv_tanh_done")
        s_conv = sem("conv_done")
        s_gth = sem("gate_tanh_done")
        s_gate = sem("gate_done")
        s_t = sem("turn_ready")
        s_tf = sem("turn_free")
        s_rows = sem("rows_loaded")
        s_df = sem("diff_ready")
        s_exp = sem("exp_done")
        s_m = sem("decay_ready")
        s_y = sem("y_ready")
        s_z1 = sem("y_free")
        s_z = sem("z_done")
        s_zhi = sem("z_hi_done")
        s_zlo = sem("z_lo_done")
        s_sq = sem("square_done")
        s_sqs = sem("square_sum_done")
        s_ss = sem("token_sum_ready")
        s_ms = sem("mean_square_done")
        s_r = sem("rms_done")
        s_ou = sem("wo_used")
        s_oin = sem("out_in_ready")
        s_ofi = sem("out_added_in")
        s_of = sem("out_added")
        s_cur = sem("in_params")
        s_curs = sem("ssd_params")
        s_v = sem("vector_step")
        s_var = sem("variances")
        s_rst = sem("input_rstds")
        s_nt = sem("normed_tile")
        s_nT = sem("normed_turned")
        s_nhi = sem("normed_hi")
        s_nlo = sem("normed_lo")
        s_u = sem("layernormed")
        s_res = sem("residual_started")
        s_dt = sem("dt_projected")
        s_dtv = sem("dt_vector")
        s_dta = sem("dt_scalar")
        s_dtt = sem("dt_turned")
        s_dtT = sem("dt_kept")
        s_skip = sem("skip_spread")
        s_rows1 = sem("rows_of_ones")
        s_vt = sem("vector_tap")
        s_pa = sem("prologue_scalar")
        s_pp = sem("prologue_gpsimd")
        s_acs = sem("acs_stored")
        s_dtw = sem("dt_weights_split")
        s_perm = sem("perm_loaded")
        s_iota = sem("numbers_ready")
        s_ctx = [sem(f"context_loaded{c}") for c in range(BATCH * DK)]
        s_cs = sem("context_scaled")
        s_q2 = sem("context_quantised")
        s_ffw = sem("ffn_loaded")
        s_tp = sem("take_put_ready")
        s_uph = sem("up_hi_done")
        s_upl = sem("up_lo_done")
        s_cq = sem("q2_sums_ready")
        s_ev = sem("variance_ready")
        s_ep = sem("rstd_ready")
        s_aff = sem("quant_scales")
        s_x1 = sem("norm_scaled")
        s_q1 = sem("norm_quantised")
        s_q1t = sem("q1_turned")
        s_q1a = sem("q1T_kept_scalar")
        s_q1v = sem("q1T_kept_vector")
        s_rs = sem("q1_sums_ready")
        s_rq = sem("row_terms_ready")
        s_pr = sem("product_ready")
        s_px = sem("product_scaled")
        s_f = sem("features")
        s_ft = sem("features_turned")
        s_fhi = sem("features_hi")
        s_flo = sem("features_lo")
        s_p = sem("features_permuted")
        s_phi = sem("permuted_hi")
        s_plo = sem("permuted_lo")
        s_up = sem("up_ready")
        s_gl = sem("gelu_done")
        s_dn = sem("down_ready")
        s_dlo = sem("down_split")
        s_fin = sem("ffn_ready")
        s_store = sem("out_tile_ready")
        s_out = sem("out_stored")

        v = hdt[:, 2:4, :].rearrange("p a (b n) -> p (a b) n", b=2)
        u = eA[:, :, :, :].rearrange("p a b n -> p (a b) n")
        sp_e, sp_w, dt_h, acs = (hid[:, i, :] for i in range(4, 8))
        sp_v, sp_a = gate[:, 4, :], gate[:, 5, :]
        sp_c, sp_l = (eB[:, i, :, :].rearrange("p a n -> p (a n)") for i in range(2))
        r1, r2, one_row, sp_r = z[:, 0, :], z[:, 1, :], sq[:, :], sqsum[:, :]
        parts = gate[:, 6:8, :].bitcast(BF16).rearrange("p a n -> p (a n)")[:, 0:3 * TOK].rearrange(
            "p (r n) -> p r n", r=3)
        wdt_raw = rawo[:, 0, :]
        dt_slot = WO_RING - 1
        ctx_raw = [raw[:, 0, :], raw[:, 1, :], raw[:, 2, :], th[:, 0, :], th[:, 1, :], gth[:, :], bc[:, 0, :],
                   bc[:, 1, :]]
        q2 = hid[:, 0:4, :].rearrange("p a n -> p (a n)").bitcast(BF16).rearrange("p (c n) -> p c n", c=BATCH * DK)
        e1 = hdt[:, 2:4, :].rearrange("p a (b n) -> p (a b) n", b=2)
        q1 = eA[:, 0, :, :].rearrange("p a n -> p (a n)").bitcast(BF16).rearrange("p (t d) -> p t d", t=TT)
        q1T = eA[:, 1, :, :].rearrange("p a n -> p (a n)").bitcast(BF16).rearrange("p (k n) -> p k n", k=DK)
        perm_row_i = rawo[:, 1, :].bitcast(I32)
        take = w_hi[:, 0:DK, :]
        put = w_lo[:, 0:DK, :]
        up_raw, up_hi, up_lo = (a[:, 0, :].rearrange("p (a m) -> p a m", a=DK) for a in (rawo, wo_hi, wo_lo))
        down_sb = rawo[:, 1, :].rearrange("p (h d) -> p h d", h=FH)
        f_hi, f_lo = h_hi, h_lo
        p_hi, p_lo = z_hi, z_lo
        gel = gate

        def out_bank(t):
            return ps_in[:, t - 2, :] if t >= 2 else ps_o[:, t, :]

        def feature_bank(k):
            return (ps_df[:, 0, :], ps_df[:, 1, :], ps_y[:, :], ps_t[:, :])[k]

        def permuted_bank(k):
            return (ps_in if k < 2 else ps_o)[:, k % 2, :]

        def final_bank(t):
            return (ps_df if t < 2 else ps_o)[:, t % 2, :]

        def turned_bank(k):
            return (ps_df if k < 2 else ps_o)[:, k % 2, :]

        def first_tiles(n):
            if isinstance(n, int) and n < 2:
                return range(W_RING) if n == 0 else range(0)
            return range(4)

        def step_tiles(n, t):
            if isinstance(n, int) and n == 0:
                return range(W_RING + 2 * t, W_RING + 2 * t + 2)
            return range(4 + 2 * t, min(4 + 2 * t + 2, NIN))

        def out_tile_at(t):
            return {0: 2, 1: 3, 3: 4, 4: 5, 5: 6, 6: 7}.get(t)

        def bank_in(n, i):
            if isinstance(n, int) and n == 0 and i % 4 >= 2:
                return ps_o[:, i % 2, :]
            return ps_in[:, i % 2, :]

        loops = GROUPS
        last_m = GROUPS - 1

        block = ctx.enter_context(nc.Block())

        @block.sync
        def _(sp):
            for t in range(TT):
                sp.dma_start(res[:, t, :], x[t * P:(t + 1) * P, :]).then_inc(s_x[t], 16)
            loads = [(nw[:, :], norm_w), (hcol[:, 0:1], dt_bias), (hcol[:, 1:2], a_log), (d2[:, :], d_skip),
                     (gn_in[:, :], gnorm), (convp[:, :, :], conv_par),
                     (qs[:, :], quant.partition_broadcast(P))]
            for dst, src in loads:
                sp.dma_start(dst, src).then_inc(s_par, 16)
            sp.dma_start(wdt_raw, w_dt).then_inc(s_wdt, 16)
            sp.dma_start(perm_row_i, perm.partition_broadcast(P)).then_inc(s_perm, 16)
            sp.dma_start(perm_col_i[:, :], perm_by_part).then_inc(s_perm, 16)

            def rows(g):
                for q in range(4):
                    src = acs_dram[:, bass.ds(g * GH + 4 * q, 4), :]
                    sp.dma_start(mov[32 * q:32 * q + 3, :, :], src).then_inc(s_rows, 16)
                    sp.dma_start(sta[32 * q + 3:32 * q + 6, :, :], src).then_inc(s_rows, 16)

            def load_in(n, i):
                wait(sp, s_lo, since(NIN * n, i, RAW_RING))
                sp.dma_start(raw[:, i % RAW_RING, :], w_in[bass.ds(n, 1), i, :, :]
                             .rearrange("a p c -> (a p) c")).then_inc(s_raw[i % RAW_RING], 16)

            def load_out(m, q):
                wait(sp, s_olo, since(CT * m, q, RAWO_RING))
                sp.dma_start(rawo[:, q % RAWO_RING, :], w_out[bass.ds(m, 1), q, :, :]
                             .rearrange("a p c -> (a p) c")).then_inc(s_rawo[q % RAWO_RING], 16)

            def iteration(n, do_in, do_ssd):
                m = n - 1
                if not do_ssd:
                    for i in range(NIN + 4):
                        load_in(n + i // NIN, i % NIN)
                        if i == 12:
                            sp.wait_ge(s_dtv, 4)
                            sp.dma_start(acs_dram.rearrange("r h t -> h r t"), parts).then_inc(s_acs, 16)
                        if i == 15:
                            sp.wait_ge(s_acs, 16)
                            sp.wait_ge(s_rows1, 2)
                            rows(n)
                    return
                for i in range(NIN):
                    if do_in and not (isinstance(n, int) and n == 1 and i < 4):
                        load_in(n, i)
                    if i >= 13 and i % 2:
                        load_out(m, (i - 13) // 2)
                if do_in:
                    sp.wait_ge(s_df, 3 * CT * m + 3 * CT)
                    rows(n)
                if do_ssd:
                    for q in range(3, CT):
                        load_out(m, q)

            iteration(0, True, False)
            iteration(1, True, True)
            with sp.Fori(2, loops) as n:
                iteration(n, True, True)

            def load_context(blocks):
                for c in blocks:
                    sp.dma_start(ctx_raw[c], ctx_in[c // DK, (c % DK) * P:(c % DK + 1) * P, :])\
                      .then_inc(s_ctx[c], 16)

            sp.wait_ge(s_lo, NIN * GROUPS)
            load_context((0, 1, 2))
            load_out(last_m, 0)
            load_out(last_m, 1)
            sp.wait_ge(s_conv, NCONV * GROUPS)
            sp.wait_ge(s_gate, CT * GROUPS)
            load_context((3, 4, 5))
            sp.wait_ge(s_t, (CT + 2) * GROUPS)
            load_context((6, 7))
            for q in range(2, CT):
                load_out(last_m, q)
            sp.wait_ge(s_olo, CT * GROUPS)
            sp.dma_start(up_raw, up).then_inc(s_ffw, 16)
            sp.dma_start(down_sb, down).then_inc(s_ffw, 16)
            for t in range(TT):
                sp.wait_ge(s_store, t + 1)
                sp.dma_start(out[t * P:(t + 1) * P, :], res[:, t, :]).then_inc(s_out, 16)
            sp.wait_ge(s_out, 16 * TT)

        @block.gpsimd
        def _(pool):
            pool.memset(ident[:, :], 0.0).then_inc(s_pp, 1)
            pool.memset(half[:, :, :], -0.5).then_inc(s_pp, 1)
            pool.memset(cut[:, :, :], 0.0).then_inc(s_pp, 1)
            pool.memset(sel[:, :], 1.0).then_inc(s_pp, 1)
            pool.wait_ge(s_pp, 4)
            pool.affine_select(out=ident[:, :], in_=ident[:, :], compare_op=ALU.not_equal, fill=1.0, base=0,
                               pattern=[[-1, P]], channel_multiplier=1).then_inc(s_pp, 1)
            pool.affine_select(out=cut[:, :, :], in_=cut[:, :, :], compare_op=ALU.is_ge, fill=CUT, base=0,
                               pattern=[[0, 2 * BATCH], [1, P]], channel_multiplier=-1).then_inc(s_pp, 1)
            pool.affine_select(out=sel[:, :], in_=sel[:, :], compare_op=ALU.is_ge, fill=0.0, base=0,
                               pattern=[[1, P]], channel_multiplier=-HD).then_inc(s_pp, 1)
            pool.wait_ge(s_pp, 7)
            pool.affine_select(out=sel[:, :], in_=sel[:, :], compare_op=ALU.is_ge, fill=0.0, base=HD - 1,
                               pattern=[[-1, P]], channel_multiplier=HD).then_inc(s_pp, 1)
            pool.iota(iota_row[:, :], [[1, D]], base=0, channel_multiplier=0,
                      allow_small_or_imprecise_dtypes=True).then_inc(s_iota, 1)
            pool.iota(dcol[:, :], [[P, DK]], base=0, channel_multiplier=1,
                      allow_small_or_imprecise_dtypes=True).then_inc(s_iota, 1)
            pool.memset(mov[:, :, :], -1.0).then_inc(s_rows1, 1)
            pool.memset(sta[:, :, :], 1.0).then_inc(s_rows1, 1)
            pool.wait_ge(s_var, 2)
            pool.tensor_tensor(rstds[:, :, :], rstds[:, :, :], half[:, :, :], ALU.pow).then_inc(s_rst, 1)

            def split_in(n, i):
                pool.wait_ge(s_hi, NIN * n + i + 1)
                wait(pool, s_in, since(NIN * n, i, W_RING))
                pool.tensor_tensor(w_lo[:, i % W_RING, :], raw[:, i % RAW_RING, :],
                                   w_hi[:, i % W_RING, :].bitcast(F32), ALU.subtract).then_inc(s_lo, 1)

            def split_out(m, q):
                pool.wait_ge(s_ohi, CT * m + q + 1)
                wait(pool, s_ou, since(CT * m, q, WO_RING))
                pool.tensor_tensor(wo_lo[:, q % WO_RING, :], rawo[:, q % RAWO_RING, :],
                                   wo_hi[:, q % WO_RING, :].bitcast(F32), ALU.subtract).then_inc(s_olo, 1)

            def add_square(m, t):
                pool.wait_ge(s_sq, CT * m + t + 1)
                if t > 1:
                    pool.wait_ge(s_sqs, (CT - 1) * m + t - 1)
                pool.tensor_tensor(sqsum[:, :], sqsum[:, :], sq[:, :], ALU.add).then_inc(s_sqs, 1)

            def group_rms(m):
                pool.wait_ge(s_ms, m + 1)
                pool.tensor_tensor(rgrp[:, :], ssum[:, :], half[:, 0, :], ALU.pow).then_inc(s_r, 1)

            def iteration(n, do_in, do_ssd):
                m = n - 1
                if do_in:
                    for i in first_tiles(n):
                        split_in(n, i)
                        if not do_ssd and i == 0:
                            pool.wait_ge(s_pa, 2)
                            pool.tensor_tensor(wo_lo[:, dt_slot, :], wdt_raw, wo_hi[:, dt_slot, :].bitcast(F32),
                                               ALU.subtract).then_inc(s_dtw, 1)
                for t in range(CT):
                    if do_in:
                        for i in step_tiles(n, t):
                            split_in(n, i)
                    if not do_ssd and t >= CT - TT:
                        k = t - (CT - TT)
                        pool.wait_ge(s_u, k + 1)
                        pool.tensor_tensor(res[:, k, :], res[:, k, :], u[:, k, :], ALU.add)\
                            .then_inc(s_res, 1)
                    if do_ssd:
                        if t:
                            add_square(m, t)
                        if t >= 4:
                            split_out(m, t - 4)
                if do_ssd:
                    split_out(m, 4)
                    split_out(m, 5)
                    group_rms(m)
                    split_out(m, 6)
                    split_out(m, 7)

            iteration(0, True, False)
            iteration(1, True, True)
            with pool.Fori(2, loops) as n:
                iteration(n, True, True)

            for q in range(2):
                split_out(last_m, q)
            for t in range(CT):
                if t:
                    add_square(last_m, t)
                if out_tile_at(t):
                    split_out(last_m, out_tile_at(t))
            group_rms(last_m)

            pool.wait_ge(s_uph, 1)
            pool.tensor_tensor(up_lo, up_raw, up_hi.bitcast(F32), ALU.subtract).then_inc(s_upl, 1)
            for k in range(2):
                pool.wait_ge(s_ev, k + 1)
                pool.tensor_tensor(rstd[:, :], rstd[:, :], half[:, 0, :], ALU.pow).then_inc(s_ep, 1)

        @block.scalar
        def _(act):
            def cast_in(n, i):
                act.wait_ge(s_raw[i % RAW_RING], (NIN // RAW_RING * 16) * n + 16 * (i // RAW_RING + 1))
                wait(act, s_in, since(NIN * n, i, W_RING))
                act.activation(w_hi[:, i % W_RING, :], raw[:, i % RAW_RING, :], ACT.Copy).then_inc(s_hi, 1)

            def cast_out(m, q):
                act.wait_ge(s_rawo[q % RAWO_RING], (CT // RAWO_RING * 16) * m + 16 * (q // RAWO_RING + 1))
                wait(act, s_ou, since(CT * m, q, WO_RING))
                act.activation(wo_hi[:, q % WO_RING, :], rawo[:, q % RAWO_RING, :], ACT.Copy).then_inc(s_ohi, 1)

            def conv_dst(c):
                return bc[:, c, :] if c < 2 else hid[:, c - 2, :]

            def tap0(n, c, do_ssd):
                i = c if c < 2 else 2 * c - 1
                act.wait_ge(s_in, NIN * n + i + 1)
                if c == 0:
                    act.wait_ge(s_cur, 2 * n + 1)
                if c < 2:
                    wait(act, s_t, (CT + 2) * n)
                elif do_ssd:
                    act.wait_ge(s_z1, CT * (n - 1) + c - 1)
                act.activation(conv_dst(c), bank_in(n, i), ACT.Identity, scale=curc[:, c * PAR + 3:c * PAR + 4],
                               bias=curc[:, c * PAR + 4:c * PAR + 5]).then_inc(s_tap0, 1)

            def conv_tanh(n, c):
                act.wait_ge(s_taps, NCONV * n + c + 1)
                wait(act, s_conv, since(NCONV * n, c, 2))
                act.activation(th[:, c % 2, :], conv_dst(c), ACT.Tanh, scale=0.5).then_inc(s_cth, 1)

            def gate_tanh(n, t):
                act.wait_ge(s_in, NIN * n + 3 + 2 * t)
                wait(act, s_gate, CT * n + t)
                act.activation(gth[:, :], bank_in(n, 2 + 2 * t), ACT.Tanh, scale=0.5).then_inc(s_gth, 1)

            def exps(m, t, banks):
                for k in banks:
                    act.wait_ge(s_df, 3 * CT * m + 3 * t + k + 1)
                    if k == 0:
                        if isinstance(m, int) and m == 0 and t == 0:
                            act.wait_ge(s_res, TT)
                        wait(act, s_y, since(CT * m, t, 2))
                    dst = eA[:, t % 2, k, :] if k < 2 else eB[:, t % 2, :, :].rearrange("p a n -> p (a n)")
                    act.activation(dst, ps_df[:, (3 * t + k) % 2, :], ACT.Exp).then_inc(s_exp, 1)

            def z_high_and_square(m, t):
                act.wait_ge(s_z, CT * m + t + 1)
                wait(act, s_ou, CT * m)
                act.activation(z_hi[:, t, :], z[:, t % 2, :], ACT.Copy,
                               scale=curs[:, CT + t:CT + t + 1]).then_inc(s_zhi, 1)
                if t == 0:
                    wait(act, s_ss, m)
                else:
                    wait(act, s_sqs, (CT - 1) * m + t - 1)
                act.activation(sqsum[:, :] if t == 0 else sq[:, :], z[:, t % 2, :],
                               ACT.Square).then_inc(s_sq, 1)

            def iteration(n, do_in, do_ssd):
                m = n - 1
                if do_in:
                    for i in (range(2, 4) if not do_ssd else first_tiles(n)):
                        cast_in(n, i)
                    tap0(n, 0, do_ssd)
                    if not do_ssd:
                        dt_exp()
                    tap0(n, 1, do_ssd)
                    if not do_ssd:
                        cast_in(n, 4)
                        cast_in(n, 5)
                    conv_tanh(n, 0)
                    conv_tanh(n, 1)
                    if not do_ssd:
                        dt_log()
                for t in range(CT):
                    if do_in:
                        if t:
                            tap0(n, t + 1, do_ssd)
                    if do_ssd and t + 1 < CT:
                        exps(m, t + 1, (0, 1))
                    if not do_ssd:
                        gate_tanh(n, t)
                    if do_in and t:
                        conv_tanh(n, t + 1)
                    if do_ssd:
                        z_high_and_square(m, t)
                        if t + 1 < CT:
                            exps(m, t + 1, (2,))
                    if do_in:
                        if do_ssd:
                            gate_tanh(n, t)
                        for i in step_tiles(n, t):
                            cast_in(n, i)
                    if do_ssd and t >= 4:
                        cast_out(m, t - 4)
                if do_in:
                    tap0(n, CT + 1, do_ssd)
                    conv_tanh(n, CT + 1)
                if do_ssd:
                    cast_out(m, 4)
                    cast_out(m, 5)
                if do_in:
                    exps(n, 0, (0, 1))
                if do_ssd:
                    cast_out(m, 6)
                    cast_out(m, 7)
                if do_in:
                    exps(n, 0, (2,))

            def dt_exp():
                act.wait_ge(s_dtv, 1)
                act.activation(sp_e, sp_a, ACT.Exp, scale=-1.0).then_inc(s_dta, 1)

            def dt_log():
                act.wait_ge(s_dtv, 2)
                act.activation(sp_l, sp_w, ACT.Ln).then_inc(s_dta, 1)
                act.preload_act_table(ACT.Exp)
                act.wait_ge(s_dta, 2)
                act.activation(sp_r, sp_l, ACT.Exp, scale=-1.0).then_inc(s_dta, 1)

            act.wait_ge(s_par, 16 * 7)
            act.activation(hcol[:, 2:3], hcol[:, 1:2], ACT.Exp).then_inc(s_pa, 1)
            cast_in(0, 0)
            act.wait_ge(s_nT, TT)
            for k in range(DK):
                act.activation(h_hi[:, k, :], turned_bank(k), ACT.Copy, scale=nw[:, k:k + 1]).then_inc(s_nhi, 1)
            act.wait_ge(s_wdt, 16)
            act.activation(wo_hi[:, dt_slot, :], wdt_raw, ACT.Copy).then_inc(s_pa, 1)
            cast_in(0, 1)
            iteration(0, True, False)
            iteration(1, True, True)
            with act.Fori(2, loops) as n:
                iteration(n, True, True)

            cast_out(last_m, 0)
            cast_out(last_m, 1)
            for t in range(CT):
                if t + 1 < CT:
                    exps(last_m, t + 1, (0, 1, 2))
                z_high_and_square(last_m, t)
                if out_tile_at(t):
                    cast_out(last_m, out_tile_at(t))
                act.wait_ge(s_ctx[t], 16)
                act.activation(ctx_raw[t], ctx_raw[t], ACT.Identity, scale=qd[:, 1:2], bias=qs[:, 3:4])\
                   .then_inc(s_cs, 1)
            act.wait_ge(s_ffw, 32)
            act.wait_ge(s_ou, CT * GROUPS)
            act.activation(up_hi, up_raw, ACT.Copy).then_inc(s_uph, 1)
            act.preload_act_table(ACT.Gelu)

            act.wait_ge(s_aff, 1)
            for t in range(TT):
                act.activation(e1[:, t, :], res[:, t, :], ACT.Identity, scale=qa[:, t:t + 1],
                               bias=qb[:, t:t + 1]).then_inc(s_x1, 1)
            act.wait_ge(s_q1t, 1)
            act.activation(q1T[:, 0:2, :].rearrange("p a n -> p (a n)"), ps_y[:, :].bitcast(BF16), ACT.Copy)\
               .then_inc(s_q1a, 1)
            act.wait_ge(s_rq, 1)
            for t in range(TT):
                act.wait_ge(s_pr, t + 1)
                act.activation(e1[:, t, :], out_bank(t), ACT.Identity, scale=qd[:, 4:5], bias=rowq[:, t:t + 1])\
                   .then_inc(s_px, 1)

            act.wait_ge(s_ft, 1)
            for k in range(DK):
                act.activation(f_hi[:, k, :], feature_bank(k), ACT.Copy).then_inc(s_fhi, 1)
            for k in range(DK):
                act.wait_ge(s_p, k + 1)
                act.activation(p_hi[:, k, :], permuted_bank(k), ACT.Copy).then_inc(s_phi, 1)
            for h in range(FH):
                act.wait_ge(s_up, h + 1)
                if h >= CT:
                    act.wait_ge(s_dn, (h - CT) // 4 + 1)
                act.activation(gel[:, h % CT, :], ps_in[:, h % 2, :], ACT.Gelu).then_inc(s_gl, 1)

        @block.vector
        def _(dve):
            chain = [0]

            def step(ins):
                chain[0] += 1
                ins.then_inc(s_v, 1)
                dve.wait_ge(s_v, chain[0])

            for t in range(TT):
                dve.wait_ge(s_x[t], 16)
                dve.bn_stats(stats[:, t, :], res[:, t, :]).then_inc(s_v, 1)
            for t in range(TT):
                dve.wait_ge(s_v, t + 1)
                dve.bn_aggr(mv[:, t, :], stats[:, t, :]).then_inc(s_v, 1)
            chain[0] = 2 * TT
            dve.wait_ge(s_v, 2 * TT)
            dve.tensor_scalar(rstds[:, 0, :], mv[:, :, 1], EPS, None, ALU.add).then_inc(s_var, 1)
            dve.wait_ge(s_var, 1)
            dve.scalar_tensor_tensor(rstds[:, 1, :], rstds[:, 0, :], EPS, mv[:, :, 1], ALU.mult, ALU.add)\
               .then_inc(s_var, 1)
            dve.wait_ge(s_rst, 1)
            for t in range(TT):
                dve.tensor_scalar(v[:, t, :], res[:, t, :], mv[:, t, 0:1], rstds[:, 1, t:t + 1],
                                  ALU.subtract, ALU.mult).then_inc(s_nt, 1)
            dve.memset(ones[:, :], 1.0)
            dve.memset(ones_b[:, :], 1.0)
            dve.wait_ge(s_pp, 5)
            dve.tensor_copy(ident_b[:, :], ident[:, :])
            dve.memset(one_row, 1.0)
            dve.wait_ge(s_par, 16 * 7)
            for k in range(DK):
                dve.wait_ge(s_nhi, k + 1)
                dve.scalar_tensor_tensor(h_lo[:, k, :], turned_bank(k), nw[:, k:k + 1],
                                         h_hi[:, k, :].bitcast(F32), ALU.mult, ALU.subtract).then_inc(s_nlo, 1)

            def dt_abs():
                dve.wait_ge(s_dt, 1)
                step(dve.tensor_scalar(sp_v, ps_y[:, :], hcol[:, 0:1], None, ALU.add))
                dve.scalar_tensor_tensor(sp_a, sp_v, -1.0, sp_v, ALU.mult, ALU.max).then_inc(s_dtv, 1)

            def dt_w():
                dve.wait_ge(s_dta, 1)
                dve.tensor_scalar(sp_w, sp_e, 1.0, None, ALU.add).then_inc(s_dtv, 1)
                dve.wait_ge(s_dtv, 2)
                step(dve.tensor_scalar(sp_a, sp_w, -1.0, None, ALU.add))
                step(dve.tensor_tensor(sp_c, sp_e, sp_a, ALU.subtract))

            def dt_sum():
                dve.wait_ge(s_dta, 3)
                step(dve.tensor_tensor(sp_c, sp_c, sp_r, ALU.mult))
                step(dve.tensor_tensor(sp_c, sp_c, sp_l, ALU.add))
                dve.scalar_tensor_tensor(dt_h, sp_v, 0.0, sp_c, ALU.max, ALU.add).then_inc(s_dtv, 1)
                dve.wait_ge(s_dtv, 3)
                step(dve.tensor_scalar(r1, dt_h, hcol[:, 2:3], -1.0, ALU.mult, ALU.mult))

            def dt_keep():
                dve.wait_ge(s_dtt, 1)
                dve.tensor_scalar(dtT[:, :, :], ps_t[:, :].rearrange("p (c h) -> p c h", c=TT), 0.5, None,
                                  ALU.mult).then_inc(s_dtT, 1)
                dve.wait_ge(s_dtT, 1)
                dve.tensor_copy(dtg[:, :, :], dtT[:, :, 0:GH]).then_inc(s_cur, 1)
                dve.wait_ge(s_cur, 2)

            def running_sums():
                for b in range(BATCH):
                    seq = slice(b * SEQ, (b + 1) * SEQ)
                    step(dve.tensor_tensor_scan(acs[:, seq], one_row[:, seq], r1[:, seq], 0.0, ALU.mult, ALU.add))
                step(dve.tensor_copy(parts[:, 0, :], acs))

            def other_parts():
                step(dve.tensor_tensor(r1, acs, parts[:, 0, :], ALU.subtract))
                step(dve.tensor_copy(parts[:, 1, :], r1))
                step(dve.tensor_tensor(r2, r1, parts[:, 1, :], ALU.subtract))
                dve.tensor_copy(parts[:, 2, :], r2).then_inc(s_dtv, 1)

            def layernormed():
                for t in range(TT):
                    dve.tensor_scalar(u[:, t, :], res[:, t, :], mv[:, t, 0:1], rstds[:, 0, t:t + 1],
                                      ALU.subtract, ALU.mult).then_inc(s_u, 1)
                for k in range(2):
                    step(dve.reciprocal(qd[:, k:k + 1], qs[:, 2 * k:2 * k + 1]))
                    step(dve.tensor_scalar(qd[:, 2 + k:3 + k], qs[:, 2 * k + 1:2 * k + 2], -128.0, None, ALU.add))
                step(dve.tensor_tensor(qd[:, 4:5], qs[:, 0:1], qs[:, 2:3], ALU.mult))
                step(dve.scalar_tensor_tensor(qd[:, 5:6], qd[:, 2:3], -1.0, qd[:, 4:5], ALU.mult, ALU.mult))
                step(dve.tensor_scalar(qd[:, 6:7], qd[:, 2:3], float(D), None, ALU.mult))
                step(dve.scalar_tensor_tensor(qd[:, 7:8], qd[:, 3:4], -1.0, qd[:, 4:5], ALU.mult, ALU.mult))
                dve.wait_ge(s_perm, 32)
                step(dve.tensor_copy(perm_row[:, :], perm_row_i))
                step(dve.tensor_copy(perm_col[:, :], perm_col_i[:, :]))
                dve.tensor_scalar(skipgn[:, :, CT:2 * CT], gn_in[:, :].rearrange("p (g t) -> p g t", g=GROUPS),
                                  0.5, None, ALU.mult).then_inc(s_v, 1)
                chain[0] += 1
                dve.wait_ge(s_skip, 1)
                step(dve.tensor_scalar(skipgn[:, :, 0:CT], ps_df[:, 0, 0:GROUPS * CT]
                                       .rearrange("p (g t) -> p g t", g=GROUPS), 0.5, None, ALU.mult))

            def conv_dst(c):
                return bc[:, c, :] if c < 2 else hid[:, c - 2, :]

            def taps(n, c):
                i = c if c < 2 else 2 * c - 1
                dve.wait_ge(s_tap0, NCONV * n + c + 1)
                y = conv_dst(c).rearrange("p (b s) -> p b s", b=BATCH)
                src = bank_in(n, i).rearrange("p (b s) -> p b s", b=BATCH)
                for a in range(1, TAPS):
                    last = dve.scalar_tensor_tensor(y[:, :, a:], src[:, :, 0:SEQ - a],
                                                    curc[:, c * PAR + 3 - a:c * PAR + 4 - a], y[:, :, a:],
                                                    ALU.mult, ALU.add)
                    if a < TAPS - 1:
                        last.then_inc(s_vt, 1)
                        dve.wait_ge(s_vt, (TAPS - 2) * (NCONV * n + c) + a)
                last.then_inc(s_taps, 1)

            def conv_silu(n, c):
                dve.wait_ge(s_cth, NCONV * n + c + 1)
                dve.scalar_tensor_tensor(conv_dst(c), th[:, c % 2, :], 1.0, conv_dst(c), ALU.add, ALU.mult)\
                   .then_inc(s_conv, 1)

            def gated(n, t):
                dve.wait_ge(s_gth, CT * n + t + 1)
                if isinstance(n, int) and n == 0 and t == 6:
                    dve.wait_ge(s_acs, 16)
                dve.scalar_tensor_tensor(gate[:, t, :], gth[:, :], 1.0, bank_in(n, 2 + 2 * t), ALU.add, ALU.mult)\
                   .then_inc(s_gate, 1)

            def turned(n, t):
                dve.wait_ge(s_t, (CT + 2) * n + t + 1)
                dve.tensor_tensor(
                    hdt[:, :, t * P:(t + 1) * P].rearrange("p c (h q) -> p c h q", h=2),
                    ps_t[:, :].rearrange("p (c h q) -> p c h q", c=TT, h=2),
                    dtg[:, :, 2 * t:2 * t + 2].unsqueeze(3).broadcast_to([P, TT, 2, HD]),
                    ALU.mult).then_inc(s_tf, 1)

            def scores(n):
                dve.wait_ge(s_t, (CT + 2) * n + CT + 1)
                dve.tensor_scalar(gmA[:, :, :], ps_t[:, :].rearrange("p (b i) -> p b i", b=BATCH), 0.25, None,
                                  ALU.mult).then_inc(s_tf, 1)
                dve.wait_ge(s_t, (CT + 2) * n + CT + 2)
                dve.tensor_scalar(gmB[:, :, :], ps_t[:, 0:BATCH * P].rearrange("p (b i) -> p b i", b=BATCH), 0.25,
                                  None, ALU.mult).then_inc(s_tf, 1)

            def decays_a(m, t):
                dve.wait_ge(s_exp, 3 * CT * m + 3 * t + 2)
                if t == 0:
                    dve.wait_ge(s_tf, (CT + 2) * (m + 1))
                a = eA[:, t % 2, :, :]
                dve.tensor_tensor(a, a, gmA[:, :, :].rearrange("p b i -> p (b i)").unsqueeze(1)
                                  .broadcast_to([P, 2, TOK]), ALU.mult)

            def decays_b(m, t):
                dve.wait_ge(s_exp, 3 * CT * m + 3 * t + 3)
                b = eB[:, t % 2, :, :]
                dve.tensor_tensor(b, b, gmB[:, :, :].rearrange("p b i -> p (b i)").unsqueeze(1)
                                  .broadcast_to([P, 2, BATCH * P]), ALU.mult).then_inc(s_m, 1)

            def ssd_params(m):
                wait(dve, s_zhi, CT * m)
                dve.tensor_copy(curs[:, :], skipgn[:, bass.ds(m, 1), :].rearrange("p a c -> p (a c)"))\
                   .then_inc(s_curs, 1)

            def skip_and_gate(m, t):
                dve.wait_ge(s_y, CT * m + t + 1)
                wait(dve, s_sq, since(CT * m, t, 2))
                dve.scalar_tensor_tensor(z[:, t % 2, :], hid[:, t, :], curs[:, t:t + 1], ps_y[:, :],
                                         ALU.mult, ALU.add).then_inc(s_z1, 1)
                dve.wait_ge(s_z1, CT * m + t + 1)
                dve.tensor_tensor(z[:, t % 2, :], z[:, t % 2, :], gate[:, t, :], ALU.mult).then_inc(s_z, 1)

            def z_low(m, t):
                dve.wait_ge(s_zhi, CT * m + t + 1)
                wait(dve, s_ou, CT * m)
                dve.scalar_tensor_tensor(z_lo[:, t, :], z[:, t % 2, :], curs[:, CT + t:CT + t + 1],
                                         z_hi[:, t, :].bitcast(F32), ALU.mult, ALU.subtract).then_inc(s_zlo, 1)

            def mean_square(m):
                dve.wait_ge(s_ss, m + 1)
                dve.tensor_scalar(ssum[:, :], ps_y[:, 0:TT], 1.0 / (4 * GC), EPS, ALU.mult, ALU.add)\
                   .then_inc(s_ms, 1)

            def add_output(t):
                dve.scalar_tensor_tensor(res[:, t, :], out_bank(t), rgrp[:, t:t + 1], res[:, t, :],
                                         ALU.mult, ALU.add).then_inc(s_ofi if t >= 2 else s_of, 1)

            def iteration(n, do_in, do_ssd):
                m = n - 1
                if do_in:
                    wait(dve, s_tap0, NCONV * n)
                    dve.tensor_copy(curc[:, :], convp[:, bass.ds(n, 1), :].rearrange("p a c -> p (a c)"))\
                       .then_inc(s_cur, 1)
                    if do_ssd:
                        dve.tensor_copy(dtg[:, :, :], dtT[:, :, bass.ds(n * GH, GH)]).then_inc(s_cur, 1)
                if do_ssd:
                    ssd_params(m)
                if do_in:
                    dve.wait_ge(s_cur, 2 * n + (2 if do_ssd else 1))
                    taps(n, 0)
                    if not do_ssd:
                        dt_abs()
                    taps(n, 1)
                    conv_silu(n, 0)
                    conv_silu(n, 1)
                    if not do_ssd:
                        dt_w()
                if do_ssd:
                    dve.wait_ge(s_curs, m + 1)
                for t in range(CT):
                    if do_in and t:
                        taps(n, t + 1)
                    if do_ssd:
                        skip_and_gate(m, t)
                    if not do_ssd:
                        gated(n, t)
                    if do_in and t:
                        conv_silu(n, t + 1)
                    if do_ssd:
                        if t + 1 < CT:
                            decays_a(m, t + 1)
                        z_low(m, t)
                        if t + 1 < CT:
                            decays_b(m, t + 1)
                    if not do_ssd and t == 1:
                        dt_keep()
                    if do_in:
                        if do_ssd:
                            gated(n, t)
                        if t:
                            turned(n, t - 1)
                    if not do_ssd and t < 4:
                        (dt_sum, running_sums, other_parts, layernormed)[t]()
                if do_in:
                    taps(n, CT + 1)
                    conv_silu(n, CT + 1)
                if do_ssd:
                    mean_square(m)
                if do_in:
                    turned(n, CT - 1)
                    scores(n)
                    decays_a(n, 0)
                    decays_b(n, 0)
                if do_ssd:
                    dve.wait_ge(s_r, m + 1)
                    dve.wait_ge(s_oin, m + 1)
                    for t in (2, 3, 0, 1):
                        if t == 0:
                            dve.wait_ge(s_ou, CT * (m + 1))
                        add_output(t)

            iteration(0, True, False)
            iteration(1, True, True)
            with dve.Fori(2, loops) as n:
                iteration(n, True, True)

            def round_context(c):
                dve.wait_ge(s_cs, c + 1)
                step(dve.tensor_scalar(ctx_raw[c], ctx_raw[c], 0.0, 255.0, ALU.max, ALU.min))
                dve.tensor_scalar(q2[:, c, :], ctx_raw[c], MAGIC, -(MAGIC + 128.0), ALU.add, ALU.add)\
                   .then_inc(s_q2, 1)

            def one_hot(k):
                dve.tensor_scalar(take[:, k, :], perm_row[:, :], dcol[:, k:k + 1], None, ALU.is_equal)\
                   .then_inc(s_tp, 1)
                dve.tensor_scalar(put[:, k, :], iota_row[:, :], perm_col[:, k:k + 1], None, ALU.is_equal)\
                   .then_inc(s_tp, 1)

            ssd_params(last_m)
            dve.wait_ge(s_curs, GROUPS)
            dve.wait_ge(s_iota, 2)
            for t in range(CT):
                if t + 1 < CT:
                    decays_a(last_m, t + 1)
                skip_and_gate(last_m, t)
                if t + 1 < CT:
                    decays_b(last_m, t + 1)
                z_low(last_m, t)
                round_context(t)
                if t < DK:
                    one_hot(t)
            mean_square(last_m)

            def variance_of_all():
                dve.wait_ge(s_v, chain[0])
                for t in range(TT):
                    dve.bn_aggr(mv[:, t, :], stats[:, t, :]).then_inc(s_v, 1)
                chain[0] += TT
                dve.wait_ge(s_v, chain[0])
                dve.tensor_scalar(rstd[:, :], mv[:, :, 1], EPS, None, ALU.add).then_inc(s_ev, 1)

            def statistics(t):
                dve.bn_stats(stats[:, t, :], res[:, t, :]).then_inc(s_v, 1)
                chain[0] += 1

            dve.wait_ge(s_r, GROUPS)
            for pair, ready in (((2, 3), (s_oin, GROUPS)), ((0, 1), (s_ou, CT * GROUPS))):
                dve.wait_ge(*ready)
                for t in pair:
                    add_output(t)
                dve.wait_ge(s_ofi if 2 in pair else s_of, 2 * GROUPS)
                for t in pair:
                    statistics(t)
            variance_of_all()
            dve.wait_ge(s_ep, 1)
            step(dve.tensor_scalar(qa[:, :], rstd[:, :], qd[:, 0:1], None, ALU.mult))
            step(dve.tensor_tensor(qb[:, :], mv[:, :, 0], qa[:, :], ALU.mult))
            dve.tensor_scalar(qb[:, :], qb[:, :], -1.0, qs[:, 1:2], ALU.mult, ALU.add).then_inc(s_aff, 1)
            for t in range(TT):
                dve.wait_ge(s_x1, t + 1)
                step(dve.tensor_scalar(e1[:, t, :], e1[:, t, :], 0.0, 255.0, ALU.max, ALU.min))
                dve.tensor_scalar(q1[:, t, :], e1[:, t, :], MAGIC, -(MAGIC + 128.0), ALU.add, ALU.add)\
                   .then_inc(s_q1, 1)
            dve.wait_ge(s_cq, 1)
            for t in range(2):
                step(dve.scalar_tensor_tensor(res[:, t, :], ps_df[:, t // 2, :], qd[:, 5:6], res[:, t, :],
                                              ALU.mult, ALU.add))
            dve.wait_ge(s_q1t, 1)
            dve.tensor_copy(q1T[:, 2:4, :].rearrange("p a n -> p (a n)"), ps_t[:, :].bitcast(BF16)).then_inc(s_q1v, 1)
            for t in range(2, TT):
                step(dve.scalar_tensor_tensor(res[:, t, :], ps_df[:, t // 2, :], qd[:, 5:6], res[:, t, :],
                                              ALU.mult, ALU.add))
            dve.wait_ge(s_rs, 1)
            dve.tensor_scalar(rowq[:, :], ps_y[:, 0:TT], qd[:, 6:7], qd[:, 7:8], ALU.subtract, ALU.mult)\
               .then_inc(s_rq, 1)
            for t in range(TT):
                dve.wait_ge(s_px, t + 1)
                step(dve.tensor_tensor(res[:, t, :], res[:, t, :], e1[:, t, :], ALU.add))
                statistics(t)

            variance_of_all()
            dve.wait_ge(s_ep, 2)
            for t in range(TT):
                dve.tensor_scalar(e1[:, t, :], res[:, t, :], mv[:, t, 0:1], rstd[:, t:t + 1],
                                  ALU.subtract, ALU.mult).then_inc(s_f, 1)
            for k in range(DK):
                dve.wait_ge(s_fhi, k + 1)
                dve.tensor_tensor(f_lo[:, k, :], feature_bank(k), f_hi[:, k, :].bitcast(F32), ALU.subtract)\
                   .then_inc(s_flo, 1)
            for k in range(DK):
                dve.wait_ge(s_phi, k + 1)
                dve.tensor_tensor(p_lo[:, k, :], permuted_bank(k), p_hi[:, k, :].bitcast(F32), ALU.subtract)\
                   .then_inc(s_plo, 1)
            for k in range(DK):
                dve.wait_ge(s_dn, k + 1)
                src = (ps_t if k % 2 else ps_y)[:, :]
                step(dve.tensor_copy(f_hi[:, k, :], src))
                dve.tensor_tensor(f_lo[:, k, :], src, f_hi[:, k, :].bitcast(F32), ALU.subtract).then_inc(s_dlo, 1)
            for t in range(TT):
                dve.wait_ge(s_fin, t + 1)
                dve.tensor_tensor(res[:, t, :], res[:, t, :], final_bank(t), ALU.add).then_inc(s_store, 1)

        @block.tensor
        def _(pe):
            def split3(dst, lhs, rhs, first, last):
                (lh, ll), (rh, rl) = lhs, rhs
                pe.matmul(dst, lh, rh, start=first, stop=False)
                pe.matmul(dst, lh, rl, start=False, stop=False)
                return pe.matmul(dst, ll, rh, start=False, stop=last)

            pe.wait_ge(s_pp, 5)
            for t in range(TT):
                pe.wait_ge(s_nt, t + 1)
                for k in range(DK):
                    last = pe.transpose(turned_bank(k)[:, t * P:(t + 1) * P], v[:, t, k * P:(k + 1) * P],
                                        ident[:, :])
                last.then_inc(s_nT, 1)

            def dt_product():
                pe.wait_ge(s_dtw, 1)
                for k in range(DK):
                    cols = slice(k * P, (k + 1) * P)
                    last = split3(ps_y[:, :], (wo_hi[:, dt_slot, cols], wo_lo[:, dt_slot, cols]),
                                  (h_hi[:, k, :], h_lo[:, k, :]), k == 0, k == DK - 1)
                last.then_inc(s_dt, 1)
                pe.wait_ge(s_par, 16 * 7)
                pe.matmul(ps_df[:, 0, 0:GROUPS * CT], sel[:, :], d2[:, :], start=True, stop=True).then_inc(s_skip, 1)

            def dt_turn():
                pe.wait_ge(s_dtv, 3)
                for t in range(TT):
                    last = pe.transpose(ps_t[:, t * P:(t + 1) * P], dt_h[:, t * P:(t + 1) * P], ident[:, :])
                last.then_inc(s_dtt, 1)

            def project(n, i, do_ssd):
                pe.wait_ge(s_lo, NIN * n + i + 1)
                ring = 4 if isinstance(n, int) and n == 0 else 2
                if i < ring:
                    if i % 2:
                        wait(pe, s_taps, NCONV * n)
                    else:
                        wait(pe, s_gate, CT * n)
                elif i % 2 or i == ring:
                    wait(pe, s_taps, NCONV * n + (i - ring + 3) // 2)
                else:
                    wait(pe, s_gate, CT * n + (i - ring) // 2)
                if do_ssd and i == 0:
                    wait(pe, s_ofi, 2 * (n - 1))
                for k in range(DK):
                    if not do_ssd and i == 0:
                        pe.wait_ge(s_nlo, k + 1)
                    cols = slice(k * P, (k + 1) * P)
                    last = split3(bank_in(n, i), (w_hi[:, i % W_RING, cols], w_lo[:, i % W_RING, cols]),
                                  (h_hi[:, k, :], h_lo[:, k, :]), k == 0, k == DK - 1)
                last.then_inc(s_in, 1)

            def turn(n, t):
                pe.wait_ge(s_conv, NCONV * n + t + 3)
                if isinstance(n, int) and n == 0 and t == 0:
                    pe.wait_ge(s_dtT, 1)
                wait(pe, s_tf, (CT + 2) * n + t)
                for c in range(TT):
                    last = pe.transpose(ps_t[:, c * P:(c + 1) * P], hid[:, t, c * P:(c + 1) * P], ident[:, :])
                last.then_inc(s_t, 1)

            def scores_a(n):
                pe.wait_ge(s_tf, (CT + 2) * n + CT)
                for b in range(BATCH):
                    at = b * SEQ
                    last = pe.matmul(ps_t[:, at:at + SEQ], bc[:, 0, at:at + P], bc[:, 1, at:at + SEQ],
                                     start=True, stop=True)
                last.then_inc(s_t, 1)

            def scores_b(n):
                pe.wait_ge(s_tf, (CT + 2) * n + CT + 1)
                for b in range(BATCH):
                    at = b * SEQ + P
                    last = pe.matmul(ps_t[:, b * P:(b + 1) * P], bc[:, 0, at:at + P], bc[:, 1, at:at + P],
                                     start=True, stop=True)
                last.then_inc(s_t, 1)

            def diffs(m, t, banks):
                if t == 0:
                    pe.wait_ge(s_rows, 16 * 8 * (m + 1))
                for k in banks:
                    wait(pe, s_exp, since(3 * CT * m, 3 * t + k, 2))
                    bank = ps_df[:, (3 * t + k) % 2, :]
                    first = True
                    for hh in ((k,) if k < 2 else (0, 1)):
                        h = 2 * t + hh
                        q = slice(32 * (h // 4), 32 * (h // 4) + 6)
                        for b in range(BATCH):
                            at = b * SEQ if k < 2 else b * SEQ + P
                            width = SEQ if k < 2 else P
                            to = b * SEQ if k < 2 else (hh * BATCH + b) * P
                            pe.matmul(bank[:, to:to + width], sta[q, h % 4, at:at + P],
                                      mov[q, h % 4, at:at + width], start=first, stop=False, skip_group_check=True)
                            first = False
                    blocks, count = (bank.rearrange("p (b i) -> p b i", b=BATCH)[:, :, 0:P], BATCH) if k < 2 else \
                        (bank.rearrange("p (b i) -> p b i", b=2 * BATCH), 2 * BATCH)
                    last = pe.matmul(blocks, ident_b[:, :], cut[:, 0:count, :], start=False, stop=True,
                                     skip_group_check=True)
                    last.then_inc(s_df, 1)

            def outputs(m, t):
                pe.wait_ge(s_m, CT * m + t + 1)
                if t == 0:
                    wait(pe, s_ms, m)
                wait(pe, s_z1, CT * m + t)
                for b in range(BATCH):
                    at = b * SEQ
                    for half_seq in range(2):
                        for hh in range(2):
                            rows_ = slice(HD * hh, HD * (hh + 1))
                            w = hdt[:, 2 * b + half_seq, t * P + HD * hh:t * P + HD * (hh + 1)]
                            if half_seq == 0:
                                last = pe.matmul(ps_y[rows_, at:at + SEQ], w, eA[:, t % 2, hh, at:at + SEQ],
                                                 start=True, stop=False, skip_group_check=True)
                            else:
                                last = pe.matmul(ps_y[rows_, at + P:at + SEQ], w,
                                                 eB[:, t % 2, hh, b * P:(b + 1) * P],
                                                 start=False, stop=True, skip_group_check=True)
                last.then_inc(s_y, 1)

            def token_sums(m):
                pe.wait_ge(s_sqs, (CT - 1) * (m + 1))
                pe.wait_ge(s_z1, CT * (m + 1))
                for t in range(TT):
                    last = pe.matmul(ps_y[:, t:t + 1], sqsum[:, t * P:(t + 1) * P], ones[:, :],
                                     start=True, stop=True)
                last.then_inc(s_ss, 1)

            def out_pair(m, j, do_in, between=None):
                if j == 0:
                    wait(pe, s_of, 2 * m)
                pe.wait_ge(s_zlo, CT * m + 2 * j + 2)
                pe.wait_ge(s_olo, CT * m + 2 * j + 2)
                last_pair = j == CT // 2 - 1
                for pair in ((2, 3), (0, 1)) if last_pair else ((0, 1), (2, 3)):
                    if between and pair == (0, 1):
                        between(m)
                    if j == 0 and pair == (2, 3) and do_in:
                        pe.wait_ge(s_gate, CT * (m + 2))
                        pe.wait_ge(s_taps, NCONV * (m + 2))
                    for k in (2 * j, 2 * j + 1):
                        for t in pair:
                            dst = out_bank(t)
                            cols = slice(t * P, (t + 1) * P)
                            last = split3(dst, (z_hi[:, k, cols], z_lo[:, k, cols]),
                                          (wo_hi[:, k % WO_RING, :], wo_lo[:, k % WO_RING, :]), k == 0, k == CT - 1)
                        if last_pair and pair == (2, 3):
                            if k == CT - 1:
                                last.then_inc(s_oin, 1)
                        elif last_pair or pair == (2, 3):
                            last.then_inc(s_ou, 1)

            def iteration(n, do_in, do_ssd):
                m = n - 1
                if do_in and not (isinstance(n, int) and n == 1):
                    project(n, 0, do_ssd)
                    if not do_ssd:
                        dt_product()
                    project(n, 1, do_ssd)
                for t in range(CT):
                    if do_ssd:
                        outputs(m, t)
                        if t + 1 < CT:
                            diffs(m, t + 1, (0, 1))
                    if do_in:
                        project(n, 2 + 2 * t, do_ssd)
                    if do_ssd and t + 1 < CT:
                        diffs(m, t + 1, (2,))
                    if do_in:
                        project(n, 3 + 2 * t, do_ssd)
                        if not do_ssd and t == 1:
                            dt_turn()
                        if t:
                            turn(n, t - 1)
                if do_ssd:
                    out_pair(m, 0, do_in)
                    token_sums(m)
                if not do_ssd:
                    project(n + 1, 0, True)
                    project(n + 1, 1, True)
                if do_in:
                    turn(n, CT - 1)
                if do_ssd:
                    out_pair(m, 1, do_in)
                if do_in:
                    scores_a(n)
                    diffs(n, 0, (0, 1))
                if do_ssd:
                    out_pair(m, 2, do_in)
                if do_in:
                    scores_b(n)
                    diffs(n, 0, (2,))
                if do_ssd:
                    out_pair(m, 3, do_in)

            iteration(0, True, False)
            iteration(1, True, True)
            with pe.Fori(2, loops) as n:
                iteration(n, True, True)

            for t in range(CT):
                if t + 1 < CT:
                    diffs(last_m, t + 1, (0, 1))
                outputs(last_m, t)
                if t + 1 < CT:
                    diffs(last_m, t + 1, (2,))
                if t and t % 2 == 0:
                    out_pair(last_m, t // 2 - 1, False)
            out_pair(last_m, CT // 2 - 1, False, between=token_sums)

            pe.wait_ge(s_q2, BATCH * DK)
            pe.wait_ge(s_exp, 3 * CT * GROUPS)
            for b in range(BATCH):
                for k in range(DK):
                    last = pe.matmul(ps_df[:, b, :], ones_b[:, :], q2[:, b * DK + k, :],
                                     start=(k == 0), stop=(k == DK - 1))
            last.then_inc(s_cq, 1)
            pe.wait_ge(s_ms, GROUPS)
            pe.wait_ge(s_tf, (CT + 2) * GROUPS)
            for t in range(TT):
                pe.wait_ge(s_q1, t + 1)
                for k in range(DK):
                    bank = (ps_t if k >= 2 else ps_y)[:, :].bitcast(BF16)
                    at = (k % 2) * TOK + t * P
                    last = pe.transpose(bank[:, at:at + P], q1[:, t, k * P:(k + 1) * P], ident_b[:, :])
            last.then_inc(s_q1t, 1)

            def product(ks):
                for k in ks:
                    for t in range(TT):
                        last = pe.matmul(out_bank(t), q1T[:, k, t * P:(t + 1) * P], q2[:, (t // 2) * DK + k, :],
                                         start=(k == 0), stop=(k == DK - 1), skip_group_check=True)
                        if k == DK - 1:
                            last.then_inc(s_pr, 1)

            pe.wait_ge(s_q1a, 1)
            pe.wait_ge(s_of, 2 * GROUPS)
            pe.wait_ge(s_ofi, 2 * GROUPS)
            product((0, 1))
            pe.wait_ge(s_q1v, 1)
            for t in range(TT):
                for k in range(DK):
                    last = pe.matmul(ps_y[:, t:t + 1], q1T[:, k, t * P:(t + 1) * P], ones_b[:, 0:1],
                                     start=(k == 0), stop=(k == DK - 1))
            last.then_inc(s_rs, 1)
            product((2, 3))

            for t in range(TT):
                pe.wait_ge(s_f, t + 1)
                for k in range(DK):
                    last = pe.transpose(feature_bank(k)[:, t * P:(t + 1) * P], e1[:, t, k * P:(k + 1) * P],
                                        ident[:, :])
            last.then_inc(s_ft, 1)
            pe.wait_ge(s_tp, 2 * DK)
            for d in range(DK):
                pe.wait_ge(s_flo, d + 1)
                for k in range(DK):
                    for part in (f_hi, f_lo):
                        last = pe.matmul(permuted_bank(k), take[:, d, k * P:(k + 1) * P], part[:, d, :],
                                         start=(d == 0 and part is f_hi), stop=(d == DK - 1 and part is f_lo),
                                         skip_group_check=True)
                    if d == DK - 1:
                        last.then_inc(s_p, 1)

            def up_product(h):
                if h < 2:
                    pe.wait_ge(s_plo, h + 1)
                else:
                    pe.wait_ge(s_gl, h - 1)
                if h % 4 == 0:
                    pe.wait_ge(s_plo, h // 4 + 1)
                r = slice(FD * (h % 4), FD * (h % 4) + FD)
                split3(ps_in[:, h % 2, :], (up_hi[r, h // 4, :], up_lo[r, h // 4, :]),
                       (p_hi[r, h // 4, :], p_lo[r, h // 4, :]), True, True).then_inc(s_up, 1)

            def down_product(k):
                pe.wait_ge(s_gl, 4 * k + 4)
                if k >= 2:
                    pe.wait_ge(s_dlo, k - 1)
                for h in range(4 * k, 4 * k + 4):
                    last = pe.matmul((ps_t if k % 2 else ps_y)[FD * (h % 4):FD * (h % 4) + FD, :], down_sb[:, h, :],
                                     gel[:, h % CT, :], start=True, stop=True, skip_group_check=True)
                last.then_inc(s_dn, 1)

            def put_back(k):
                pe.wait_ge(s_dlo, k + 1)
                for t in range(TT):
                    for part in (f_hi, f_lo):
                        last = pe.matmul(final_bank(t), part[:, k, t * P:(t + 1) * P], put[:, k, :],
                                         start=(k == 0 and part is f_hi), stop=(k == DK - 1 and part is f_lo),
                                         skip_group_check=True)
                    if k == DK - 1:
                        last.then_inc(s_fin, 1)

            pe.wait_ge(s_upl, 1)
            for h in range(FH):
                up_product(h)
                if h >= 5 and h % 4 == 1:
                    down_product((h - 5) // 4)
                if h >= 7 and h % 4 == 3:
                    put_back((h - 7) // 4)
            down_product(3)
            put_back(3)


_INS = ["x", "ctx", "w_in", "w_dt", "w_out", "conv_par", "norm_w", "dt_bias", "a_log", "d_skip", "gnorm",
        "quant", "up", "down", "perm", "perm_by_part"]


def lay_out(np, i):
    w = np.asarray(i["L0_attn_in_proj_w"])
    bcn = GROUPS * P

    def tiles(rows):
        r = rows.reshape(-1, P, DK, P)
        return r.transpose(0, 3, 2, 1)

    gate_t = tiles(w[:INNER]).reshape(GROUPS, CT, P, DK, P)
    hid_t = tiles(w[INNER:2 * INNER]).reshape(GROUPS, CT, P, DK, P)
    b_t = tiles(w[2 * INNER:2 * INNER + bcn]).reshape(GROUPS, 1, P, DK, P)
    c_t = tiles(w[2 * INNER + bcn:2 * INNER + 2 * bcn]).reshape(GROUPS, 1, P, DK, P)
    by_turns = np.stack([gate_t, hid_t], axis=2).reshape(GROUPS, 2 * CT, P, DK, P)
    w_in = np.concatenate([b_t, c_t, by_turns], axis=1).reshape(GROUPS, NIN, P, DK * P)
    w_dt = tiles(w[2 * INNER + 2 * bcn:]).reshape(P, DK * P)
    w_out = np.asarray(i["L0_attn_out_proj_w"]).T.reshape(GROUPS, CT, P, D)

    par = np.concatenate([np.asarray(i["L0_attn_conv_w"]), np.asarray(i["L0_attn_conv_b"])[:, None]], axis=1)
    hp = par[:INNER].reshape(GROUPS, CT, P, PAR)
    bp = par[INNER:INNER + bcn].reshape(GROUPS, 1, P, PAR)
    cp = par[INNER + bcn:].reshape(GROUPS, 1, P, PAR)
    conv_par = np.concatenate([bp, cp, hp], axis=1).transpose(2, 0, 1, 3).reshape(P, GROUPS, NCONV * PAR)
    quant = np.concatenate([np.asarray(i["L0_xattn_" + n]) for n in ("x1_scale", "x1_zp", "x2_scale", "x2_zp")])
    return {
        "x": np.asarray(i["x"]).reshape(TOK, D),
        "ctx": np.asarray(i["ctx_4096"]),
        "w_in": w_in, "w_dt": w_dt, "w_out": w_out, "conv_par": conv_par,
        "norm_w": np.asarray(i["L0_attn_norm_w"]).reshape(DK, P).T,
        "dt_bias": np.asarray(i["L0_attn_dt_bias"]).reshape(HEADS, 1),
        "a_log": np.asarray(i["L0_attn_A_log"]).reshape(HEADS, 1),
        "d_skip": np.asarray(i["L0_attn_Dp"]).reshape(GROUPS * CT, 2).T,
        "gnorm": np.asarray(i["L0_attn_gnorm_w"]).reshape(GROUPS * CT, P).T,
        "quant": quant,
        "up": np.asarray(i["L0_ffn_up"]).reshape(DK, P, FM).transpose(1, 0, 2),
        "down": np.asarray(i["L0_ffn_down"]).transpose(1, 0, 2),
        "perm": np.asarray(i["L0_ffn_perm"]),
        "perm_by_part": np.asarray(i["L0_ffn_perm"]).reshape(DK, P).T,
    }


def kernel(**inputs):
    import numpy as np
    import concourse.bacc as bacc
    from concourse.bass_utils import run_bass_kernel_spmd

    nc = bacc.Bacc("TRN2", target_bir_lowering=False, num_devices=1)
    laid = lay_out(np, inputs)
    arrays, args = {}, []
    for name in _INS:
        a = np.ascontiguousarray(laid[name])
        arrays[f"in_{name}"] = a
        args.append(nc.dram_tensor(f"in_{name}", a.shape, mybir.dt.from_np(a.dtype), kind="ExternalInput").ap())
    args.append(nc.dram_tensor("out_x", (TOK, D), F32, kind="ExternalOutput").ap())
    decoder_layer(nc, *args)
    r = run_bass_kernel_spmd(nc, [arrays], core_ids=[0])
    return r.results[0]["out_x"].reshape(BATCH, SEQ, D)
```

```python
from contextlib import ExitStack

import concourse.bass as bass
from concourse import mybir

F32 = mybir.dt.float32
F32R = mybir.dt.float32r
BF16 = mybir.dt.bfloat16
I32 = mybir.dt.int32
ALU = mybir.AluOpType
ACT = mybir.ActivationFunctionType
AX_X = mybir.AxisListType.X

P = 128
BATCH, SEQ, D = 2, 256, 512
TOK = BATCH * SEQ
TT = TOK // P
DK = D // P
GROUPS, HEADS, HD = 8, 128, 64
GH = HEADS // GROUPS
INNER = HEADS * HD
GC = INNER // GROUPS
CT = GC // P
NIN = 2 + 2 * CT
NCONV = 2 + CT
TAPS = 4
PAR = TAPS + 1
EPS = 1e-5
W_RING, RAW_RING = 6, 3
WO_RING, RAWO_RING = 4, 2
CTX = 512
FH, FD, FM = 16, 32, 128
MAGIC = 1.5 * 2.0 ** 23


def since(base, i, ring):
    return base + max(i + 1 - ring, 0)


def wait(eng, sem, value):
    if isinstance(value, int) and value <= 0:
        return
    eng.wait_ge(sem, value)


def decoder_layer(nc, x, ctx_in, w_in, w_dt, w_out, conv_par, norm_w, dt_bias, a_log, d_skip,
                  gnorm, quant, up, down, perm, perm_by_part, out):
    acs_dram = nc.dram_tensor("acs_parts", [3, HEADS, TOK], BF16, kind="Internal").ap()

    with ExitStack() as ctx:
        def sb(name, shape, dt=F32):
            return ctx.enter_context(nc.sbuf_tensor(name, shape, dt))

        def psum(name, shape):
            return ctx.enter_context(nc.psum_tensor(name, shape, F32))

        def sem(name):
            return ctx.enter_context(nc.semaphore(name))

        res = sb("res", [P, TT, D])
        h_hi = sb("h_hi", [P, DK, TOK], F32R)
        h_lo = sb("h_lo", [P, DK, TOK], F32R)
        raw = sb("raw", [P, RAW_RING, DK * P])
        w_hi = sb("w_hi", [P, W_RING, DK * P], F32R)
        w_lo = sb("w_lo", [P, W_RING, DK * P], F32R)
        rawo = sb("rawo", [P, RAWO_RING, D])
        wo_hi = sb("wo_hi", [P, WO_RING, D], F32R)
        wo_lo = sb("wo_lo", [P, WO_RING, D], F32R)
        hid = sb("hid", [P, CT, TOK])
        gate = sb("gate", [P, CT, TOK])
        bc = sb("bc", [P, 2, TOK])
        th = sb("th", [P, 2, TOK])
        gth = sb("gth", [P, TOK])
        hdt = sb("hdt", [P, TT, GC])
        gmA = sb("gmA", [P, BATCH, SEQ])
        gmB = sb("gmB", [P, BATCH, P])
        eA = sb("eA", [P, 2, 2, TOK])
        eB = sb("eB", [P, 2, 2, BATCH * P])
        z = sb("z", [P, 2, TOK])
        z_hi = sb("z_hi", [P, CT, TOK], F32R)
        z_lo = sb("z_lo", [P, CT, TOK], F32R)
        sq = sb("sq", [P, TOK])
        sqsum = sb("sqsum", [P, TOK])
        mov = sb("mov", [P, 4, TOK], BF16)
        sta = sb("sta", [P, 4, TOK], BF16)
        keep = sb("keep", [P, P])
        ident_b = sb("ident_b", [P, P], BF16)
        ident = sb("ident", [P, P])
        ones = sb("ones", [P, 1])
        convp = sb("convp", [P, GROUPS, NCONV * PAR])
        curc = sb("curc", [P, NCONV * PAR])
        skipgn = sb("skipgn", [P, GROUPS, 2 * CT])
        curs = sb("curs", [P, 2 * CT])
        dtT = sb("dtT", [P, TT, HEADS])
        dtg = sb("dtg", [P, TT, GH])
        nw = sb("nw", [P, DK])
        gn_in = sb("gn_in", [P, GROUPS * CT])
        d2 = sb("d2", [2, GROUPS * CT])
        sel = sb("sel", [2, P])
        hcol = sb("hcol", [P, 3])
        half = sb("half", [P, 2, TT])
        stats = sb("stats", [P, TT, 6])
        mv = sb("mv", [P, TT, 2])
        rstd = sb("rstd", [P, TT])
        rstds = sb("rstds", [P, 2, TT])
        ssum = sb("ssum", [P, TT])
        rgrp = sb("rgrp", [P, TT])
        qs = sb("qs", [P, 4])
        qd = sb("qd", [P, 8])
        qa = sb("qa", [P, TT])
        qb = sb("qb", [P, TT])
        rowq = sb("rowq", [P, TT])
        ones_b = sb("ones_b", [P, P], BF16)
        perm_row = sb("perm_row", [P, D])
        iota_row = sb("iota_row", [P, D])
        perm_col_i = sb("perm_col_i", [P, DK], I32)
        perm_col = sb("perm_col", [P, DK])
        dcol = sb("dcol", [P, DK])

        ps_in = psum("ps_in", [P, 2, 512])
        ps_df = psum("ps_df", [P, 2, 512])
        ps_y = psum("ps_y", [P, 512])
        ps_t = psum("ps_t", [P, 512])
        ps_o = psum("ps_o", [P, 2, 512])

        s_x = [sem(f"x_loaded{t}") for t in range(TT)]
        s_par = sem("params_loaded")
        s_wdt = sem("wdt_loaded")
        s_raw = [sem(f"raw_loaded{i}") for i in range(RAW_RING)]
        s_rawo = [sem(f"rawo_loaded{i}") for i in range(RAWO_RING)]
        s_hi = sem("w_hi_done")
        s_lo = sem("w_lo_done")
        s_ohi = sem("wo_hi_done")
        s_olo = sem("wo_lo_done")
        s_in = sem("in_ready")
        s_tap0 = sem("tap0_done")
        s_taps = sem("taps_done")
        s_cth = sem("conv_tanh_done")
        s_conv = sem("conv_done")
        s_gth = sem("gate_tanh_done")
        s_gate = sem("gate_done")
        s_t = sem("turn_ready")
        s_tf = sem("turn_free")
        s_rows = sem("rows_loaded")
        s_df = sem("diff_ready")
        s_cl = sem("diff_clamped")
        s_exp = sem("exp_done")
        s_ma = sem("decay_a_ready")
        s_mb = sem("decay_b_ready")
        s_y = sem("y_ready")
        s_z1 = sem("y_free")
        s_z = sem("z_done")
        s_zhi = sem("z_hi_done")
        s_zlo = sem("z_lo_done")
        s_sq = sem("square_done")
        s_sqs = sem("square_sum_done")
        s_ss = sem("token_sum_ready")
        s_ms = sem("mean_square_done")
        s_r = sem("rms_done")
        s_ou = sem("wo_used")
        s_oin = sem("out_in_ready")
        s_ofi = sem("out_added_in")
        s_of = sem("out_added")
        s_cur = sem("in_params")
        s_curs = sem("ssd_params")
        s_v = sem("vector_step")
        s_var = sem("variances")
        s_rst = sem("input_rstds")
        s_nt = sem("normed_tile")
        s_nT = sem("normed_turned")
        s_nhi = sem("normed_hi")
        s_nlo = sem("normed_lo")
        s_u = sem("layernormed")
        s_res = sem("residual_started")
        s_dt = sem("dt_projected")
        s_dtv = sem("dt_vector")
        s_dta = sem("dt_scalar")
        s_dtt = sem("dt_turned")
        s_dtT = sem("dt_kept")
        s_skip = sem("skip_spread")
        s_rows1 = sem("rows_of_ones")
        s_vt = sem("vector_tap")
        s_pa = sem("prologue_scalar")
        s_pp = sem("prologue_gpsimd")
        s_acs = sem("acs_stored")
        s_dtw = sem("dt_weights_split")
        s_perm = sem("perm_loaded")
        s_iota = sem("numbers_ready")
        s_ctx = [sem(f"context_loaded{c}") for c in range(BATCH * DK)]
        s_cs = sem("context_scaled")
        s_q2 = sem("context_quantised")
        s_ffw = sem("ffn_loaded")
        s_tp = sem("take_put_ready")
        s_upz = sem("up_zeroed")
        s_uph = sem("up_hi_done")
        s_upl = sem("up_lo_done")
        s_cq = sem("q2_sums_ready")
        s_ev = sem("variance_ready")
        s_ep = sem("rstd_ready")
        s_aff = sem("quant_scales")
        s_x1 = sem("norm_scaled")
        s_q1 = sem("norm_quantised")
        s_q1t = sem("q1_turned")
        s_q1a = sem("q1T_kept_scalar")
        s_q1v = sem("q1T_kept_vector")
        s_rs = sem("q1_sums_ready")
        s_rq = sem("row_terms_ready")
        s_pr = sem("product_ready")
        s_px = sem("row_terms_added")
        s_f = sem("features")
        s_ft = sem("features_turned")
        s_fhi = sem("features_hi")
        s_flo = sem("features_lo")
        s_p = sem("features_permuted")
        s_phi = sem("permuted_hi")
        s_plo = sem("permuted_lo")
        s_up = sem("up_ready")
        s_gl = sem("gelu_done")
        s_dn = sem("down_ready")
        s_dlo = sem("down_split")
        s_fin = sem("ffn_ready")
        s_store = sem("out_tile_ready")
        s_out = sem("out_stored")

        v = hdt[:, 2:4, :].rearrange("p a (b n) -> p (a b) n", b=2)
        u = eA[:, :, :, :].rearrange("p a b n -> p (a b) n")
        sp_e, sp_w, dt_h, acs = (hid[:, i, :] for i in range(4, 8))
        sp_v, sp_a = gate[:, 4, :], gate[:, 5, :]
        sp_c, sp_l = (eB[:, i, :, :].rearrange("p a n -> p (a n)") for i in range(2))
        r1, r2, one_row, sp_r = z[:, 0, :], z[:, 1, :], sq[:, :], sqsum[:, :]
        parts = gate[:, 6:8, :].bitcast(BF16).rearrange("p a n -> p (a n)")[:, 0:3 * TOK].rearrange(
            "p (r n) -> p r n", r=3)
        wdt_raw = rawo[:, 0, :]
        dt_slot = WO_RING - 1
        ctx_raw = [raw[:, 0, :], raw[:, 1, :], raw[:, 2, :], th[:, 0, :], th[:, 1, :], gth[:, :], bc[:, 0, :],
                   bc[:, 1, :]]
        q2 = hid[:, 0:4, :].rearrange("p a n -> p (a n)").bitcast(BF16).rearrange("p (c n) -> p c n", c=BATCH * DK)
        e1 = hdt[:, 2:4, :].rearrange("p a (b n) -> p (a b) n", b=2)
        q1 = eA[:, 0, :, :].rearrange("p a n -> p (a n)").bitcast(BF16).rearrange("p (t d) -> p t d", t=TT)
        q1T = eA[:, 1, :, :].rearrange("p a n -> p (a n)").bitcast(BF16).rearrange("p (k n) -> p k n", k=DK)
        perm_row_i = rawo[:, 1, :].bitcast(I32)
        take = w_hi[:, 0:DK, :]
        put = w_lo[:, 0:DK, :]
        up_raw = rawo[:, 0, :].rearrange("p (a m) -> p a m", a=DK)
        up_hi, up_lo = (a[:, :, :].rearrange("p k (j m) -> p k j m", j=4) for a in (wo_hi, wo_lo))
        down_sb = rawo[:, 1, :].rearrange("p (h d) -> p h d", h=FH)
        f_hi, f_lo = h_hi, h_lo
        p_hi, p_lo = z_hi, z_lo
        free_hdt = hdt[:, 0:2, :].rearrange("p a (b n) -> p (a b) n", b=2)
        gel = [gate[:, i, :] for i in range(8)] + [hid[:, i, :] for i in range(4, 8)] + \
            [free_hdt[:, i, :] for i in range(4)]

        def out_bank(t):
            return ps_in[:, t - 2, :] if t >= 2 else ps_o[:, t, :]

        def feature_bank(k):
            return (ps_df[:, 0, :], ps_df[:, 1, :], ps_y[:, :], ps_t[:, :])[k]

        def permuted_bank(k):
            return (ps_in if k < 2 else ps_o)[:, k % 2, :]

        def df_bank(m, t, k):
            if isinstance(m, int) and m == last_m and t:
                return (ps_df[:, 0, :], ps_df[:, 1, :], ps_t[:, :])[k]
            return ps_df[:, (3 * t + k) % 2, :]

        def wide_bank(i):
            return permuted_bank(i % 4)

        def turned_bank(k):
            return (ps_df if k < 2 else ps_o)[:, k % 2, :]

        def first_tiles(n):
            if isinstance(n, int) and n < 2:
                return range(W_RING) if n == 0 else range(0)
            return range(4)

        def step_tiles(n, t):
            if isinstance(n, int) and n == 0:
                return range(W_RING + 2 * t, W_RING + 2 * t + 2)
            return range(4 + 2 * t, min(4 + 2 * t + 2, NIN))

        def out_tile_at(t):
            return {0: 2, 1: 3, 3: 4, 4: 5, 5: 6, 6: 7}.get(t)

        def diagonal(bank, k):
            return bank.rearrange("p (b i) -> p b i", b=BATCH)[:, :, 0:P] if k < 2 else bank

        def bank_in(n, i):
            if isinstance(n, int) and n == 0 and i % 4 >= 2:
                return ps_o[:, i % 2, :]
            return ps_in[:, i % 2, :]

        loops = GROUPS
        last_m = GROUPS - 1

        block = ctx.enter_context(nc.Block())

        @block.sync
        def _(sp):
            for t in range(TT):
                sp.dma_start(res[:, t, :], x[t * P:(t + 1) * P, :]).then_inc(s_x[t], 16)
            loads = [(nw[:, :], norm_w), (hcol[:, 0:1], dt_bias), (hcol[:, 1:2], a_log), (d2[:, :], d_skip),
                     (gn_in[:, :], gnorm), (convp[:, :, :], conv_par),
                     (qs[:, :], quant.partition_broadcast(P))]
            for dst, src in loads:
                sp.dma_start(dst, src).then_inc(s_par, 16)
            sp.dma_start(wdt_raw, w_dt).then_inc(s_wdt, 16)
            sp.dma_start(perm_row_i, perm.partition_broadcast(P)).then_inc(s_perm, 16)
            sp.dma_start(perm_col_i[:, :], perm_by_part).then_inc(s_perm, 16)

            def rows(g):
                for q in range(4):
                    src = acs_dram[:, bass.ds(g * GH + 4 * q, 4), :]
                    sp.dma_start(mov[32 * q:32 * q + 3, :, :], src).then_inc(s_rows, 16)
                    sp.dma_start(sta[32 * q + 3:32 * q + 6, :, :], src).then_inc(s_rows, 16)

            def load_in(n, i):
                wait(sp, s_lo, since(NIN * n, i, RAW_RING))
                sp.dma_start(raw[:, i % RAW_RING, :], w_in[bass.ds(n, 1), i, :, :]
                             .rearrange("a p c -> (a p) c")).then_inc(s_raw[i % RAW_RING], 16)

            def load_out(m, q):
                wait(sp, s_olo, since(CT * m, q, RAWO_RING))
                sp.dma_start(rawo[:, q % RAWO_RING, :], w_out[bass.ds(m, 1), q, :, :]
                             .rearrange("a p c -> (a p) c")).then_inc(s_rawo[q % RAWO_RING], 16)

            def iteration(n, do_in, do_ssd):
                m = n - 1
                if not do_ssd:
                    for i in range(NIN + 4):
                        load_in(n + i // NIN, i % NIN)
                        if i == 14:
                            sp.wait_ge(s_dtv, 4)
                            sp.dma_start(acs_dram.rearrange("r h t -> h r t"), parts).then_inc(s_acs, 16)
                        if i == 17:
                            sp.wait_ge(s_acs, 16)
                            sp.wait_ge(s_rows1, 2)
                            rows(n)
                    return
                for i in range(NIN):
                    if do_in and not (isinstance(n, int) and n == 1 and i < 4):
                        load_in(n, i)
                    if i >= 13 and i % 2:
                        load_out(m, (i - 13) // 2)
                if do_in:
                    sp.wait_ge(s_df, 3 * CT * m + 3 * CT)
                    rows(n)
                if do_ssd:
                    for q in range(3, CT):
                        load_out(m, q)

            iteration(0, True, False)
            iteration(1, True, True)
            with sp.Fori(2, loops) as n:
                iteration(n, True, True)

            def load_context(blocks):
                for c in blocks:
                    sp.dma_start(ctx_raw[c], ctx_in[c // DK, (c % DK) * P:(c % DK + 1) * P, :])\
                      .then_inc(s_ctx[c], 16)

            sp.wait_ge(s_lo, NIN * GROUPS)
            load_context((0, 1, 2))
            load_out(last_m, 0)
            load_out(last_m, 1)
            sp.wait_ge(s_conv, NCONV * GROUPS)
            sp.wait_ge(s_gate, CT * GROUPS)
            load_context((3, 4, 5))
            sp.wait_ge(s_t, (CT + 2) * GROUPS)
            load_context((6, 7))
            for q in range(2, CT):
                load_out(last_m, q)
            sp.wait_ge(s_olo, CT * GROUPS)
            sp.dma_start(up_raw, up).then_inc(s_ffw, 16)
            sp.dma_start(down_sb, down).then_inc(s_ffw, 16)
            for t in range(TT):
                sp.wait_ge(s_store, t + 1)
                sp.dma_start(out[t * P:(t + 1) * P, :], res[:, t, :]).then_inc(s_out, 16)
            sp.wait_ge(s_out, 16 * TT)

        @block.gpsimd
        def _(pool):
            pool.memset(ident[:, :], 0.0).then_inc(s_pp, 1)
            pool.memset(half[:, :, :], -0.5).then_inc(s_pp, 1)
            pool.memset(keep[:, :], 0.25).then_inc(s_pp, 1)
            pool.memset(sel[:, :], 1.0).then_inc(s_pp, 1)
            pool.wait_ge(s_pp, 4)
            pool.affine_select(out=ident[:, :], in_=ident[:, :], compare_op=ALU.not_equal, fill=1.0, base=0,
                               pattern=[[-1, P]], channel_multiplier=1).then_inc(s_pp, 1)
            pool.affine_select(out=keep[:, :], in_=keep[:, :], compare_op=ALU.is_ge, fill=0.0, base=0,
                               pattern=[[1, P]], channel_multiplier=-1).then_inc(s_pp, 1)
            pool.affine_select(out=sel[:, :], in_=sel[:, :], compare_op=ALU.is_ge, fill=0.0, base=0,
                               pattern=[[1, P]], channel_multiplier=-HD).then_inc(s_pp, 1)
            pool.wait_ge(s_pp, 7)
            pool.affine_select(out=sel[:, :], in_=sel[:, :], compare_op=ALU.is_ge, fill=0.0, base=HD - 1,
                               pattern=[[-1, P]], channel_multiplier=HD).then_inc(s_pp, 1)
            pool.iota(iota_row[:, :], [[1, D]], base=0, channel_multiplier=0,
                      allow_small_or_imprecise_dtypes=True).then_inc(s_iota, 1)
            pool.iota(dcol[:, :], [[P, DK]], base=0, channel_multiplier=1,
                      allow_small_or_imprecise_dtypes=True).then_inc(s_iota, 1)
            pool.memset(mov[:, :, :], 1.0).then_inc(s_rows1, 1)
            pool.memset(sta[:, :, :], -1.0).then_inc(s_rows1, 1)
            pool.wait_ge(s_var, 2)
            pool.tensor_tensor(rstds[:, :, :], rstds[:, :, :], half[:, :, :], ALU.pow).then_inc(s_rst, 1)

            def split_in(n, i):
                pool.wait_ge(s_hi, NIN * n + i + 1)
                wait(pool, s_in, since(NIN * n, i, W_RING))
                pool.tensor_tensor(w_lo[:, i % W_RING, :], raw[:, i % RAW_RING, :],
                                   w_hi[:, i % W_RING, :].bitcast(F32), ALU.subtract).then_inc(s_lo, 1)

            def split_out(m, q):
                pool.wait_ge(s_ohi, CT * m + q + 1)
                wait(pool, s_ou, since(CT * m, q, WO_RING))
                pool.tensor_tensor(wo_lo[:, q % WO_RING, :], rawo[:, q % RAWO_RING, :],
                                   wo_hi[:, q % WO_RING, :].bitcast(F32), ALU.subtract).then_inc(s_olo, 1)

            def decays_b(m, t):
                pool.wait_ge(s_exp, 3 * CT * m + 3 * t + 3)
                if t == 0:
                    pool.wait_ge(s_tf, (CT + 2) * (m + 1))
                b = eB[:, t % 2, :, :]
                pool.tensor_tensor(b, b, gmB[:, :, :].rearrange("p b i -> p (b i)").unsqueeze(1)
                                   .broadcast_to([P, 2, BATCH * P]), ALU.mult).then_inc(s_mb, 1)

            def add_square(m, t):
                pool.wait_ge(s_sq, CT * m + t + 1)
                if t > 1:
                    pool.wait_ge(s_sqs, (CT - 1) * m + t - 1)
                pool.tensor_tensor(sqsum[:, :], sqsum[:, :], sq[:, :], ALU.add).then_inc(s_sqs, 1)

            def group_rms(m):
                pool.wait_ge(s_ms, m + 1)
                pool.tensor_tensor(rgrp[:, :], ssum[:, :], half[:, 0, :], ALU.pow).then_inc(s_r, 1)

            def iteration(n, do_in, do_ssd):
                m = n - 1
                if do_in:
                    for i in first_tiles(n):
                        split_in(n, i)
                        if not do_ssd and i == 0:
                            pool.wait_ge(s_pa, 2)
                            pool.tensor_tensor(wo_lo[:, dt_slot, :], wdt_raw, wo_hi[:, dt_slot, :].bitcast(F32),
                                               ALU.subtract).then_inc(s_dtw, 1)
                for t in range(CT):
                    if do_ssd and t + 1 < CT:
                        decays_b(m, t + 1)
                    if do_in:
                        for i in step_tiles(n, t):
                            split_in(n, i)
                    if not do_ssd and t >= CT - TT:
                        k = t - (CT - TT)
                        pool.wait_ge(s_u, k + 1)
                        pool.tensor_tensor(res[:, k, :], res[:, k, :], u[:, k, :], ALU.add)\
                            .then_inc(s_res, 1)
                    if do_ssd:
                        if t:
                            add_square(m, t)
                        if t >= 4:
                            split_out(m, t - 4)
                if do_ssd:
                    split_out(m, 4)
                    split_out(m, 5)
                    group_rms(m)
                    split_out(m, 6)
                    split_out(m, 7)
                if do_in:
                    decays_b(n, 0)

            iteration(0, True, False)
            iteration(1, True, True)
            with pool.Fori(2, loops) as n:
                iteration(n, True, True)

            for q in range(2):
                split_out(last_m, q)
            for t in range(CT):
                if t + 1 < CT:
                    decays_b(last_m, t + 1)
                if t:
                    add_square(last_m, t)
                if out_tile_at(t):
                    split_out(last_m, out_tile_at(t))
            group_rms(last_m)

            for k, tiles in enumerate((slice(2, 4), slice(0, 2), slice(0, 2), slice(2, 4))):
                pool.wait_ge(s_ev, k + 1)
                pool.tensor_tensor(rstd[:, tiles], rstd[:, tiles], half[:, 0, tiles], ALU.pow).then_inc(s_ep, 1)
            pool.wait_ge(s_ep, 4)
            for j in range(4):
                r = slice(FD * j, FD * (j + 1))
                pool.wait_ge(s_uph, j + 1)
                pool.tensor_tensor(up_lo[r, :, j, :], up_raw[r, :, :], up_hi[r, :, j, :].bitcast(F32),
                                   ALU.subtract).then_inc(s_upl, 1)

        @block.scalar
        def _(act):
            def cast_in(n, i):
                act.wait_ge(s_raw[i % RAW_RING], (NIN // RAW_RING * 16) * n + 16 * (i // RAW_RING + 1))
                wait(act, s_in, since(NIN * n, i, W_RING))
                act.activation(w_hi[:, i % W_RING, :], raw[:, i % RAW_RING, :], ACT.Copy).then_inc(s_hi, 1)

            def cast_out(m, q):
                act.wait_ge(s_rawo[q % RAWO_RING], (CT // RAWO_RING * 16) * m + 16 * (q // RAWO_RING + 1))
                wait(act, s_ou, since(CT * m, q, WO_RING))
                act.activation(wo_hi[:, q % WO_RING, :], rawo[:, q % RAWO_RING, :], ACT.Copy).then_inc(s_ohi, 1)

            def conv_dst(c):
                return bc[:, c, :] if c < 2 else hid[:, c - 2, :]

            def tap0(n, c, do_ssd):
                i = c if c < 2 else 2 * c - 1
                act.wait_ge(s_in, NIN * n + i + 1)
                if c == 0:
                    act.wait_ge(s_cur, 2 * n + 1)
                if c < 2:
                    wait(act, s_t, (CT + 2) * n)
                elif do_ssd:
                    act.wait_ge(s_z1, CT * (n - 1) + c - 1)
                act.activation(conv_dst(c), bank_in(n, i), ACT.Identity, scale=curc[:, c * PAR + 3:c * PAR + 4],
                               bias=curc[:, c * PAR + 4:c * PAR + 5]).then_inc(s_tap0, 1)

            def conv_tanh(n, c):
                act.wait_ge(s_taps, NCONV * n + c + 1)
                wait(act, s_conv, since(NCONV * n, c, 2))
                act.activation(th[:, c % 2, :], conv_dst(c), ACT.Tanh, scale=0.5).then_inc(s_cth, 1)

            def gate_tanh(n, t):
                act.wait_ge(s_in, NIN * n + 3 + 2 * t)
                wait(act, s_gate, CT * n + t)
                act.activation(gth[:, :], bank_in(n, 2 + 2 * t), ACT.Tanh, scale=0.5).then_inc(s_gth, 1)

            def exps(m, t, banks):
                for k in banks:
                    act.wait_ge(s_df, 3 * CT * m + 3 * t + k + 1)
                    blocks = diagonal(df_bank(m, t, k), k)
                    act.activation(blocks, blocks, ACT.Relu).then_inc(s_cl, 1)
                for k in banks:
                    act.wait_ge(s_cl, 3 * CT * m + 3 * t + k + 1)
                    if k == 0:
                        if isinstance(m, int) and m == 0 and t == 0:
                            act.wait_ge(s_res, TT)
                        wait(act, s_y, since(CT * m, t, 2))
                    dst = eA[:, t % 2, k, :] if k < 2 else eB[:, t % 2, :, :].rearrange("p a n -> p (a n)")
                    act.activation(dst, df_bank(m, t, k), ACT.Exp, scale=-1.0).then_inc(s_exp, 1)

            def z_high_and_square(m, t):
                act.wait_ge(s_z, CT * m + t + 1)
                wait(act, s_ou, CT * m)
                act.activation(z_hi[:, t, :], z[:, t % 2, :], ACT.Copy,
                               scale=curs[:, CT + t:CT + t + 1]).then_inc(s_zhi, 1)
                if t == 0:
                    wait(act, s_ss, m)
                else:
                    wait(act, s_sqs, (CT - 1) * m + t - 1)
                act.activation(sqsum[:, :] if t == 0 else sq[:, :], z[:, t % 2, :],
                               ACT.Square).then_inc(s_sq, 1)

            def iteration(n, do_in, do_ssd):
                m = n - 1
                if do_in:
                    for i in (range(2, 4) if not do_ssd else first_tiles(n)):
                        cast_in(n, i)
                    tap0(n, 0, do_ssd)
                    if not do_ssd:
                        dt_exp()
                    tap0(n, 1, do_ssd)
                    if not do_ssd:
                        cast_in(n, 4)
                        cast_in(n, 5)
                    conv_tanh(n, 0)
                    conv_tanh(n, 1)
                    if not do_ssd:
                        dt_log()
                for t in range(CT):
                    if do_in:
                        if t:
                            tap0(n, t + 1, do_ssd)
                    if do_ssd and t + 1 < CT:
                        exps(m, t + 1, (0, 1))
                    if not do_ssd:
                        gate_tanh(n, t)
                    if do_in and t:
                        conv_tanh(n, t + 1)
                    if do_ssd:
                        if t + 1 < CT:
                            exps(m, t + 1, (2,))
                        z_high_and_square(m, t)
                    if do_in:
                        if do_ssd:
                            gate_tanh(n, t)
                        for i in step_tiles(n, t):
                            cast_in(n, i)
                    if do_ssd and t >= 4:
                        cast_out(m, t - 4)
                if do_in:
                    tap0(n, CT + 1, do_ssd)
                    conv_tanh(n, CT + 1)
                if do_ssd:
                    cast_out(m, 4)
                    cast_out(m, 5)
                if do_in:
                    exps(n, 0, (0, 1))
                if do_ssd:
                    cast_out(m, 6)
                    cast_out(m, 7)
                if do_in:
                    exps(n, 0, (2,))

            def dt_exp():
                act.wait_ge(s_dtv, 1)
                act.activation(sp_e, sp_a, ACT.Exp, scale=-1.0).then_inc(s_dta, 1)

            def dt_log():
                act.wait_ge(s_dtv, 2)
                act.activation(sp_l, sp_w, ACT.Ln).then_inc(s_dta, 1)
                act.preload_act_table(ACT.Exp)
                act.wait_ge(s_dta, 2)
                act.activation(sp_r, sp_l, ACT.Exp, scale=-1.0).then_inc(s_dta, 1)

            act.wait_ge(s_par, 16 * 7)
            act.activation(hcol[:, 2:3], hcol[:, 1:2], ACT.Exp).then_inc(s_pa, 1)
            cast_in(0, 0)
            act.wait_ge(s_nT, TT)
            for k in range(DK):
                act.activation(h_hi[:, k, :], turned_bank(k), ACT.Copy, scale=nw[:, k:k + 1]).then_inc(s_nhi, 1)
            act.wait_ge(s_wdt, 16)
            act.activation(wo_hi[:, dt_slot, :], wdt_raw, ACT.Copy).then_inc(s_pa, 1)
            cast_in(0, 1)
            iteration(0, True, False)
            iteration(1, True, True)
            with act.Fori(2, loops) as n:
                iteration(n, True, True)

            cast_out(last_m, 0)
            cast_out(last_m, 1)
            for t in range(CT):
                if t + 1 < CT:
                    exps(last_m, t + 1, (0, 1, 2))
                z_high_and_square(last_m, t)
                if out_tile_at(t):
                    cast_out(last_m, out_tile_at(t))
                act.wait_ge(s_ctx[t], 16)
                act.activation(ctx_raw[t], ctx_raw[t], ACT.Identity, scale=qd[:, 1:2], bias=qs[:, 3:4])\
                   .then_inc(s_cs, 1)
            act.preload_act_table(ACT.Gelu)

            for k, t in enumerate((2, 3, 0, 1)):
                act.wait_ge(s_aff, k // 2 + 1)
                act.activation(e1[:, t, :], res[:, t, :], ACT.Identity, scale=qa[:, t:t + 1],
                               bias=qb[:, t:t + 1]).then_inc(s_x1, 1)
            act.wait_ge(s_q1t, 1)
            act.activation(q1T[:, 0:2, :].rearrange("p a n -> p (a n)"), ps_y[:, :].bitcast(BF16), ACT.Copy)\
               .then_inc(s_q1a, 1)

            act.wait_ge(s_rq, 1)
            for t in range(TT):
                act.activation(res[:, t, :], res[:, t, :], ACT.Identity, bias=rowq[:, t:t + 1]).then_inc(s_px, 1)

            act.wait_ge(s_ffw, 32)
            act.wait_ge(s_ou, CT * GROUPS)
            for w in (wo_hi, wo_lo):
                act.activation(w[:, :, :].rearrange("p a n -> p (a n)"), ones[:, :].broadcast_to([P, WO_RING * D]),
                               ACT.Copy, scale=0.0).then_inc(s_upz, 1)
            act.wait_ge(s_upz, 2)
            for j in range(4):
                r = slice(FD * j, FD * (j + 1))
                act.activation(up_hi[r, :, j, :], up_raw[r, :, :], ACT.Copy).then_inc(s_uph, 1)
            act.wait_ge(s_ft, 1)
            for k in range(DK):
                act.activation(f_hi[:, k, :], feature_bank(k), ACT.Copy).then_inc(s_fhi, 1)
            for k in range(DK):
                act.wait_ge(s_p, k + 1)
                act.activation(p_hi[:, k, :], permuted_bank(k), ACT.Copy).then_inc(s_phi, 1)
            for h in range(FH):
                act.wait_ge(s_up, h + 1)
                act.activation(gel[h], wide_bank(h), ACT.Gelu).then_inc(s_gl, 1)

        @block.vector
        def _(dve):
            chain = [0]

            def step(ins):
                chain[0] += 1
                ins.then_inc(s_v, 1)
                dve.wait_ge(s_v, chain[0])

            for t in range(TT):
                dve.wait_ge(s_x[t], 16)
                dve.bn_stats(stats[:, t, :], res[:, t, :]).then_inc(s_v, 1)
            for t in range(TT):
                dve.wait_ge(s_v, t + 1)
                dve.bn_aggr(mv[:, t, :], stats[:, t, :]).then_inc(s_v, 1)
            chain[0] = 2 * TT
            dve.wait_ge(s_v, 2 * TT)
            dve.tensor_scalar(rstds[:, 0, :], mv[:, :, 1], EPS, None, ALU.add).then_inc(s_var, 1)
            dve.wait_ge(s_var, 1)
            dve.scalar_tensor_tensor(rstds[:, 1, :], rstds[:, 0, :], EPS, mv[:, :, 1], ALU.mult, ALU.add)\
               .then_inc(s_var, 1)
            dve.wait_ge(s_rst, 1)
            for t in range(TT):
                dve.tensor_scalar(v[:, t, :], res[:, t, :], mv[:, t, 0:1], rstds[:, 1, t:t + 1],
                                  ALU.subtract, ALU.mult).then_inc(s_nt, 1)
            dve.memset(ones[:, :], 1.0)
            dve.memset(ones_b[:, :], 1.0)
            dve.wait_ge(s_pp, 5)
            dve.tensor_copy(ident_b[:, :], ident[:, :])
            dve.memset(one_row, 1.0)
            for t in range(TT):
                dve.tensor_scalar(u[:, t, :], res[:, t, :], mv[:, t, 0:1], rstds[:, 0, t:t + 1],
                                  ALU.subtract, ALU.mult).then_inc(s_u, 1)
            dve.wait_ge(s_par, 16 * 7)
            for k in range(DK):
                dve.wait_ge(s_nhi, k + 1)
                dve.scalar_tensor_tensor(h_lo[:, k, :], turned_bank(k), nw[:, k:k + 1],
                                         h_hi[:, k, :].bitcast(F32), ALU.mult, ALU.subtract).then_inc(s_nlo, 1)

            dve.tensor_scalar(skipgn[:, :, CT:2 * CT], gn_in[:, :].rearrange("p (g t) -> p g t", g=GROUPS),
                              0.5, None, ALU.mult)
            dve.wait_ge(s_perm, 32)
            dve.tensor_copy(perm_row[:, :], perm_row_i)
            dve.tensor_copy(perm_col[:, :], perm_col_i[:, :])
            for k in range(2):
                dve.reciprocal(qd[:, k:k + 1], qs[:, 2 * k:2 * k + 1])
                dve.tensor_scalar(qd[:, 2 + k:3 + k], qs[:, 2 * k + 1:2 * k + 2], -128.0, None, ALU.add)
            step(dve.tensor_tensor(qd[:, 4:5], qs[:, 0:1], qs[:, 2:3], ALU.mult))
            dve.scalar_tensor_tensor(qd[:, 5:6], qd[:, 2:3], -1.0, qd[:, 4:5], ALU.mult, ALU.mult)
            dve.tensor_scalar(qd[:, 6:7], qd[:, 2:3], float(D), None, ALU.mult)
            step(dve.scalar_tensor_tensor(qd[:, 7:8], qd[:, 3:4], -1.0, qd[:, 4:5], ALU.mult, ALU.mult))

            def dt_abs():
                dve.wait_ge(s_dt, 1)
                step(dve.tensor_scalar(sp_v, ps_y[:, :], hcol[:, 0:1], None, ALU.add))
                dve.scalar_tensor_tensor(sp_a, sp_v, -1.0, sp_v, ALU.mult, ALU.max).then_inc(s_dtv, 1)

            def dt_w():
                dve.wait_ge(s_dta, 1)
                dve.tensor_scalar(sp_w, sp_e, 1.0, None, ALU.add).then_inc(s_dtv, 1)
                dve.wait_ge(s_dtv, 2)
                step(dve.tensor_scalar(sp_a, sp_w, -1.0, None, ALU.add))
                step(dve.tensor_tensor(sp_c, sp_e, sp_a, ALU.subtract))

            def dt_sum():
                dve.wait_ge(s_dta, 3)
                step(dve.tensor_tensor(sp_c, sp_c, sp_r, ALU.mult))
                step(dve.tensor_tensor(sp_c, sp_c, sp_l, ALU.add))
                dve.scalar_tensor_tensor(dt_h, sp_v, 0.0, sp_c, ALU.max, ALU.add).then_inc(s_dtv, 1)
                dve.wait_ge(s_dtv, 3)
                step(dve.tensor_scalar(r1, dt_h, hcol[:, 2:3], -1.0, ALU.mult, ALU.mult))

            def dt_keep():
                dve.wait_ge(s_dtt, 1)
                dve.tensor_scalar(dtT[:, :, :], ps_y[:, :].rearrange("p (c h) -> p c h", c=TT), 0.5, None,
                                  ALU.mult).then_inc(s_dtT, 1)
                dve.wait_ge(s_dtT, 1)
                dve.tensor_copy(dtg[:, :, :], dtT[:, :, 0:GH]).then_inc(s_cur, 1)
                dve.wait_ge(s_cur, 2)

            def running_sums():
                for b in range(BATCH):
                    seq = slice(b * SEQ, (b + 1) * SEQ)
                    step(dve.tensor_tensor_scan(acs[:, seq], one_row[:, seq], r1[:, seq], 0.0, ALU.mult, ALU.add))
                step(dve.tensor_copy(parts[:, 0, :], acs))

            def other_parts():
                step(dve.tensor_tensor(r1, acs, parts[:, 0, :], ALU.subtract))
                step(dve.tensor_copy(parts[:, 1, :], r1))
                step(dve.tensor_tensor(r2, r1, parts[:, 1, :], ALU.subtract))
                dve.tensor_copy(parts[:, 2, :], r2).then_inc(s_dtv, 1)

            def skip_params():
                dve.wait_ge(s_skip, 1)
                step(dve.tensor_scalar(skipgn[:, :, 0:CT], ps_df[:, 0, 0:GROUPS * CT]
                                       .rearrange("p (g t) -> p g t", g=GROUPS), 0.5, None, ALU.mult))

            def conv_dst(c):
                return bc[:, c, :] if c < 2 else hid[:, c - 2, :]

            def taps(n, c):
                i = c if c < 2 else 2 * c - 1
                dve.wait_ge(s_tap0, NCONV * n + c + 1)
                y = conv_dst(c).rearrange("p (b s) -> p b s", b=BATCH)
                src = bank_in(n, i).rearrange("p (b s) -> p b s", b=BATCH)
                for a in range(1, TAPS):
                    last = dve.scalar_tensor_tensor(y[:, :, a:], src[:, :, 0:SEQ - a],
                                                    curc[:, c * PAR + 3 - a:c * PAR + 4 - a], y[:, :, a:],
                                                    ALU.mult, ALU.add)
                    if a < TAPS - 1:
                        last.then_inc(s_vt, 1)
                        dve.wait_ge(s_vt, (TAPS - 2) * (NCONV * n + c) + a)
                last.then_inc(s_taps, 1)

            def conv_silu(n, c):
                dve.wait_ge(s_cth, NCONV * n + c + 1)
                dve.scalar_tensor_tensor(conv_dst(c), th[:, c % 2, :], 1.0, conv_dst(c), ALU.add, ALU.mult)\
                   .then_inc(s_conv, 1)

            def gated(n, t):
                dve.wait_ge(s_gth, CT * n + t + 1)
                if isinstance(n, int) and n == 0 and t == 6:
                    dve.wait_ge(s_acs, 16)
                dve.scalar_tensor_tensor(gate[:, t, :], gth[:, :], 1.0, bank_in(n, 2 + 2 * t), ALU.add, ALU.mult)\
                   .then_inc(s_gate, 1)

            def turned(n, t):
                dve.wait_ge(s_t, (CT + 2) * n + t + 1)
                dve.tensor_tensor(
                    hdt[:, :, t * P:(t + 1) * P].rearrange("p c (h q) -> p c h q", h=2),
                    ps_t[:, :].rearrange("p (c h q) -> p c h q", c=TT, h=2),
                    dtg[:, :, 2 * t:2 * t + 2].unsqueeze(3).broadcast_to([P, TT, 2, HD]),
                    ALU.mult).then_inc(s_tf, 1)

            def scores(n):
                dve.wait_ge(s_t, (CT + 2) * n + CT + 1)
                src = ps_t[:, :].rearrange("p (b i) -> p b i", b=BATCH)
                dve.tensor_tensor(gmA[:, :, 0:P], src[:, :, 0:P], keep[:, :].unsqueeze(1).broadcast_to([P, BATCH, P]),
                                  ALU.mult)
                dve.tensor_scalar(gmA[:, :, P:SEQ], src[:, :, P:SEQ], 0.25, None, ALU.mult).then_inc(s_tf, 1)
                dve.wait_ge(s_t, (CT + 2) * n + CT + 2)
                dve.tensor_tensor(gmB[:, :, :], ps_t[:, 0:BATCH * P].rearrange("p (b i) -> p b i", b=BATCH),
                                  keep[:, :].unsqueeze(1).broadcast_to([P, BATCH, P]), ALU.mult).then_inc(s_tf, 1)

            def decays_a(m, t):
                dve.wait_ge(s_exp, 3 * CT * m + 3 * t + 2)
                if t == 0:
                    dve.wait_ge(s_tf, (CT + 2) * (m + 1))
                a = eA[:, t % 2, :, :]
                dve.tensor_tensor(a, a, gmA[:, :, :].rearrange("p b i -> p (b i)").unsqueeze(1)
                                  .broadcast_to([P, 2, TOK]), ALU.mult).then_inc(s_ma, 1)

            def ssd_params(m):
                wait(dve, s_zhi, CT * m)
                dve.tensor_copy(curs[:, :], skipgn[:, bass.ds(m, 1), :].rearrange("p a c -> p (a c)"))\
                   .then_inc(s_curs, 1)

            def skip_and_gate(m, t):
                dve.wait_ge(s_y, CT * m + t + 1)
                wait(dve, s_sq, since(CT * m, t, 2))
                dve.scalar_tensor_tensor(z[:, t % 2, :], hid[:, t, :], curs[:, t:t + 1], ps_y[:, :],
                                         ALU.mult, ALU.add).then_inc(s_z1, 1)
                dve.wait_ge(s_z1, CT * m + t + 1)
                dve.tensor_tensor(z[:, t % 2, :], z[:, t % 2, :], gate[:, t, :], ALU.mult).then_inc(s_z, 1)

            def z_low(m, t):
                dve.wait_ge(s_zhi, CT * m + t + 1)
                wait(dve, s_ou, CT * m)
                dve.scalar_tensor_tensor(z_lo[:, t, :], z[:, t % 2, :], curs[:, CT + t:CT + t + 1],
                                         z_hi[:, t, :].bitcast(F32), ALU.mult, ALU.subtract).then_inc(s_zlo, 1)

            def mean_square(m):
                dve.wait_ge(s_ss, m + 1)
                dve.tensor_scalar(ssum[:, :], ps_y[:, 0:TT], 1.0 / (4 * GC), EPS, ALU.mult, ALU.add)\
                   .then_inc(s_ms, 1)

            def add_output(t):
                dve.scalar_tensor_tensor(res[:, t, :], out_bank(t), rgrp[:, t:t + 1], res[:, t, :],
                                         ALU.mult, ALU.add).then_inc(s_ofi if t >= 2 else s_of, 1)

            def iteration(n, do_in, do_ssd):
                m = n - 1
                lag = 1 if do_ssd else 2
                if do_in:
                    wait(dve, s_tap0, NCONV * n)
                    dve.tensor_copy(curc[:, :], convp[:, bass.ds(n, 1), :].rearrange("p a c -> p (a c)"))\
                       .then_inc(s_cur, 1)
                    if do_ssd:
                        dve.tensor_copy(dtg[:, :, :], dtT[:, :, bass.ds(n * GH, GH)]).then_inc(s_cur, 1)
                if do_ssd:
                    ssd_params(m)
                if do_in:
                    dve.wait_ge(s_cur, 2 * n + (2 if do_ssd else 1))
                    taps(n, 0)
                    if not do_ssd:
                        dt_abs()
                    taps(n, 1)
                    conv_silu(n, 0)
                    conv_silu(n, 1)
                    if not do_ssd:
                        dt_w()
                if do_ssd:
                    dve.wait_ge(s_curs, m + 1)
                for t in range(CT):
                    if do_in and t:
                        taps(n, t + 1)
                    if do_ssd:
                        skip_and_gate(m, t)
                    if not do_ssd:
                        gated(n, t)
                    if do_in and t:
                        conv_silu(n, t + 1)
                    if do_ssd:
                        if t + 1 < CT:
                            decays_a(m, t + 1)
                        z_low(m, t)
                    if not do_ssd and t == 2:
                        dt_keep()
                    if do_in:
                        if do_ssd:
                            gated(n, t)
                        if t >= lag:
                            turned(n, t - lag)
                    if not do_ssd and 1 <= t < 5:
                        (dt_sum, running_sums, other_parts, skip_params)[t - 1]()
                if do_in:
                    if not do_ssd:
                        turned(n, CT - 2)
                    taps(n, CT + 1)
                    conv_silu(n, CT + 1)
                if do_ssd:
                    mean_square(m)
                if do_in:
                    turned(n, CT - 1)
                    scores(n)
                    decays_a(n, 0)
                if do_ssd:
                    dve.wait_ge(s_r, m + 1)
                    dve.wait_ge(s_oin, m + 1)
                    for t in (2, 3, 0, 1):
                        if t == 0:
                            dve.wait_ge(s_ou, CT * (m + 1))
                        add_output(t)

            iteration(0, True, False)
            iteration(1, True, True)
            with dve.Fori(2, loops) as n:
                iteration(n, True, True)

            def round_context(c):
                dve.wait_ge(s_cs, c + 1)
                step(dve.tensor_scalar(ctx_raw[c], ctx_raw[c], 0.0, 255.0, ALU.max, ALU.min))
                dve.tensor_scalar(q2[:, c, :], ctx_raw[c], MAGIC, -(MAGIC + 128.0), ALU.add, ALU.add)\
                   .then_inc(s_q2, 1)

            def one_hot(k):
                dve.tensor_scalar(take[:, k, :], perm_row[:, :], dcol[:, k:k + 1], None, ALU.is_equal)\
                   .then_inc(s_tp, 1)
                dve.tensor_scalar(put[:, k, :], iota_row[:, :], perm_col[:, k:k + 1], None, ALU.is_equal)\
                   .then_inc(s_tp, 1)

            ssd_params(last_m)
            dve.wait_ge(s_curs, GROUPS)
            dve.wait_ge(s_iota, 2)
            for t in range(CT):
                skip_and_gate(last_m, t)
                if t + 1 < CT:
                    decays_a(last_m, t + 1)
                z_low(last_m, t)
                round_context(t)
                if t < DK:
                    one_hot(t)
            mean_square(last_m)

            def variance(tiles):
                dve.wait_ge(s_v, chain[0])
                for t in tiles:
                    dve.bn_aggr(mv[:, t, :], stats[:, t, :]).then_inc(s_v, 1)
                chain[0] += 2
                dve.wait_ge(s_v, chain[0])
                two = slice(tiles[0], tiles[0] + 2)
                dve.tensor_scalar(rstd[:, two], mv[:, two, 1], EPS, None, ALU.add).then_inc(s_ev, 1)

            def statistics(t):
                dve.bn_stats(stats[:, t, :], res[:, t, :]).then_inc(s_v, 1)
                chain[0] += 1

            def quant_scales(tiles):
                two = slice(tiles[0], tiles[0] + 2)
                step(dve.tensor_scalar(qa[:, two], rstd[:, two], qd[:, 0:1], None, ALU.mult))
                step(dve.tensor_tensor(qb[:, two], mv[:, two, 0], qa[:, two], ALU.mult))
                dve.tensor_scalar(qb[:, two], qb[:, two], -1.0, qs[:, 1:2], ALU.mult, ALU.add).then_inc(s_aff, 1)

            def round_norm(t, done):
                dve.wait_ge(s_x1, done + 1)
                step(dve.tensor_scalar(e1[:, t, :], e1[:, t, :], 0.0, 255.0, ALU.max, ALU.min))
                dve.tensor_scalar(q1[:, t, :], e1[:, t, :], MAGIC, -(MAGIC + 128.0), ALU.add, ALU.add)\
                   .then_inc(s_q1, 1)

            dve.wait_ge(s_r, GROUPS)
            for pair, ready in (((2, 3), (s_oin, GROUPS)), ((0, 1), (s_ou, CT * GROUPS))):
                dve.wait_ge(*ready)
                for t in pair:
                    add_output(t)
                dve.wait_ge(s_ofi if 2 in pair else s_of, 2 * GROUPS)
                for t in pair:
                    statistics(t)
                if 0 in pair:
                    dve.wait_ge(s_ep, 1)
                    quant_scales((2, 3))
                variance(pair)
            round_norm(2, 0)
            round_norm(3, 1)
            dve.wait_ge(s_ep, 2)
            quant_scales((0, 1))
            round_norm(0, 2)
            round_norm(1, 3)
            dve.wait_ge(s_cq, 1)
            for t in range(2):
                step(dve.scalar_tensor_tensor(res[:, t, :], ps_df[:, t // 2, :], qd[:, 5:6], res[:, t, :],
                                              ALU.mult, ALU.add))
            dve.wait_ge(s_q1t, 1)
            dve.tensor_copy(q1T[:, 2:4, :].rearrange("p a n -> p (a n)"), ps_t[:, :].bitcast(BF16)).then_inc(s_q1v, 1)
            for t in range(2, TT):
                step(dve.scalar_tensor_tensor(res[:, t, :], ps_df[:, t // 2, :], qd[:, 5:6], res[:, t, :],
                                              ALU.mult, ALU.add))
            dve.wait_ge(s_rs, 1)
            dve.tensor_scalar(rowq[:, :], ps_y[:, 0:TT], qd[:, 6:7], qd[:, 7:8], ALU.subtract, ALU.mult)\
               .then_inc(s_rq, 1)
            for t in range(TT):
                dve.wait_ge(s_px, t + 1)
                dve.wait_ge(s_pr, t + 1)
                step(dve.scalar_tensor_tensor(res[:, t, :], out_bank(t), qd[:, 4:5], res[:, t, :],
                                              ALU.mult, ALU.add))
                statistics(t)
                if t % 2:
                    variance((t - 1, t))

            for t in range(TT):
                dve.wait_ge(s_ep, 3 + t // 2)
                dve.tensor_scalar(e1[:, t, :], res[:, t, :], mv[:, t, 0:1], rstd[:, t:t + 1],
                                  ALU.subtract, ALU.mult).then_inc(s_f, 1)
            for k in range(DK):
                dve.wait_ge(s_fhi, k + 1)
                dve.tensor_tensor(f_lo[:, k, :], feature_bank(k), f_hi[:, k, :].bitcast(F32), ALU.subtract)\
                   .then_inc(s_flo, 1)
            for k in range(DK):
                dve.wait_ge(s_phi, k + 1)
                dve.tensor_tensor(p_lo[:, k, :], permuted_bank(k), p_hi[:, k, :].bitcast(F32), ALU.subtract)\
                   .then_inc(s_plo, 1)
            for k in range(DK):
                dve.wait_ge(s_dn, k + 1)
                src = feature_bank(k)
                step(dve.tensor_copy(f_hi[:, k, :], src))
                dve.tensor_tensor(f_lo[:, k, :], src, f_hi[:, k, :].bitcast(F32), ALU.subtract).then_inc(s_dlo, 1)
            for t in range(TT):
                dve.wait_ge(s_fin, t + 1)
                dve.tensor_tensor(res[:, t, :], res[:, t, :], wide_bank(t), ALU.add).then_inc(s_store, 1)

        @block.tensor
        def _(pe):
            def split3(dst, lhs, rhs, first, last):
                (lh, ll), (rh, rl) = lhs, rhs
                pe.matmul(dst, lh, rh, start=first, stop=False)
                pe.matmul(dst, lh, rl, start=False, stop=False)
                return pe.matmul(dst, ll, rh, start=False, stop=last)

            pe.wait_ge(s_pp, 5)
            for t in range(TT):
                pe.wait_ge(s_nt, t + 1)
                for k in range(DK):
                    last = pe.transpose(turned_bank(k)[:, t * P:(t + 1) * P], v[:, t, k * P:(k + 1) * P],
                                        ident[:, :])
                last.then_inc(s_nT, 1)

            def dt_product():
                pe.wait_ge(s_dtw, 1)
                for k in range(DK):
                    cols = slice(k * P, (k + 1) * P)
                    last = split3(ps_y[:, :], (wo_hi[:, dt_slot, cols], wo_lo[:, dt_slot, cols]),
                                  (h_hi[:, k, :], h_lo[:, k, :]), k == 0, k == DK - 1)
                last.then_inc(s_dt, 1)
                pe.wait_ge(s_par, 16 * 7)
                pe.matmul(ps_df[:, 0, 0:GROUPS * CT], sel[:, :], d2[:, :], start=True, stop=True).then_inc(s_skip, 1)

            def dt_turn():
                pe.wait_ge(s_dtv, 3)
                for t in range(TT):
                    last = pe.transpose(ps_y[:, t * P:(t + 1) * P], dt_h[:, t * P:(t + 1) * P], ident[:, :])
                last.then_inc(s_dtt, 1)

            def project(n, i, do_ssd):
                pe.wait_ge(s_lo, NIN * n + i + 1)
                ring = 4 if isinstance(n, int) and n == 0 else 2
                if i < ring:
                    if i % 2:
                        wait(pe, s_taps, NCONV * n)
                    else:
                        wait(pe, s_gate, CT * n)
                elif i % 2 or i == ring:
                    wait(pe, s_taps, NCONV * n + (i - ring + 3) // 2)
                else:
                    wait(pe, s_gate, CT * n + (i - ring) // 2)
                if do_ssd and i == 0:
                    wait(pe, s_ofi, 2 * (n - 1))
                for k in range(DK):
                    if not do_ssd and i == 0:
                        pe.wait_ge(s_nlo, k + 1)
                    cols = slice(k * P, (k + 1) * P)
                    last = split3(bank_in(n, i), (w_hi[:, i % W_RING, cols], w_lo[:, i % W_RING, cols]),
                                  (h_hi[:, k, :], h_lo[:, k, :]), k == 0, k == DK - 1)
                last.then_inc(s_in, 1)

            def turn(n, t):
                pe.wait_ge(s_conv, NCONV * n + t + 3)
                wait(pe, s_tf, (CT + 2) * n + t)
                for c in range(TT):
                    last = pe.transpose(ps_t[:, c * P:(c + 1) * P], hid[:, t, c * P:(c + 1) * P], ident[:, :])
                last.then_inc(s_t, 1)

            def scores_a(n):
                pe.wait_ge(s_tf, (CT + 2) * n + CT)
                for b in range(BATCH):
                    at = b * SEQ
                    last = pe.matmul(ps_t[:, at:at + SEQ], bc[:, 0, at:at + P], bc[:, 1, at:at + SEQ],
                                     start=True, stop=True)
                last.then_inc(s_t, 1)

            def scores_b(n):
                pe.wait_ge(s_tf, (CT + 2) * n + CT + 1)
                for b in range(BATCH):
                    at = b * SEQ + P
                    last = pe.matmul(ps_t[:, b * P:(b + 1) * P], bc[:, 0, at:at + P], bc[:, 1, at:at + P],
                                     start=True, stop=True)
                last.then_inc(s_t, 1)

            def diffs(m, t, banks):
                if t == 0:
                    pe.wait_ge(s_rows, 16 * 8 * (m + 1))
                for k in banks:
                    if isinstance(m, int) and m == last_m and t:
                        pe.wait_ge(s_exp, 3 * CT * m + (3 if t == 1 else 3 * (t - 1) + k + 1))
                    else:
                        wait(pe, s_exp, since(3 * CT * m, 3 * t + k, 2))
                    bank = df_bank(m, t, k)
                    heads = (k,) if k < 2 else (0, 1)
                    for hh in heads:
                        h = 2 * t + hh
                        q = slice(32 * (h // 4), 32 * (h // 4) + 6)
                        for b in range(BATCH):
                            at = b * SEQ if k < 2 else b * SEQ + P
                            width = SEQ if k < 2 else P
                            to = b * SEQ if k < 2 else (hh * BATCH + b) * P
                            last = pe.matmul(bank[:, to:to + width], sta[q, h % 4, at:at + P],
                                             mov[q, h % 4, at:at + width], start=True, stop=True)
                    last.then_inc(s_df, 1)

            def outputs(m, t):
                pe.wait_ge(s_ma, CT * m + t + 1)
                pe.wait_ge(s_mb, CT * m + t + 1)
                if t == 0:
                    wait(pe, s_ms, m)
                wait(pe, s_z1, CT * m + t)
                for b in range(BATCH):
                    at = b * SEQ
                    for half_seq in range(2):
                        for hh in range(2):
                            rows_ = slice(HD * hh, HD * (hh + 1))
                            w = hdt[:, 2 * b + half_seq, t * P + HD * hh:t * P + HD * (hh + 1)]
                            if half_seq == 0:
                                last = pe.matmul(ps_y[rows_, at:at + SEQ], w, eA[:, t % 2, hh, at:at + SEQ],
                                                 start=True, stop=False, skip_group_check=True)
                            else:
                                last = pe.matmul(ps_y[rows_, at + P:at + SEQ], w,
                                                 eB[:, t % 2, hh, b * P:(b + 1) * P],
                                                 start=False, stop=True, skip_group_check=True)
                last.then_inc(s_y, 1)

            def token_sums(m):
                pe.wait_ge(s_sqs, (CT - 1) * (m + 1))
                pe.wait_ge(s_z1, CT * (m + 1))
                for t in range(TT):
                    last = pe.matmul(ps_y[:, t:t + 1], sqsum[:, t * P:(t + 1) * P], ones[:, :],
                                     start=True, stop=True)
                last.then_inc(s_ss, 1)

            def out_pair(m, j, token_tiles, do_in):
                first_use = j == 0 and 0 in token_tiles
                if first_use:
                    wait(pe, s_of, 2 * m)
                pe.wait_ge(s_zlo, CT * m + 2 * j + 2)
                pe.wait_ge(s_olo, CT * m + 2 * j + 2)
                if j == 0 and 2 in token_tiles and do_in:
                    pe.wait_ge(s_gate, CT * (m + 2))
                    pe.wait_ge(s_taps, NCONV * (m + 2))
                frees = 0 if j == CT // 2 - 1 else 2
                for k in (2 * j, 2 * j + 1):
                    for t in token_tiles:
                        cols = slice(t * P, (t + 1) * P)
                        last = split3(out_bank(t), (z_hi[:, k, cols], z_lo[:, k, cols]),
                                      (wo_hi[:, k % WO_RING, :], wo_lo[:, k % WO_RING, :]), k == 0, k == CT - 1)
                    if frees in token_tiles:
                        last.then_inc(s_ou, 1)
                    elif k == CT - 1:
                        last.then_inc(s_oin, 1)

            def iteration(n, do_in, do_ssd):
                m = n - 1
                lag = 1 if do_ssd else 2
                if do_in and not (isinstance(n, int) and n == 1):
                    project(n, 0, do_ssd)
                    if not do_ssd:
                        dt_product()
                    project(n, 1, do_ssd)
                for t in range(CT):
                    if do_ssd:
                        outputs(m, t)
                        if t + 1 < CT:
                            diffs(m, t + 1, (0, 1))
                    if do_in:
                        project(n, 2 + 2 * t, do_ssd)
                    if do_ssd and t + 1 < CT:
                        diffs(m, t + 1, (2,))
                    if do_in:
                        project(n, 3 + 2 * t, do_ssd)
                        if not do_ssd and t == 2:
                            dt_turn()
                        if t >= lag:
                            turn(n, t - lag)
                if do_ssd:
                    out_pair(m, 0, (0, 1), do_in)
                    out_pair(m, 1, (0, 1), do_in)
                if not do_ssd:
                    turn(n, CT - 2)
                    project(n + 1, 0, True)
                    project(n + 1, 1, True)
                turn(n, CT - 1)
                if do_ssd:
                    out_pair(m, 0, (2, 3), do_in)
                    token_sums(m)
                    out_pair(m, 1, (2, 3), do_in)
                scores_a(n)
                diffs(n, 0, (0, 1))
                if do_ssd:
                    out_pair(m, 2, (0, 1), do_in)
                    out_pair(m, 2, (2, 3), do_in)
                scores_b(n)
                diffs(n, 0, (2,))
                if do_ssd:
                    out_pair(m, 3, (2, 3), do_in)
                    out_pair(m, 3, (0, 1), do_in)

            iteration(0, True, False)
            iteration(1, True, True)
            with pe.Fori(2, loops) as n:
                iteration(n, True, True)

            pe.wait_ge(s_tf, (CT + 2) * GROUPS)
            def out_tile(k):
                if k == 0:
                    pe.wait_ge(s_of, 2 * last_m)
                pe.wait_ge(s_zlo, CT * last_m + k + 1)
                pe.wait_ge(s_olo, CT * last_m + k + 1)
                for t in (0, 1, 2, 3) if k < CT - 1 else (2, 3, 0, 1):
                    cols = slice(t * P, (t + 1) * P)
                    last = split3(out_bank(t), (z_hi[:, k, cols], z_lo[:, k, cols]),
                                  (wo_hi[:, k % WO_RING, :], wo_lo[:, k % WO_RING, :]), k == 0, k == CT - 1)
                    if k == CT - 1 and t == 3:
                        last.then_inc(s_oin, 1)
                last.then_inc(s_ou, 1)

            for t in range(CT):
                if t + 1 < CT:
                    diffs(last_m, t + 1, (0, 1, 2))
                outputs(last_m, t)
                if t >= 2:
                    out_tile(t - 2)
            out_tile(CT - 2)
            token_sums(last_m)
            out_tile(CT - 1)

            pe.wait_ge(s_q2, BATCH * DK)
            pe.wait_ge(s_exp, 3 * CT * GROUPS)
            for b in range(BATCH):
                for k in range(DK):
                    last = pe.matmul(ps_df[:, b, :], ones_b[:, :], q2[:, b * DK + k, :],
                                     start=(k == 0), stop=(k == DK - 1))
            last.then_inc(s_cq, 1)
            pe.wait_ge(s_ms, GROUPS)
            pe.wait_ge(s_tf, (CT + 2) * GROUPS)
            for done, t in enumerate((2, 3, 0, 1)):
                pe.wait_ge(s_q1, done + 1)
                for k in range(DK):
                    bank = (ps_t if k >= 2 else ps_y)[:, :].bitcast(BF16)
                    at = (k % 2) * TOK + t * P
                    last = pe.transpose(bank[:, at:at + P], q1[:, t, k * P:(k + 1) * P], ident_b[:, :])
            last.then_inc(s_q1t, 1)

            def product(t, ks):
                for k in ks:
                    last = pe.matmul(out_bank(t), q1T[:, k, t * P:(t + 1) * P], q2[:, (t // 2) * DK + k, :],
                                     start=(k == 0), stop=(k == DK - 1), skip_group_check=True)
                return last

            pe.wait_ge(s_q1a, 1)
            pe.wait_ge(s_of, 2 * GROUPS)
            pe.wait_ge(s_ofi, 2 * GROUPS)
            for t in range(TT):
                product(t, (0, 1))
            pe.wait_ge(s_q1v, 1)
            for t in range(TT):
                for k in range(DK):
                    last = pe.matmul(ps_y[:, t:t + 1], q1T[:, k, t * P:(t + 1) * P], ones_b[:, 0:1],
                                     start=(k == 0), stop=(k == DK - 1))
            last.then_inc(s_rs, 1)
            for t in range(TT):
                product(t, (2, 3)).then_inc(s_pr, 1)

            for t in range(TT):
                pe.wait_ge(s_f, t + 1)
                for k in range(DK):
                    last = pe.transpose(feature_bank(k)[:, t * P:(t + 1) * P], e1[:, t, k * P:(k + 1) * P],
                                        ident[:, :])
            last.then_inc(s_ft, 1)
            pe.wait_ge(s_tp, 2 * DK)
            for d in range(DK):
                pe.wait_ge(s_flo, d + 1)
                for k in range(DK):
                    for part in (f_hi, f_lo):
                        last = pe.matmul(permuted_bank(k), take[:, d, k * P:(k + 1) * P], part[:, d, :],
                                         start=(d == 0 and part is f_hi), stop=(d == DK - 1 and part is f_lo),
                                         skip_group_check=True)
                    if d == DK - 1:
                        last.then_inc(s_p, 1)

            def up_product(h):
                if h < 4:
                    pe.wait_ge(s_plo, h + 1)
                else:
                    pe.wait_ge(s_gl, h - 3)
                if h >= 4 and h % 4 == 0:
                    pe.wait_ge(s_plo, h // 4 + 1)
                k, j = h // 4, h % 4
                split3(wide_bank(h), (up_hi[:, k, j, :], up_lo[:, k, j, :]), (p_hi[:, k, :], p_lo[:, k, :]),
                       True, True).then_inc(s_up, 1)

            def down_product(k):
                pe.wait_ge(s_gl, 4 * k + 4)
                for h in range(4 * k, 4 * k + 4):
                    last = pe.matmul(feature_bank(k)[FD * (h % 4):FD * (h % 4) + FD, :], down_sb[:, h, :],
                                     gel[h], start=True, stop=True, skip_group_check=True)
                last.then_inc(s_dn, 1)

            def put_back(k, t):
                pe.wait_ge(s_dlo, k + 1)
                for part in (f_hi, f_lo):
                    last = pe.matmul(wide_bank(t), part[:, k, t * P:(t + 1) * P], put[:, k, :],
                                     start=(k == 0 and part is f_hi), stop=(k == DK - 1 and part is f_lo),
                                     skip_group_check=True)
                if k == DK - 1:
                    last.then_inc(s_fin, 1)

            pe.wait_ge(s_upl, 4)
            for h in range(FH):
                up_product(h)
            for k in range(DK):
                down_product(k)
            for k in range(DK):
                for t in range(TT):
                    put_back(k, t)


_INS = ["x", "ctx", "w_in", "w_dt", "w_out", "conv_par", "norm_w", "dt_bias", "a_log", "d_skip", "gnorm",
        "quant", "up", "down", "perm", "perm_by_part"]


def lay_out(np, i):
    w = np.asarray(i["L0_attn_in_proj_w"])
    bcn = GROUPS * P

    def tiles(rows):
        r = rows.reshape(-1, P, DK, P)
        return r.transpose(0, 3, 2, 1)

    gate_t = tiles(w[:INNER]).reshape(GROUPS, CT, P, DK, P)
    hid_t = tiles(w[INNER:2 * INNER]).reshape(GROUPS, CT, P, DK, P)
    b_t = tiles(w[2 * INNER:2 * INNER + bcn]).reshape(GROUPS, 1, P, DK, P)
    c_t = tiles(w[2 * INNER + bcn:2 * INNER + 2 * bcn]).reshape(GROUPS, 1, P, DK, P)
    by_turns = np.stack([gate_t, hid_t], axis=2).reshape(GROUPS, 2 * CT, P, DK, P)
    w_in = np.concatenate([b_t, c_t, by_turns], axis=1).reshape(GROUPS, NIN, P, DK * P)
    w_dt = tiles(w[2 * INNER + 2 * bcn:]).reshape(P, DK * P)
    w_out = np.asarray(i["L0_attn_out_proj_w"]).T.reshape(GROUPS, CT, P, D)

    par = np.concatenate([np.asarray(i["L0_attn_conv_w"]), np.asarray(i["L0_attn_conv_b"])[:, None]], axis=1)
    hp = par[:INNER].reshape(GROUPS, CT, P, PAR)
    bp = par[INNER:INNER + bcn].reshape(GROUPS, 1, P, PAR)
    cp = par[INNER + bcn:].reshape(GROUPS, 1, P, PAR)
    conv_par = np.concatenate([bp, cp, hp], axis=1).transpose(2, 0, 1, 3).reshape(P, GROUPS, NCONV * PAR)
    quant = np.concatenate([np.asarray(i["L0_xattn_" + n]) for n in ("x1_scale", "x1_zp", "x2_scale", "x2_zp")])
    return {
        "x": np.asarray(i["x"]).reshape(TOK, D),
        "ctx": np.asarray(i["ctx_4096"]),
        "w_in": w_in, "w_dt": w_dt, "w_out": w_out, "conv_par": conv_par,
        "norm_w": np.asarray(i["L0_attn_norm_w"]).reshape(DK, P).T,
        "dt_bias": np.asarray(i["L0_attn_dt_bias"]).reshape(HEADS, 1),
        "a_log": np.asarray(i["L0_attn_A_log"]).reshape(HEADS, 1),
        "d_skip": np.asarray(i["L0_attn_Dp"]).reshape(GROUPS * CT, 2).T,
        "gnorm": np.asarray(i["L0_attn_gnorm_w"]).reshape(GROUPS * CT, P).T,
        "quant": quant,
        "up": np.asarray(i["L0_ffn_up"]).reshape(DK, P, FM).transpose(1, 0, 2),
        "down": np.asarray(i["L0_ffn_down"]).transpose(1, 0, 2),
        "perm": np.asarray(i["L0_ffn_perm"]),
        "perm_by_part": np.asarray(i["L0_ffn_perm"]).reshape(DK, P).T,
    }


def kernel(**inputs):
    import numpy as np
    import concourse.bacc as bacc
    from concourse.bass_utils import run_bass_kernel_spmd

    nc = bacc.Bacc("TRN2", target_bir_lowering=False, num_devices=1)
    laid = lay_out(np, inputs)
    arrays, args = {}, []
    for name in _INS:
        a = np.ascontiguousarray(laid[name])
        arrays[f"in_{name}"] = a
        args.append(nc.dram_tensor(f"in_{name}", a.shape, mybir.dt.from_np(a.dtype), kind="ExternalInput").ap())
    args.append(nc.dram_tensor("out_x", (TOK, D), F32, kind="ExternalOutput").ap())
    decoder_layer(nc, *args)
    r = run_bass_kernel_spmd(nc, [arrays], core_ids=[0])
    return r.results[0]["out_x"].reshape(BATCH, SEQ, D)
```
